# Optimizing a Trainium2 kernel written in Bass

```python
import numpy as np
import jax
import jax.numpy as jnp

def _softmax(x, axis=-1):
    return jax.nn.softmax(x, axis=axis)

def _gelu(x):
    return jax.nn.gelu(x, approximate=True)

def _silu(x):
    return jax.nn.silu(x)

def _sigmoid(x):
    return jax.nn.sigmoid(x)

def _layernorm(x, axis=-1, eps=1e-05):
    m = jnp.mean(x, axis=axis, keepdims=True)
    v = jnp.var(x, axis=axis, keepdims=True)
    return (x - m) / jnp.sqrt(v + eps)

def _scatter_add(tgt, idx, src, axis=0):
    return tgt.at[idx].add(src)

def _segment_sum(src, seg, n):
    return jax.ops.segment_sum(src, seg, n)
kernel_name = 'mk_adj_ffn_d2_adj_r2_90f83a'

def setup_inputs(seed: int=0):
    np.random.seed(seed)
    _w = jnp.asarray

    def _rec_inputs():
        import jax
        import jax.numpy as jnp
        _gk = jax.random.key(seed)
        x = -0.0002928 + 1 * jax.random.normal(jax.random.fold_in(_gk, 1), (64, 128, 128), jnp.float32)
        _a = jax.random.bernoulli(jax.random.fold_in(_gk, 2), 0.03125, (64, 128, 128))
        adj = _a.astype(jnp.int32)
        return (x, adj)
    x, adj = _rec_inputs()

    def _L0_gnn_setup():
        import jax, jax.numpy as jnp
        import numpy as np
        NEG_BIG = -9000000000000000.0
        key = jax.random.key(seed)
        k1, k2, k3, k4 = jax.random.split(key, 4)
        B, N, F_in, F_out = (4, 2048, 128, 128)
        h = jax.random.normal(k1, (B, N, F_in), dtype=jnp.float32)
        adj = jax.random.randint(k2, (B, N, N), 0, 2, dtype=jnp.int32)
        bW = 1.414 * np.sqrt(6.0 / (F_in + F_out))
        W = jax.random.uniform(k3, (F_in, F_out), minval=-bW, maxval=bW, dtype=jnp.float32)
        ba = 1.414 * np.sqrt(6.0 / (2 * F_out + 1))
        a = jax.random.uniform(k4, (2 * F_out, 1), minval=-ba, maxval=ba, dtype=jnp.float32)
        return {'h': h, 'adj': adj, 'W': W, 'a': a}
    _L0_gnn_all = _L0_gnn_setup()
    _L0_gnn_in = {k: v for k, v in _L0_gnn_all.items() if k in ('W', 'a')}
    del _L0_gnn_all

    def _L0_ffn_setup():
        import jax, jax.numpy as jnp
        import numpy as np
        B, S, D, F, E, K = (8, 1024, 128, 512, 8, 2)
        key = jax.random.key(seed)
        ks = jax.random.split(key, 10)
        s = 0.02
        return {'x': jax.random.normal(ks[0], (B, S, D), dtype=jnp.float32), 'Wr': jax.random.normal(ks[1], (D, E), dtype=jnp.float32) * s, 'W1s': jax.random.normal(ks[2], (D, F), dtype=jnp.float32) * s, 'b1s': jnp.zeros((F,), dtype=jnp.float32), 'W2s': jax.random.normal(ks[3], (F, D), dtype=jnp.float32) * s, 'b2s': jnp.zeros((D,), dtype=jnp.float32), 'W1p': jax.random.normal(ks[4], (E, D, F), dtype=jnp.float32) * s, 'b1p': jnp.zeros((E, F), dtype=jnp.float32), 'W2p': jax.random.normal(ks[5], (E, F, D), dtype=jnp.float32) * s, 'b2p': jnp.zeros((E, D), dtype=jnp.float32)}
    _L0_ffn_all = _L0_ffn_setup()
    _L0_ffn_in = {k: v for k, v in _L0_ffn_all.items() if k in ('Wr', 'W1s', 'b1s', 'W2s', 'b2s', 'W1p', 'b1p', 'W2p', 'b2p')}
    del _L0_ffn_all

    def _L1_gnn_setup():
        import jax, jax.numpy as jnp
        import numpy as np
        ALPHA = 0.2
        NEG_PAD = jnp.float32(-2.0 ** 31)

        def _gru_cell(inp, h, w_ih, w_hh, b_ih, b_hh):
            H = h.shape[-1]
            gi = inp @ w_ih.T + b_ih
            gh = h @ w_hh.T + b_hh
            i_r, i_z, i_n = (gi[:, :H], gi[:, H:2 * H], gi[:, 2 * H:])
            h_r, h_z, h_n = (gh[:, :H], gh[:, H:2 * H], gh[:, 2 * H:])
            r = jax.nn.sigmoid(i_r + h_r)
            z = jax.nn.sigmoid(i_z + h_z)
            n = jnp.tanh(i_n + r * h_n)
            return (1.0 - z) * n + z * h
        key = jax.random.key(seed)
        ks = jax.random.split(key, 8)
        B, N, D = (8, 1024, 128)
        H = 128
        return {'adj_mask': jax.random.randint(ks[0], (B, N, N), 0, 2, dtype=jnp.int32), 'x': jax.random.normal(ks[1], (B, N, D), dtype=jnp.float32), 'W': jax.random.normal(ks[2], (D, H), dtype=jnp.float32) * (1.0 / np.sqrt(D)), 'a': jax.random.normal(ks[3], (2 * H, 1), dtype=jnp.float32) * 0.05, 'w_ih': jax.random.normal(ks[4], (3 * H, D), dtype=jnp.float32) * (1.0 / np.sqrt(D)), 'w_hh': jax.random.normal(ks[5], (3 * H, H), dtype=jnp.float32) * (1.0 / np.sqrt(H)), 'b_ih': jnp.zeros((3 * H,), dtype=jnp.float32), 'b_hh': jnp.zeros((3 * H,), dtype=jnp.float32)}
    _L1_gnn_all = _L1_gnn_setup()
    _L1_gnn_in = {k: v for k, v in _L1_gnn_all.items() if k in ('W', 'a', 'w_ih', 'w_hh', 'b_ih', 'b_hh')}
    del _L1_gnn_all

    def _L1_ffn_setup():
        import jax, jax.numpy as jnp
        import numpy as np
        B, K, D = (256, 16, 128)
        E = 32
        H = int(D * 0.25)
        key = jax.random.key(seed)
        ks = jax.random.split(key, 7)
        d_rs = D ** (-0.5)
        h_rs = H ** (-0.5)
        x = jax.random.normal(ks[0], (B, K, D), dtype=jnp.float32)
        router_w = jax.random.uniform(ks[1], (E, D), jnp.float32, -d_rs, d_rs)
        router_b = jax.random.uniform(ks[2], (E,), jnp.float32, -d_rs, d_rs)
        W1 = jax.random.uniform(ks[3], (E, D, H), jnp.float32, -h_rs, h_rs)
        b1 = jax.random.uniform(ks[4], (E, H), jnp.float32, -h_rs, h_rs)
        W2 = jax.random.uniform(ks[5], (E, H, D), jnp.float32, -d_rs, d_rs)
        b2 = jax.random.uniform(ks[6], (E, D), jnp.float32, -d_rs, d_rs)
        return {'x': x, 'router_w': router_w, 'router_b': router_b, 'W1': W1, 'b1': b1, 'W2': W2, 'b2': b2}
    _L1_ffn_all = _L1_ffn_setup()
    _L1_ffn_in = {k: v for k, v in _L1_ffn_all.items() if k in ('router_w', 'router_b', 'W1', 'b1', 'W2', 'b2')}
    del _L1_ffn_all
    return {'x': x, 'adj': adj, 'L0_gnn_W': _L0_gnn_in['W'], 'L0_gnn_a': _L0_gnn_in['a'], 'L0_ffn_Wr': _L0_ffn_in['Wr'], 'L0_ffn_W1s': _L0_ffn_in['W1s'], 'L0_ffn_b1s': _L0_ffn_in['b1s'], 'L0_ffn_W2s': _L0_ffn_in['W2s'], 'L0_ffn_b2s': _L0_ffn_in['b2s'], 'L0_ffn_W1p': _L0_ffn_in['W1p'], 'L0_ffn_b1p': _L0_ffn_in['b1p'], 'L0_ffn_W2p': _L0_ffn_in['W2p'], 'L0_ffn_b2p': _L0_ffn_in['b2p'], 'L1_gnn_W': _L1_gnn_in['W'], 'L1_gnn_a': _L1_gnn_in['a'], 'L1_gnn_w_ih': _L1_gnn_in['w_ih'], 'L1_gnn_w_hh': _L1_gnn_in['w_hh'], 'L1_gnn_b_ih': _L1_gnn_in['b_ih'], 'L1_gnn_b_hh': _L1_gnn_in['b_hh'], 'L1_ffn_router_w': _L1_ffn_in['router_w'], 'L1_ffn_router_b': _L1_ffn_in['router_b'], 'L1_ffn_W1': _L1_ffn_in['W1'], 'L1_ffn_b1': _L1_ffn_in['b1'], 'L1_ffn_W2': _L1_ffn_in['W2'], 'L1_ffn_b2': _L1_ffn_in['b2']}

def reference(x, adj, L0_gnn_W, L0_gnn_a, L0_ffn_Wr, L0_ffn_W1s, L0_ffn_b1s, L0_ffn_W2s, L0_ffn_b2s, L0_ffn_W1p, L0_ffn_b1p, L0_ffn_W2p, L0_ffn_b2p, L1_gnn_W, L1_gnn_a, L1_gnn_w_ih, L1_gnn_w_hh, L1_gnn_b_ih, L1_gnn_b_hh, L1_ffn_router_w, L1_ffn_router_b, L1_ffn_W1, L1_ffn_b1, L1_ffn_W2, L1_ffn_b2):
    import jax
    import jax.numpy as jnp

    def _L0_gnn_ref(h, adj, W, a):
        import jax, jax.numpy as jnp
        import numpy as np
        NEG_BIG = -9000000000000000.0
        F_out = W.shape[1]
        Wh = jnp.einsum('bnf,fo->bno', h, W)
        src = Wh @ a[:F_out, 0]
        dst = Wh @ a[F_out:, 0]
        e = jax.nn.leaky_relu(src[:, :, None] + dst[:, None, :], negative_slope=0.2)
        scores = jnp.where(adj > 0, e, jnp.float32(NEG_BIG))
        attention = jax.nn.softmax(scores, axis=2)
        h_prime = jnp.einsum('bij,bjo->bio', attention, Wh)
        return jax.nn.relu(h_prime)

    def _L0_ffn_ref(x, Wr, W1s, b1s, W2s, b2s, W1p, b1p, W2p, b2p):
        import jax, jax.numpy as jnp
        import numpy as np
        B, S, D, F, E, K = (8, 1024, 128, 512, 8, 2)
        gelu = lambda t: jax.nn.gelu(t, approximate=False)
        shared = gelu(x @ W1s + b1s) @ W2s + b2s
        rw = jax.nn.softmax(x @ Wr, axis=-1)
        topw, topi = jax.lax.top_k(rw, K)
        topw = topw / jnp.sum(topw, axis=-1, keepdims=True)
        mask = jnp.sum(jax.nn.one_hot(topi, E, dtype=topw.dtype) * topw[..., None], axis=-2)
        h = gelu(jnp.einsum('bsd,edf->bsef', x, W1p) + b1p)
        priv = jnp.einsum('bsef,efd->bsed', h, W2p) + b2p
        routed = jnp.einsum('bsed,bse->bsd', priv, mask)
        return shared + routed

    def _L1_gnn_ref(adj_mask, x, W, a, w_ih, w_hh, b_ih, b_hh):
        import jax, jax.numpy as jnp
        import numpy as np
        ALPHA = 0.2
        NEG_PAD = jnp.float32(-2.0 ** 31)

        def _gru_cell(inp, h, w_ih, w_hh, b_ih, b_hh):
            H = h.shape[-1]
            gi = inp @ w_ih.T + b_ih
            gh = h @ w_hh.T + b_hh
            i_r, i_z, i_n = (gi[:, :H], gi[:, H:2 * H], gi[:, 2 * H:])
            h_r, h_z, h_n = (gh[:, :H], gh[:, H:2 * H], gh[:, 2 * H:])
            r = jax.nn.sigmoid(i_r + h_r)
            z = jax.nn.sigmoid(i_z + h_z)
            n = jnp.tanh(i_n + r * h_n)
            return (1.0 - z) * n + z * h
        B, N, D = x.shape
        H = W.shape[1]
        Wh = jnp.einsum('bnd,dh->bnh', x, W)
        Wh1 = Wh @ a[:H, :]
        Wh2 = Wh @ a[H:, :]
        e = jax.nn.leaky_relu(Wh1 + jnp.swapaxes(Wh2, 1, 2), negative_slope=ALPHA)
        scores = jnp.where(adj_mask > 0, e, NEG_PAD)
        attention = jax.nn.softmax(scores, axis=2)
        graph_out = jnp.einsum('bnm,bmh->bnh', attention, Wh)
        out = _gru_cell(graph_out.reshape(-1, H), x.reshape(-1, H), w_ih, w_hh, b_ih, b_hh)
        return out.reshape(B, N, H)

    def _L1_ffn_ref(x, router_w, router_b, W1, b1, W2, b2):
        import jax, jax.numpy as jnp
        import numpy as np
        B, K, D = (256, 16, 128)
        E = 32
        H = int(D * 0.25)
        xf = x.reshape(-1, D)
        logits = xf @ router_w.T + router_b
        idx = jnp.argmax(logits, axis=-1)
        w1t = jnp.take(W1, idx, axis=0)
        h = jnp.einsum('nd,ndh->nh', xf, w1t) + jnp.take(b1, idx, axis=0)
        h = jax.nn.relu(h)
        w2t = jnp.take(W2, idx, axis=0)
        out = jnp.einsum('nh,nhd->nd', h, w2t) + jnp.take(b2, idx, axis=0)
        out = jax.nn.relu(out)
        return out.reshape(x.shape)
    x = x + _L0_gnn_ref(_layernorm(x, axis=-1), adj, L0_gnn_W, L0_gnn_a)
    x = x + _L0_ffn_ref(_layernorm(x, axis=-1), L0_ffn_Wr, L0_ffn_W1s, L0_ffn_b1s, L0_ffn_W2s, L0_ffn_b2s, L0_ffn_W1p, L0_ffn_b1p, L0_ffn_W2p, L0_ffn_b2p)
    x = x + _L1_gnn_ref(adj, _layernorm(x, axis=-1), L1_gnn_W, L1_gnn_a, L1_gnn_w_ih, L1_gnn_w_hh, L1_gnn_b_ih, L1_gnn_b_hh)
    x = x + _L1_ffn_ref(_layernorm(x, axis=-1), L1_ffn_router_w, L1_ffn_router_b, L1_ffn_W1, L1_ffn_b1, L1_ffn_W2, L1_ffn_b2)
    return x

_drawn_inputs = setup_inputs


def setup_inputs(seed=0):
    import zlib

    import numpy as np

    out = dict(_drawn_inputs(seed))
    spreads = {'L0_ffn_b1s': (0.0, 0.302),
     'L0_ffn_b2s': (0.0, 0.1),
     'L0_ffn_b1p': (0.0, 0.405),
     'L0_ffn_b2p': (0.0, 0.1),
     'L1_gnn_b_ih': (0.0, 0.1),
     'L1_gnn_b_hh': (0.0, 0.35)}
    factors = {'L1_ffn_b1': 7.204, 'L1_ffn_b2': 2.877}
    for name, (base, spread) in spreads.items():
        noise = np.random.default_rng([zlib.crc32(name.encode()), seed]).standard_normal(out[name].shape)
        drawn = base * np.exp(spread * noise) if base else spread * noise
        out[name] = jnp.asarray(drawn.astype(out[name].dtype))
    for name, factor in factors.items():
        out[name] = (out[name] * factor).astype(out[name].dtype)
    return out
```

```python
from contextlib import ExitStack, contextmanager

import concourse.bass as bass
from concourse import mybir

P = 128
B = 64
GT = 4
G = B // GT
TOK = GT * P
U = 2
E0, F0, K0 = 8, 512, 2
FC = F0 // P
EF = E0 + 1
E1, H1 = 32, 32
EC = P // H1
C1 = E1 // EC
EPS = 1e-5
SLOPE = 0.2
BIG = 2.0 ** 60

F32 = mybir.dt.float32
F32R = mybir.dt.float32r
BF16 = mybir.dt.bfloat16
I32 = mybir.dt.int32
U32 = mybir.dt.uint32
ALU = mybir.AluOpType
ACT = mybir.ActivationFunctionType
AXX = mybir.AxisListType.X


def ready(eng, sem, i, u):
    eng.wait_ge(sem, U * i + (u + 1 + U))


def freed(eng, sem, i, u):
    eng.wait_ge(sem, U * i + (u + 1))


def landed(eng, sem, i):
    eng.wait_ge(sem, 16 * i + 16)


@contextmanager
def phase_semaphores(nc, prefix):
    with ExitStack() as ctx:
        made = []

        def sem(name):
            made.append(ctx.enter_context(nc.semaphore(prefix + name)))
            return made[-1]

        yield sem
        with nc.Block() as block:
            @block.gpsimd
            def _(pool):
                for s in made:
                    pool.sem_clear(s)


def stages(sem, names):
    return {name: sem(name) for name in names.split()}


def normalise(nc, dve, i, src, T, S, n, arrived, meanwhile=None):
    for u in range(U):
        arrived(u)
        for t in range(GT):
            last = nc.vector.bn_stats(T.stats[u][:, t, :], src[u][:, t, :])
        last.then_inc(S["stats" + n], 1)
    for u in range(U):
        ready(dve, S["stats" + n], i, u)
        even, odd = T.stats[u][:, :, 0:3], T.stats[u][:, :, 3:6]
        nc.vector.tensor_tensor(T.half[u][:, 0], even[:, :, 1], odd[:, :, 1], ALU.add)
        nc.vector.tensor_tensor(T.half[u][:, 1], even[:, :, 1], odd[:, :, 1], ALU.subtract)
        nc.vector.tensor_tensor(T.half[u][:, 2], even[:, :, 2], odd[:, :, 2], ALU.add).then_inc(S["halves" + n], 1)
    for u in range(U):
        ready(dve, S["halves" + n], i, u)
        nc.vector.tensor_scalar(T.mom[u][:, 0], T.half[u][:, 0], 0.5, None, ALU.mult)
        nc.vector.scalar_tensor_tensor(T.mom[u][:, 1], T.half[u][:, 1], 0.25, T.half[u][:, 1], ALU.mult, ALU.mult)
        nc.vector.tensor_scalar(T.mom[u][:, 2], T.half[u][:, 2], 1.0 / P, EPS, ALU.mult, ALU.add).then_inc(S["moments" + n], 1)
    for u in range(U):
        ready(dve, S["moments" + n], i, u)
        nc.vector.tensor_tensor(T.var[u][:], T.mom[u][:, 1], T.mom[u][:, 2], ALU.add).then_inc(S["var" + n], 1)
    if meanwhile is not None:
        meanwhile()
    for u in range(U):
        ready(dve, S["rstd" + n], i, u)
        for t in range(GT):
            last = nc.vector.tensor_scalar(T.xn[u][:, t, :], src[u][:, t, :], T.mom[u][:, 0, t:t + 1], T.rstd[u][:, t:t + 1],
                                           ALU.subtract, ALU.mult)
        last.then_inc(S["xn" + n], 1)


def one_hot(nc, dve, i, src, T, S, K, experts, k, came, n):
    def wide(a):
        return a.unsqueeze(2).to_broadcast([P, GT, experts])

    index_of = K.iota[:, 0:experts].unsqueeze(1).to_broadcast([P, GT, experts])
    for u in range(U):
        ready(dve, came, i, u)
        nc.vector.tensor_reduce(T.top[u][:, k], src[u][:], AXX, ALU.max).then_inc(S[n + "_max"], 1)
    for u in range(U):
        ready(dve, S[n + "_max"], i, u)
        nc.vector.tensor_tensor(T.equal[u][:], src[u][:], wide(T.top[u][:, k]), ALU.is_equal).then_inc(S[n + "_eq"], 1)
    for u in range(U):
        ready(dve, S[n + "_eq"], i, u)
        nc.vector.scalar_tensor_tensor(T.key[u][:], T.equal[u][:], -float(experts), index_of, ALU.mult, ALU.add).then_inc(S[n + "_key"], 1)
    for u in range(U):
        ready(dve, S[n + "_key"], i, u)
        nc.vector.tensor_reduce(T.index[u][:, k], T.key[u][:], AXX, ALU.min).then_inc(S[n + "_index"], 1)
    for u in range(U):
        ready(dve, S[n + "_index"], i, u)
        nc.vector.tensor_tensor(T.hot[u][:, k], T.key[u][:], wide(T.index[u][:, k]), ALU.is_equal).then_inc(S[n + "_hot"], 1)


class Tiles:

    def __init__(self, sb, experts, picks):
        self.stats, self.half, self.mom = sb("stats", [P, GT, 6]), sb("half", [P, 3, GT]), sb("mom", [P, 3, GT])
        self.var, self.rstd, self.xn = sb("var", [P, GT]), sb("rstd", [P, GT]), sb("xn", [P, GT, P])
        self.equal, self.key = sb("equal", [P, GT, experts]), sb("key", [P, GT, experts])
        self.top, self.index = sb("top", [P, picks, GT]), sb("index", [P, picks, GT])
        self.hot = sb("hot", [P, picks, GT, experts])


def setup(nc, ctx, K, W):
    with phase_semaphores(nc, "setup_") as sem, ExitStack() as tmp:
        def sb(name, shape, dt=F32):
            return tmp.enter_context(nc.sbuf_tensor(name, shape, dt))

        a_col = sb("a_col", [P, 4])
        a_rep = sb("a_rep", [P, 4, P])
        w_t = sb("w_t", [P, 2, P])
        loaded, zeroed, ident_made, ident_cast = sem("loaded"), sem("zeroed"), sem("ident_made"), sem("ident_cast")
        wt_ps, wt_sb, rep_made, wa_ps, wa_sb = sem("wt_ps"), sem("wt_sb"), sem("rep_made"), sem("wa_ps"), sem("wa_sb")
        iota_made = sem("iota_made")
        ps = tmp.enter_context(nc.psum_tensor("setup_ps", [P, 2, 512], F32))
        ps2 = tmp.enter_context(nc.psum_tensor("setup_ps2", [P, 512], F32))
        block = tmp.enter_context(nc.Block())
        loads = [
            (K.w_att[:, 0, :], W["L0_gnn_W"]), (K.w_att[:, 1, :], W["L1_gnn_W"]),
            (a_col[:, 0:2], W["L0_gnn_a"]),
            (a_col[:, 2:4], W["L1_gnn_a"]),
            (K.w_r0[:], W["L0_ffn_Wr"]),
        ]

        @block.sync
        def _(sp):
            for dst, src in loads:
                sp.dma_start(dst, src).then_inc(loaded, 16)

        @block.gpsimd
        def _(pool):
            nc.gpsimd.memset(K.ident[:], 0.0).then_inc(zeroed, 1)
            nc.gpsimd.memset(K.nhalf[:], -0.5)
            nc.gpsimd.iota(K.iota_i[:], [[1, E1]], base=0, channel_multiplier=0).then_inc(iota_made, 1)
            pool.wait_ge(zeroed, 1)
            nc.gpsimd.affine_select(out=K.ident[:], in_=K.ident[:], compare_op=ALU.not_equal, fill=1.0, base=0,
                                    pattern=[[-1, P]], channel_multiplier=1).then_inc(ident_made, 1)

        @block.tensor
        def _(pe):
            pe.wait_ge(ident_made, 1)
            pe.wait_ge(loaded, 16 * len(loads))
            for l in range(2):
                last = nc.tensor.transpose(ps[:, l, 0:P], K.w_att[:, l, :], K.ident[:])
            last.then_inc(wt_ps, 1)
            pe.wait_ge(wt_sb, 1)
            pe.wait_ge(rep_made, 1)
            for l in range(2):
                for k in range(2):
                    m = 2 * l + k
                    last = nc.tensor.matmul(ps2[:, m * P:(m + 1) * P], w_t[:, l, :], a_rep[:, m, :], start=True, stop=True)
            last.then_inc(wa_ps, 1)

        @block.vector
        def _(dve):
            dve.wait_ge(iota_made, 1)
            nc.vector.tensor_copy(K.iota[:], K.iota_i[:])
            dve.wait_ge(ident_made, 1)
            nc.vector.tensor_copy(K.ident_b[:], K.ident[:]).then_inc(ident_cast, 1)
            dve.wait_ge(loaded, 16 * len(loads))
            nc.vector.tensor_copy(a_rep[:], a_col[:].unsqueeze(2).to_broadcast([P, 4, P])).then_inc(rep_made, 1)
            dve.wait_ge(wt_ps, 1)
            nc.vector.tensor_copy(w_t[:], ps[:, :, 0:P]).then_inc(wt_sb, 1)
            dve.wait_ge(wa_ps, 1)
            nc.vector.tensor_copy(K.w_score[:], ps2[:].rearrange("p (m f) -> p m f", m=4)).then_inc(wa_sb, 1)


class Constants:
    def __init__(self, ctx, nc):
        def sb(name, shape, dt=F32):
            return ctx.enter_context(nc.sbuf_tensor(name, shape, dt))

        self.ident = sb("ident", [P, P])
        self.ident_b = sb("ident_b", [P, P], BF16)
        self.nhalf = sb("nhalf", [P, GT])
        self.iota_i = sb("iota_i", [P, E1], I32)
        self.iota = sb("iota", [P, E1])
        self.w_att = sb("w_att", [P, 2, P])
        self.w_score = sb("w_score", [P, 4, P])
        self.w_r0 = sb("w_r0", [P, E0])


def phase_a(nc, K, X, XNT, MASK, x, adj):
    with phase_semaphores(nc, "a_") as sem, ExitStack() as ctx:
        def sb(name, shape, dt=F32):
            return [ctx.enter_context(nc.sbuf_tensor(f"a_{name}{u}", shape, dt)) for u in range(U)]

        def bank(name):
            return [ctx.enter_context(nc.psum_tensor(f"a_{name}{u}", [P, 512], F32)) for u in range(U)]

        adj_sb = sb("adj", [P, GT, P], I32)
        closed = sb("closed", [P, TOK], BF16)
        x_new, x1 = sb("x_new", [P, GT, P]), sb("x1", [P, GT, P])
        T = Tiles(sb, E0, K0)
        xnt = sb("xnt", [P, TOK])
        wh, scaled, score = sb("wh", [P, GT, P]), sb("scaled", [P, TOK]), sb("score", [P, GT, P])
        neg_max, sums, inv = sb("neg_max", [P, GT]), sb("sums", [P, GT]), sb("inv", [P, GT])
        prob, prob_t, gain = sb("prob", [P, GT, P]), sb("prob_t", [P, GT, P]), sb("gain", [P, GT, P])
        logit, rest = sb("logit", [P, GT, E0]), sb("rest", [P, GT, E0])
        gap, ratio, den = sb("gap", [P, GT]), sb("ratio", [P, GT]), sb("den", [P, GT])
        weight = sb("weight", [P, K0, GT])
        hotw = sb("hotw", [P, K0, GT, E0])
        ps_t, ps_w, ps_e, ps_r = bank("ps_t"), bank("ps_w"), bank("ps_e"), bank("ps_r")

        S = stages(sem, """
            closed stats halves moments var rstd xn xnt_ps xnt wh_ps score_ps wh scaled score neg_max prob inv
            prob_t_ps prob_t mixed gain x1 stats1 halves1 moments1 var1 rstd1 xn1 xnt1_ps xnt1 kept logit_ps logit
            first_max first_eq first_key first_index first_hot rest second_max second_eq second_key
            second_index second_hot gap ratio den w0 w1 hotw mask x_kept""")
        x_in = [sem(f"x_in{u}") for u in range(U)]
        adj_in = [sem(f"adj_in{u}") for u in range(U)]
        both = range(U)
        xd = x.rearrange("b p f -> p b f")
        ad = adj.rearrange("b p f -> p b f")

        with nc.Block() as start:
            @start.gpsimd
            def _(pool):
                for s in S.values():
                    pool.sem_inc(s, U)

        block = ctx.enter_context(nc.Block())

        @block.sync
        def _(sp):
            with sp.Fori(0, G // U) as i:
                for u in both:
                    freed(sp, S["x1"], i, u)
                    sp.dma_start(x_new[u][:], xd[:, bass.ds((U * i + u) * GT, GT), :]).then_inc(x_in[u], 16)
                    freed(sp, S["closed"], i, u)
                    sp.dma_start(adj_sb[u][:], ad[:, bass.ds((U * i + u) * GT, GT), :]).then_inc(adj_in[u], 16)

        @block.gpsimd
        def _(pool):
            with pool.Fori(0, G // U) as i:
                for u in both:
                    ready(pool, S["var"], i, u)
                    nc.gpsimd.tensor_tensor(T.rstd[u][:], T.var[u][:], K.nhalf[:], ALU.pow).then_inc(S["rstd"], 1)
                for u in both:
                    ready(pool, S["x1"], i, u)
                    nc.gpsimd.tensor_copy(X[:, bass.ds((U * i + u) * GT, GT), :], x1[u][:]).then_inc(S["x_kept"], 1)
                for u in both:
                    ready(pool, S["var1"], i, u)
                    nc.gpsimd.tensor_tensor(T.rstd[u][:], T.var[u][:], K.nhalf[:], ALU.pow).then_inc(S["rstd1"], 1)
                for u in both:
                    ready(pool, S["xnt1"], i, u)
                    nc.gpsimd.tensor_copy(XNT[:, bass.ds((U * i + u) * TOK, TOK)], xnt[u][:]).then_inc(S["kept"], 1)

        @block.vector
        def _(dve):
            with dve.Fori(0, G // U) as i:
                def close():
                    for u in both:
                        landed(dve, adj_in[u], i)
                        freed(dve, S["score_ps"], i, u)
                        nc.vector.tensor_scalar(closed[u][:], adj_sb[u][:].rearrange("p t f -> p (t f)"), 0.0, -BIG,
                                                ALU.is_le, ALU.mult).then_inc(S["closed"], 1)

                normalise(nc, dve, i, x_new, T, S, "", lambda u: landed(dve, x_in[u], i), close)
                for u in both:
                    ready(dve, S["scaled"], i, u)
                    freed(dve, S["prob"], i, u)
                    nc.vector.tensor_tensor(score[u][:].rearrange("p t f -> p (t f)"), scaled[u][:], ps_e[u][:],
                                            ALU.max).then_inc(S["score"], 1)
                for u in both:
                    ready(dve, S["score"], i, u)
                    nc.vector.tensor_reduce(neg_max[u][:], score[u][:], AXX, ALU.max, negate=True).then_inc(S["neg_max"], 1)
                for u in both:
                    ready(dve, S["prob"], i, u)
                    nc.vector.reciprocal(inv[u][:], sums[u][:]).then_inc(S["inv"], 1)
                for u in both:
                    ready(dve, S["inv"], i, u)
                    ready(dve, S["mixed"], i, u)
                    for t in range(GT):
                        last = nc.vector.tensor_scalar(gain[u][:, t, :], ps_w[u][:, t * P:(t + 1) * P], inv[u][:, t:t + 1],
                                                       0.0, ALU.mult, ALU.max)
                    last.then_inc(S["gain"], 1)
                for u in both:
                    ready(dve, S["gain"], i, u)
                    freed(dve, S["x_kept"], i, u)
                    nc.vector.tensor_tensor(x1[u][:], x_new[u][:], gain[u][:], ALU.add).then_inc(S["x1"], 1)
                normalise(nc, dve, i, x1, T, S, "1", lambda u: ready(dve, S["x1"], i, u))
                for u in both:
                    ready(dve, S["logit_ps"], i, u)
                    nc.vector.tensor_copy(logit[u][:].rearrange("p t e -> p (t e)"), ps_r[u][:, 0:GT * E0]).then_inc(S["logit"], 1)
                def wide(a):
                    return a.unsqueeze(2).to_broadcast([P, GT, E0])

                one_hot(nc, dve, i, logit, T, S, K, E0, 0, S["logit"], "first")
                for u in both:
                    ready(dve, S["first_hot"], i, u)
                    nc.vector.scalar_tensor_tensor(rest[u][:], T.hot[u][:, 0], -BIG, logit[u][:], ALU.mult, ALU.add).then_inc(S["rest"], 1)
                one_hot(nc, dve, i, rest, T, S, K, E0, 1, S["rest"], "second")
                for u in both:
                    nc.vector.tensor_tensor(gap[u][:], T.top[u][:, 1], T.top[u][:, 0], ALU.subtract).then_inc(S["gap"], 1)
                for u in both:
                    ready(dve, S["ratio"], i, u)
                    nc.vector.tensor_scalar(den[u][:], ratio[u][:], 1.0, None, ALU.add).then_inc(S["den"], 1)
                for u in both:
                    ready(dve, S["den"], i, u)
                    nc.vector.reciprocal(weight[u][:, 0], den[u][:]).then_inc(S["w0"], 1)
                for u in both:
                    ready(dve, S["w0"], i, u)
                    nc.vector.tensor_tensor(weight[u][:, 1], weight[u][:, 0], ratio[u][:], ALU.mult).then_inc(S["w1"], 1)
                for u in both:
                    ready(dve, S["second_hot"], i, u)
                    ready(dve, S["w1"], i, u)
                    for k in range(K0):
                        last = nc.vector.tensor_tensor(hotw[u][:, k], T.hot[u][:, k], wide(weight[u][:, k]), ALU.mult)
                    last.then_inc(S["hotw"], 1)
                for u in both:
                    ready(dve, S["hotw"], i, u)
                    nc.vector.tensor_tensor(MASK[:, bass.ds((U * i + u) * GT, GT), :], hotw[u][:, 0], hotw[u][:, 1],
                                            ALU.add).then_inc(S["mask"], 1)

        @block.scalar
        def _(act):
            with act.Fori(0, G // U) as i:
                for u in both:
                    ready(act, S["xnt_ps"], i, u)
                    freed(act, S["kept"], i, u)
                    nc.scalar.copy(xnt[u][:], ps_t[u][:]).then_inc(S["xnt"], 1)
                for u in both:
                    ready(act, S["wh_ps"], i, u)
                    nc.scalar.copy(wh[u][:].rearrange("p t f -> p (t f)"), ps_w[u][:]).then_inc(S["wh"], 1)
                    ready(act, S["score_ps"], i, u)
                    nc.scalar.mul(scaled[u][:], ps_e[u][:], SLOPE).then_inc(S["scaled"], 1)
                for u in both:
                    ready(act, S["neg_max"], i, u)
                    freed(act, S["prob_t_ps"], i, u)
                    for t in range(GT):
                        last = nc.scalar.activation(prob[u][:, t, :], score[u][:, t, :], ACT.Exp, bias=neg_max[u][:, t:t + 1],
                                                    accum_out=sums[u][:, t:t + 1])
                    last.then_inc(S["prob"], 1)
                for u in both:
                    ready(act, S["prob_t_ps"], i, u)
                    nc.scalar.copy(prob_t[u][:].rearrange("p t f -> p (t f)"), ps_t[u][:]).then_inc(S["prob_t"], 1)
                for u in both:
                    ready(act, S["xnt1_ps"], i, u)
                    nc.scalar.copy(xnt[u][:], ps_e[u][:]).then_inc(S["xnt1"], 1)
                for u in both:
                    ready(act, S["gap"], i, u)
                    nc.scalar.activation(ratio[u][:], gap[u][:], ACT.Exp).then_inc(S["ratio"], 1)

        @block.tensor
        def _(pe):
            with pe.Fori(0, G // U) as i:
                for u in both:
                    ready(pe, S["xn"], i, u)
                    freed(pe, S["prob_t"], i, u)
                    for t in range(GT):
                        last = nc.tensor.transpose(ps_t[u][:, t * P:(t + 1) * P], T.xn[u][:, t, :], K.ident[:])
                    last.then_inc(S["xnt_ps"], 1)
                for u in both:
                    ready(pe, S["xnt"], i, u)
                    freed(pe, S["gain"], i, u)
                    for t in range(GT):
                        last = nc.tensor.matmul(ps_w[u][:, t * P:(t + 1) * P], xnt[u][:, t * P:(t + 1) * P], K.w_att[:, 0, :],
                                                start=True, stop=True)
                    last.then_inc(S["wh_ps"], 1)
                    freed(pe, S["xnt1"], i, u)
                    ready(pe, S["closed"], i, u)
                    nc.tensor.matmul(ps_e[u][:], K.w_score[:, 1, :], xnt[u][:], start=True, stop=False)
                    for t in range(GT):
                        nc.tensor.matmul(ps_e[u][:, t * P:(t + 1) * P], xnt[u][:, t * P:(t + 1) * P], K.w_score[:, 0, :],
                                         start=False, stop=False, skip_group_check=True)
                    nc.tensor.matmul(ps_e[u][:], K.ident_b[:], closed[u][:], start=False, stop=True).then_inc(S["score_ps"], 1)
                for u in both:
                    ready(pe, S["prob"], i, u)
                    for t in range(GT):
                        last = nc.tensor.transpose(ps_t[u][:, t * P:(t + 1) * P], prob[u][:, t, :], K.ident[:])
                    last.then_inc(S["prob_t_ps"], 1)
                for u in both:
                    ready(pe, S["prob_t"], i, u)
                    for t in range(GT):
                        last = nc.tensor.matmul(ps_w[u][:, t * P:(t + 1) * P], prob_t[u][:, t, :], wh[u][:, t, :],
                                                start=True, stop=True)
                    last.then_inc(S["mixed"], 1)
                for u in both:
                    ready(pe, S["xn1"], i, u)
                    for t in range(GT):
                        last = nc.tensor.transpose(ps_e[u][:, t * P:(t + 1) * P], T.xn[u][:, t, :], K.ident[:])
                    last.then_inc(S["xnt1_ps"], 1)
                for u in both:
                    ready(pe, S["xnt1"], i, u)
                    freed(pe, S["logit"], i, u)
                    for t in range(GT):
                        last = nc.tensor.matmul(ps_r[u][:, t * E0:(t + 1) * E0], xnt[u][:, t * P:(t + 1) * P], K.w_r0[:],
                                                start=True, stop=True)
                    last.then_inc(S["logit_ps"], 1)


def phase_b(nc, K, X, XNT, MASK, W):
    with phase_semaphores(nc, "b_") as sem, ExitStack() as ctx:
        def sb(name, shape, dt=F32):
            return ctx.enter_context(nc.sbuf_tensor("b_" + name, shape, dt))

        w1 = [sb(f"w1_{h}", [P, EF, F0], F32R) for h in "hl"]
        w2 = [sb(f"w2_{h}", [P, EF, FC, P], F32R) for h in "hl"]
        b1 = sb("b1", [P, EF, FC])
        b2s = sb("b2s", [P, 1])
        b2p = sb("b2p", [E0, P])
        select = sb("select", [E0, E0, P], F32R)
        stage = [sb(f"stage{k}", [P, F0]) for k in range(2)]
        xs = [sb(f"x_{h}", [P, TOK], F32R) for h in "hl"]
        gate_in = sb("gate_in", [P, GT, E0])
        gate_t = sb("gate_t", [E0, TOK])
        gates = [sb(f"gate_{h}", [E0, TOK], F32R) for h in "hl"]
        hidden = [sb(f"hidden{k}", [P, TOK]) for k in range(2)]
        hs = [[sb(f"hs{k}{h}", [P, TOK], F32R) for h in "hl"] for k in range(2)]
        gate = [sb(f"gate{k}", [P, TOK]) for k in range(2)]
        gated = [sb(f"gated{k}", [P, TOK]) for k in range(2)]
        total = sb("total", [P, TOK])

        def bank(name, n):
            return [ctx.enter_context(nc.psum_tensor(f"b_{name}{k}", [P, 512], F32)) for k in range(n)]

        ps_h, ps_y, ps_g, ps_t = bank("ps_h", 3), bank("ps_y", 2), bank("ps_g", 2), bank("ps_t", 1)[0]

        loaded = [sem(f"loaded{k}") for k in range(2)]
        rest_loaded, w_high, w_split, select_made = sem("rest_loaded"), sem("w_high"), sem("w_split"), sem("select_made")
        select_zero, select_f32 = sem("select_zero"), sem("select_f32")
        pieces = [(w1, e, None) for e in range(EF)] + [(w2, e, None) for e in range(EF)]

        def source(n):
            e = n % EF
            if n < EF:
                return W["L0_ffn_W1s"] if e == 0 else W["L0_ffn_W1p"][e - 1]
            w = W["L0_ffn_W2s"] if e == 0 else W["L0_ffn_W2p"][e - 1]
            return w.rearrange("(c f) d -> f c d", c=FC)

        def part(n, h):
            return (w1 if n < EF else w2)[h][:, n % EF]

        with ExitStack() as tmp:
            sel_f = tmp.enter_context(nc.sbuf_tensor("b_sel_f", [E0, E0 * P], F32))
            block = tmp.enter_context(nc.Block())

            @block.sync
            def _(sp):
                sp.dma_start(b1[:, 0, :], W["L0_ffn_b1s"]).then_inc(rest_loaded, 16)
                sp.dma_start(b1[:, 1:, :], W["L0_ffn_b1p"]).then_inc(rest_loaded, 16)
                sp.dma_start(b2s[:], W["L0_ffn_b2s"]).then_inc(rest_loaded, 16)
                sp.dma_start(b2p[:], W["L0_ffn_b2p"]).then_inc(rest_loaded, 16)
                for n in range(2 * EF):
                    if n >= 2:
                        sp.wait_ge(w_split, n - 1)
                    dst = stage[n % 2][:] if n < EF else stage[n % 2][:].rearrange("p (c d) -> p c d", c=FC)
                    sp.dma_start(dst, source(n)).then_inc(loaded[n % 2], 16)
                sp.wait_ge(rest_loaded, 64)

            @block.scalar
            def _(act):
                for n in range(2 * EF):
                    act.wait_ge(loaded[n % 2], 16 * (n // 2 + 1))
                    flat = part(n, 0) if n < EF else part(n, 0).rearrange("p c d -> p (c d)")
                    nc.scalar.copy(flat, stage[n % 2][:]).then_inc(w_high, 1)

            @block.vector
            def _(dve):
                for n in range(2 * EF):
                    dve.wait_ge(w_high, n + 1)
                    hi, lo = (part(n, h) if n < EF else part(n, h).rearrange("p c d -> p (c d)") for h in range(2))
                    nc.vector.tensor_tensor(lo, stage[n % 2][:], hi.bitcast(F32), ALU.subtract).then_inc(w_split, 1)
                dve.wait_ge(select_f32, 1)
                nc.vector.tensor_copy(select[:].rearrange("k e p -> k (e p)"), sel_f[:]).then_inc(select_made, 1)

            @block.gpsimd
            def _(pool):
                nc.gpsimd.memset(sel_f[:], 0.0).then_inc(select_zero, 1)
                pool.wait_ge(select_zero, 1)
                nc.gpsimd.affine_select(out=sel_f[:].rearrange("k (e p) -> k e p", e=E0), in_=sel_f[:].rearrange("k (e p) -> k e p", e=E0),
                                        compare_op=ALU.not_equal, fill=1.0, base=0, pattern=[[-1, E0], [0, P]],
                                        channel_multiplier=1).then_inc(select_f32, 1)

        gate_copied, gate_ps, gate_rows, gate_high, gate_low = (sem("gate_" + n) for n in ("copied", "ps", "rows", "high", "low"))
        x_high, x_low = sem("x_high"), sem("x_low")
        h_ps, h_act, h_high, h_low, h_used = (sem("h_" + n) for n in ("ps", "act", "high", "low", "used"))
        y_shared, y_gated, y_summed = (sem("y_" + n) for n in ("shared", "gated", "summed"))
        g_ps, g_sb = sem("g_ps"), sem("g_sb")
        out_ps, x2 = sem("out_ps"), sem("x2")
        NH = EF * FC
        with nc.Block() as start:
            @start.gpsimd
            def _(pool):
                for s, credits in ((h_act, 3), (h_high, 2), (h_low, 2), (h_used, 2), (g_sb, 2), (y_gated, 2), (y_summed, 2),
                                   (h_ps, 1), (x2, 1), (out_ps, 1), (gate_ps, 1), (gate_low, 1)):
                    pool.sem_inc(s, credits)

        block = ctx.enter_context(nc.Block())

        @block.tensor
        def _(pe):
            with pe.Fori(0, G) as g:
                pe.wait_ge(gate_copied, g + 1)
                pe.wait_ge(x2, g + 1)
                for t in range(GT):
                    last = nc.tensor.transpose(ps_t[0:E0, t * P:(t + 1) * P], gate_in[:, t, :], K.ident[:])
                last.then_inc(gate_ps, 1)

                def up(n):
                    e, c = divmod(n, FC)
                    if n == 0:
                        pe.wait_ge(x_low, g + 1)
                    pe.wait_ge(h_act, NH * g + (n + 1))
                    for k, (a, b) in enumerate(((0, 0), (0, 1), (1, 0))):
                        last = nc.tensor.matmul(ps_h[n % 3][:], w1[a][:, e, c * P:(c + 1) * P], xs[b][:],
                                                start=(k == 0), stop=(k == 2))
                    last.then_inc(h_ps, 1)

                def down(n):
                    e, c = divmod(n, FC)
                    if c == 0:
                        if e >= 3:
                            pe.wait_ge(y_gated, E0 * g + e)
                        elif e == 2:
                            pe.wait_ge(y_shared, g + 1)
                        elif e == 1:
                            pe.wait_ge(y_gated, E0 * g + 2)
                    pe.wait_ge(h_low, NH * g + (n + 1 + 2))
                    if n == FC - 1:
                        pe.wait_ge(gate_rows, g + 1)
                        nc.tensor.matmul(ps_y[0][:], b2p[:], gate_t[:], start=False, stop=False)
                    for k, (a, b) in enumerate(((0, 0), (0, 1), (1, 0))):
                        last = nc.tensor.matmul(ps_y[e % 2][:], w2[a][:, e, c, :], hs[n % 2][b][:],
                                                start=(c == 0 and k == 0), stop=(c == FC - 1 and k == 2))
                    last.then_inc(h_used, 1)

                def spread(e):
                    pe.wait_ge(g_sb, E0 * g + e)
                    pe.wait_ge(gate_low, g + 2)
                    nc.tensor.matmul(ps_g[e % 2][:], select[:, e - 1, :], gates[0][:], start=True, stop=False)
                    nc.tensor.matmul(ps_g[e % 2][:], select[:, e - 1, :], gates[1][:], start=False, stop=True).then_inc(g_ps, 1)

                for n in range(NH + 2):
                    if n < NH:
                        up(n)
                    if n >= 2:
                        down(n - 2)
                        if (n - 2) % FC == FC - 2 and n - 2 > FC:
                            spread((n - 2) // FC)
                pe.wait_ge(y_summed, E0 * g + (E0 + 2))
                for t in range(GT):
                    last = nc.tensor.transpose(ps_t[:, t * P:(t + 1) * P], total[:, t * P:(t + 1) * P], K.ident[:])
                last.then_inc(out_ps, 1)

        @block.scalar
        def _(act):
            with act.Fori(0, G) as g:
                act.wait_ge(h_ps, NH * g + 1)
                nc.scalar.copy(xs[0][:], XNT[:, bass.ds(g * TOK, TOK)]).then_inc(x_high, 1)
                act.wait_ge(gate_ps, g + 2)
                nc.scalar.copy(gate_t[:], ps_t[0:E0, :]).then_inc(gate_rows, 1)
                act.wait_ge(gate_rows, g + 1)
                nc.scalar.copy(gates[0][:], gate_t[:]).then_inc(gate_high, 1)
                for n in range(NH):
                    e, c = divmod(n, FC)
                    act.wait_ge(h_ps, NH * g + (n + 1 + 1))
                    act.wait_ge(h_low, NH * g + (n + 1))
                    nc.scalar.activation(hidden[n % 2][:], ps_h[n % 3][:], ACT.Gelu, bias=b1[:, e, c:c + 1]).then_inc(h_act, 1)
                    if c == 3 and e == 1:
                        act.wait_ge(h_used, NH * g + (FC + 2))
                        act.wait_ge(out_ps, g + 1)
                        nc.scalar.activation(total[:], ps_y[0][:], ACT.Identity, bias=b2s[:]).then_inc(y_shared, 1)
                    if c == FC - 1 and e > 1 or n == NH - 1:
                        for f in ([e - 1] if n < NH - 1 else [e - 1, e]):
                            act.wait_ge(g_ps, E0 * g + f)
                            act.wait_ge(y_gated, E0 * g + f)
                            nc.scalar.copy(gate[f % 2][:], ps_g[f % 2][:]).then_inc(g_sb, 1)

        @block.vector
        def _(dve):
            with dve.Fori(0, G) as g:
                dve.wait_ge(gate_ps, g + 1)
                nc.vector.tensor_copy(gate_in[:], MASK[:, bass.ds(g * GT, GT), :]).then_inc(gate_copied, 1)
                dve.wait_ge(x_high, g + 1)
                nc.vector.tensor_tensor(xs[1][:], XNT[:, bass.ds(g * TOK, TOK)], xs[0][:].bitcast(F32), ALU.subtract).then_inc(x_low, 1)
                dve.wait_ge(gate_high, g + 1)
                nc.vector.tensor_tensor(gates[1][:], gate_t[:], gates[0][:].bitcast(F32), ALU.subtract).then_inc(gate_low, 1)

                def weigh(e):
                    dve.wait_ge(h_used, NH * g + (FC * (e + 1) + 2))
                    dve.wait_ge(g_sb, E0 * g + (e + 2))
                    dve.wait_ge(y_summed, E0 * g + e)
                    nc.vector.tensor_tensor(gated[e % 2][:], ps_y[e % 2][:], gate[e % 2][:], ALU.mult).then_inc(y_gated, 1)

                for n in range(NH):
                    e, c = divmod(n, FC)
                    dve.wait_ge(h_act, NH * g + (n + 1 + 3))
                    dve.wait_ge(h_used, NH * g + (n + 1))
                    nc.vector.tensor_copy(hs[n % 2][0][:], hidden[n % 2][:]).then_inc(h_high, 1)
                    dve.wait_ge(h_high, NH * g + (n + 1 + 2))
                    nc.vector.tensor_tensor(hs[n % 2][1][:], hidden[n % 2][:], hs[n % 2][0][:].bitcast(F32), ALU.subtract).then_inc(h_low, 1)
                    if c == FC - 1 and e > 1:
                        weigh(e - 1)
                weigh(E0)
                dve.wait_ge(out_ps, g + 2)
                nc.vector.tensor_tensor(X[:, bass.ds(g * GT, GT), :], X[:, bass.ds(g * GT, GT), :],
                                        ps_t[:].rearrange("p (t f) -> p t f", t=GT), ALU.add).then_inc(x2, 1)

        @block.gpsimd
        def _(pool):
            with pool.Fori(0, G) as g:
                for e in range(1, EF):
                    if e == 1:
                        pool.wait_ge(y_shared, g + 1)
                    else:
                        pool.wait_ge(y_summed, E0 * g + (e - 1 + 2))
                    pool.wait_ge(y_gated, E0 * g + (e + 2))
                    nc.gpsimd.tensor_tensor(total[:], total[:], gated[e % 2][:], ALU.add).then_inc(y_summed, 1)


def phase_c(nc, K, X, W, adj, out):
    with phase_semaphores(nc, "c_") as sem, ExitStack() as ctx:
        def one(name, shape, dt=F32):
            return ctx.enter_context(nc.sbuf_tensor("c_" + name, shape, dt))

        def sb(name, shape, dt=F32):
            return [one(f"{name}{u}", shape, dt) for u in range(U)]

        def bank(name):
            return [ctx.enter_context(nc.psum_tensor(f"c_{name}{u}", [P, 512], F32)) for u in range(U)]

        w_ih, w_hh, w_r1 = one("w_ih", [P, 3, P]), one("w_hh", [P, 3, P]), one("w_r1", [P, E1])
        b_ih, b_hh, b_gate = one("b_ih", [P, 3]), one("b_hh", [P, 3]), one("b_gate", [P, 2])
        b_r1 = one("b_r1", [P, E1])
        w1, b1 = one("w1", [P, C1, P]), one("b1", [P, C1])
        w2, b2 = one("w2", [P, C1, P]), one("b2", [E1, P])
        shut = one("shut", [E1, C1, P], BF16)
        T = Tiles(sb, E1, 1)
        adj_sb, closed = sb("adj", [P, GT, P], I32), sb("closed", [P, TOK], BF16)
        x2, x3, x4 = sb("x2", [P, GT, P]), sb("x3", [P, GT, P]), sb("x4", [P, GT, P])
        xnt, wh, scaled, score = sb("xnt", [P, TOK]), sb("wh", [P, GT, P]), sb("scaled", [P, TOK]), sb("score", [P, GT, P])
        neg_max, sums, inv = sb("neg_max", [P, GT]), sb("sums", [P, GT]), sb("inv", [P, GT])
        prob, prob_t, mixed = sb("prob", [P, GT, P]), sb("prob_t", [P, GT, P]), sb("mixed", [P, TOK])
        gate_r, gate_z, new = sb("gate_r", [P, TOK]), sb("gate_z", [P, TOK]), sb("new", [P, TOK])
        logit, hot_t, hot_m = sb("logit", [P, GT, E1]), sb("hot_t", [E1, TOK]), sb("hot_m", [E1, TOK], BF16)
        hidden = [sb(f"hidden{k}_", [P, TOK]) for k in range(2)]
        ps_t, ps_w, ps_e, ps_r = bank("ps_t"), bank("ps_w"), bank("ps_e"), bank("ps_r")
        both = range(U)

        S = stages(sem, """
            closed stats halves moments var rstd xn xnt_ps xnt wh_ps score_ps wh scaled score neg_max exp inv prob
            prob_t_ps prob_t mixed_ps mixed hn_ps r_ps z_ps in_ps gate_r gate_z hn reset pre new gap keep gru gru_ps x3
            stats1 halves1 moments1 var1 rstd1 xn1 xnt1_ps xnt1 logit_ps logit
            only_max only_eq only_key only_index only_hot hot_ps hot_t hot_m y y_t_ps x4""")
        up_ps, down_done, hidden_even, hidden_odd = sem("up_ps"), sem("down_done"), sem("hidden_even"), sem("hidden_odd")
        x_in, adj_in, out_done = [sem(f"x_in{u}") for u in both], [sem(f"adj_in{u}") for u in both], [sem(f"out{u}") for u in both]

        w_loaded, b_summed, shut_zero, shut_f32, shut_made = (sem(n) for n in ("w_loaded", "b_summed", "shut_zero", "shut_f32", "shut_made"))
        loads = [(w_ih[:], W["L1_gnn_w_ih"]), (w_hh[:], W["L1_gnn_w_hh"]), (b_ih[:], W["L1_gnn_b_ih"]), (b_hh[:], W["L1_gnn_b_hh"]),
                 (w_r1[:], W["L1_ffn_router_w"]), (b_r1[:], W["L1_ffn_router_b"].to_broadcast([P, E1])),
                 (w1[:], W["L1_ffn_W1"]), (b1[:], W["L1_ffn_b1"]), (w2[:], W["L1_ffn_W2"]), (b2[:], W["L1_ffn_b2"])]
        with ExitStack() as tmp:
            shut_f = tmp.enter_context(nc.sbuf_tensor("c_shut_f", [E1, C1 * P], F32))
            b_sum = tmp.enter_context(nc.sbuf_tensor("c_b_sum", [P, 2], F32))
            start = tmp.enter_context(nc.Block())

            @start.sync
            def _(sp):
                for dst, src in loads:
                    sp.dma_start(dst, src).then_inc(w_loaded, 16)

            @start.gpsimd
            def _(pool):
                for s in S.values():
                    pool.sem_inc(s, U)
                pool.sem_inc(hidden_even, U)
                pool.sem_inc(hidden_odd, U)
                pool.sem_inc(down_done, 2 * U)
                for u in both:
                    pool.sem_inc(out_done[u], 16)
                nc.gpsimd.memset(shut_f[:], 0.0).then_inc(shut_zero, 1)
                pool.wait_ge(shut_zero, 1)
                v = shut_f[:].rearrange("k (c e h) -> k c e h", c=C1, e=EC)
                nc.gpsimd.affine_select(out=v, in_=v, compare_op=ALU.not_equal, fill=BIG, base=0,
                                        pattern=[[-EC, C1], [-1, EC], [0, H1]], channel_multiplier=1).then_inc(shut_f32, 1)

            @start.vector
            def _(dve):
                dve.wait_ge(shut_f32, 1)
                nc.vector.tensor_copy(shut[:].rearrange("k c f -> k (c f)"), shut_f[:]).then_inc(shut_made, 1)
                dve.wait_ge(w_loaded, 16 * len(loads))
                nc.vector.tensor_tensor(b_sum[:], b_ih[:, 0:2], b_hh[:, 0:2], ALU.add).then_inc(b_summed, 1)
                dve.wait_ge(b_summed, 1)
                nc.vector.tensor_scalar(b_gate[:], b_sum[:], 0.5, None, ALU.mult)

        ad = adj.rearrange("b p f -> p b f")
        od = out.rearrange("b p f -> p b f")
        block = ctx.enter_context(nc.Block())

        def graphs(i, u):
            return bass.ds((U * i + u) * GT, GT)

        @block.sync
        def _(sp):
            def load(i, u):
                sp.dma_start(x2[u][:], X[:, graphs(i, u), :]).then_inc(x_in[u], 16)
                sp.dma_start(adj_sb[u][:], ad[:, graphs(i, u), :]).then_inc(adj_in[u], 16)

            def store(i, u):
                ready(sp, S["x4"], i, u)
                sp.dma_start(od[:, graphs(i, u), :], x4[u][:]).then_inc(out_done[u], 16)

            for u in both:
                load(0, u)
            with sp.Fori(0, G // U - 1) as i:
                for u in both:
                    ready(sp, S["closed"], i, u)
                    ready(sp, S["x3"], i, u)
                    load(i + 1, u)
                for u in both:
                    store(i, u)
            for u in both:
                store(G // U - 1, u)
            for u in both:
                sp.wait_ge(out_done[u], 16 * (G // U) + 16)

        @block.gpsimd
        def _(pool):
            with pool.Fori(0, G // U) as i:
                for n in ("", "1"):
                    for u in both:
                        ready(pool, S["var" + n], i, u)
                        nc.gpsimd.tensor_tensor(T.rstd[u][:], T.var[u][:], K.nhalf[:], ALU.pow).then_inc(S["rstd" + n], 1)

        @block.vector
        def _(dve):
            with dve.Fori(0, G // U) as i:
                def close():
                    for u in both:
                        landed(dve, adj_in[u], i)
                        freed(dve, S["score_ps"], i, u)
                        nc.vector.tensor_scalar(closed[u][:], adj_sb[u][:].rearrange("p t f -> p (t f)"), 0.0, -BIG,
                                                ALU.is_le, ALU.mult).then_inc(S["closed"], 1)

                normalise(nc, dve, i, x2, T, S, "", lambda u: landed(dve, x_in[u], i), close)
                for u in both:
                    ready(dve, S["scaled"], i, u)
                    freed(dve, S["exp"], i, u)
                    nc.vector.tensor_tensor(score[u][:].rearrange("p t f -> p (t f)"), scaled[u][:], ps_e[u][:],
                                            ALU.max).then_inc(S["score"], 1)
                for u in both:
                    ready(dve, S["score"], i, u)
                    nc.vector.tensor_reduce(neg_max[u][:], score[u][:], AXX, ALU.max, negate=True).then_inc(S["neg_max"], 1)
                for u in both:
                    ready(dve, S["exp"], i, u)
                    nc.vector.reciprocal(inv[u][:], sums[u][:]).then_inc(S["inv"], 1)
                for u in both:
                    ready(dve, S["inv"], i, u)
                    for t in range(GT):
                        last = nc.vector.tensor_scalar(prob[u][:, t, :], prob[u][:, t, :], inv[u][:, t:t + 1], None, ALU.mult)
                    last.then_inc(S["prob"], 1)
                for u in both:
                    ready(dve, S["gate_r"], i, u)
                    ready(dve, S["hn"], i, u)
                    nc.vector.scalar_tensor_tensor(gate_r[u][:], gate_r[u][:], 1.0, new[u][:], ALU.add, ALU.mult).then_inc(S["reset"], 1)
                for u in both:
                    ready(dve, S["reset"], i, u)
                    ready(dve, S["in_ps"], i, u)
                    nc.vector.scalar_tensor_tensor(gate_r[u][:], gate_r[u][:], 0.5, ps_r[u][:], ALU.mult, ALU.add).then_inc(S["pre"], 1)
                for u in both:
                    ready(dve, S["new"], i, u)
                    nc.vector.tensor_tensor(mixed[u][:], xnt[u][:], new[u][:], ALU.subtract).then_inc(S["gap"], 1)
                for u in both:
                    ready(dve, S["gap"], i, u)
                    nc.vector.scalar_tensor_tensor(mixed[u][:], gate_z[u][:], 1.0, mixed[u][:], ALU.add, ALU.mult).then_inc(S["keep"], 1)
                for u in both:
                    ready(dve, S["keep"], i, u)
                    nc.vector.scalar_tensor_tensor(mixed[u][:], mixed[u][:], 0.5, new[u][:], ALU.mult, ALU.add).then_inc(S["gru"], 1)
                for u in both:
                    ready(dve, S["gru_ps"], i, u)
                    freed(dve, S["x4"], i, u)
                    nc.vector.tensor_tensor(x3[u][:].rearrange("p t f -> p (t f)"), x2[u][:].rearrange("p t f -> p (t f)"), ps_t[u][:],
                                            ALU.add).then_inc(S["x3"], 1)
                normalise(nc, dve, i, x3, T, S, "1", lambda u: ready(dve, S["x3"], i, u))
                for u in both:
                    ready(dve, S["logit_ps"], i, u)
                    nc.vector.tensor_tensor(logit[u][:], ps_r[u][:, 0:GT * E1].rearrange("p (t e) -> p t e", e=E1),
                                            b_r1[:].unsqueeze(1).to_broadcast([P, GT, E1]), ALU.add).then_inc(S["logit"], 1)
                one_hot(nc, dve, i, logit, T, S, K, E1, 0, S["logit"], "only")
                for u in both:
                    ready(dve, S["hot_t"], i, u)
                    nc.vector.tensor_scalar(hot_m[u][:], hot_t[u][:], -1.0, None, ALU.add).then_inc(S["hot_m"], 1)
                for c in range(1, C1, 2):
                    for u in both:
                        dve.wait_ge(up_ps, U * C1 * i + (U * c + u + 1))
                        dve.wait_ge(down_done, U * C1 * i + (U * c + u + 1))
                        nc.vector.tensor_scalar(hidden[1][u][:], ps_e[u][:], b1[:, c:c + 1], 0.0, ALU.add, ALU.max).then_inc(hidden_odd, 1)
                for u in both:
                    ready(dve, S["y_t_ps"], i, u)
                    dve.wait_ge(out_done[u], 16 * i + 16)
                    nc.vector.tensor_tensor(x4[u][:].rearrange("p t f -> p (t f)"), x3[u][:].rearrange("p t f -> p (t f)"), ps_t[u][:],
                                            ALU.add).then_inc(S["x4"], 1)

        @block.scalar
        def _(act):
            with act.Fori(0, G // U) as i:
                for u in both:
                    ready(act, S["xnt_ps"], i, u)
                    nc.scalar.copy(xnt[u][:], ps_t[u][:]).then_inc(S["xnt"], 1)
                for u in both:
                    ready(act, S["wh_ps"], i, u)
                    nc.scalar.copy(wh[u][:].rearrange("p t f -> p (t f)"), ps_w[u][:]).then_inc(S["wh"], 1)
                    ready(act, S["score_ps"], i, u)
                    nc.scalar.mul(scaled[u][:], ps_e[u][:], SLOPE).then_inc(S["scaled"], 1)
                for u in both:
                    ready(act, S["neg_max"], i, u)
                    freed(act, S["prob_t_ps"], i, u)
                    for t in range(GT):
                        last = nc.scalar.activation(prob[u][:, t, :], score[u][:, t, :], ACT.Exp, bias=neg_max[u][:, t:t + 1],
                                                    accum_out=sums[u][:, t:t + 1])
                    last.then_inc(S["exp"], 1)
                for u in both:
                    ready(act, S["hn_ps"], i, u)
                    nc.scalar.activation(new[u][:], ps_w[u][:], ACT.Identity, bias=b_hh[:, 2:3]).then_inc(S["hn"], 1)
                for u in both:
                    ready(act, S["prob_t_ps"], i, u)
                    nc.scalar.copy(prob_t[u][:].rearrange("p t f -> p (t f)"), ps_t[u][:]).then_inc(S["prob_t"], 1)
                for u in both:
                    ready(act, S["mixed_ps"], i, u)
                    nc.scalar.copy(mixed[u][:], ps_w[u][:]).then_inc(S["mixed"], 1)
                for u in both:
                    ready(act, S["r_ps"], i, u)
                    nc.scalar.activation(gate_r[u][:], ps_t[u][:], ACT.Tanh, bias=b_gate[:, 0:1], scale=0.5).then_inc(S["gate_r"], 1)
                for u in both:
                    ready(act, S["z_ps"], i, u)
                    nc.scalar.activation(gate_z[u][:], ps_e[u][:], ACT.Tanh, bias=b_gate[:, 1:2], scale=0.5).then_inc(S["gate_z"], 1)
                for u in both:
                    ready(act, S["pre"], i, u)
                    nc.scalar.activation(new[u][:], gate_r[u][:], ACT.Tanh, bias=b_ih[:, 2:3]).then_inc(S["new"], 1)
                for u in both:
                    ready(act, S["xnt1_ps"], i, u)
                    nc.scalar.copy(xnt[u][:], ps_e[u][:]).then_inc(S["xnt1"], 1)
                for u in both:
                    ready(act, S["hot_ps"], i, u)
                    nc.scalar.copy(hot_t[u][:], ps_t[u][0:E1, :]).then_inc(S["hot_t"], 1)
                for c in range(0, C1, 2):
                    for u in both:
                        act.wait_ge(up_ps, U * C1 * i + (U * c + u + 1))
                        act.wait_ge(down_done, U * C1 * i + (U * c + u + 1))
                        nc.scalar.activation(hidden[0][u][:], ps_w[u][:], ACT.Relu, bias=b1[:, c:c + 1]).then_inc(hidden_even, 1)
                for u in both:
                    act.wait_ge(down_done, U * C1 * i + (U * (C1 + 1) + u + 1))
                    nc.scalar.activation(mixed[u][:], ps_r[u][:], ACT.Relu).then_inc(S["y"], 1)

        @block.tensor
        def _(pe):
            def turn(dst, src):
                for t in range(GT):
                    last = nc.tensor.transpose(dst[:, t * P:(t + 1) * P], src[:, t * P:(t + 1) * P], K.ident[:])
                return last

            def flat(a):
                return a[:].rearrange("p t f -> p (t f)")

            with pe.Fori(0, G // U) as i:
                for u in both:
                    ready(pe, S["xn"], i, u)
                    freed(pe, S["x4"], i, u)
                    turn(ps_t[u], flat(T.xn[u])).then_inc(S["xnt_ps"], 1)
                for u in both:
                    ready(pe, S["xnt"], i, u)
                    for t in range(GT):
                        last = nc.tensor.matmul(ps_w[u][:, t * P:(t + 1) * P], xnt[u][:, t * P:(t + 1) * P], K.w_att[:, 1, :],
                                                start=True, stop=True)
                    last.then_inc(S["wh_ps"], 1)
                    ready(pe, S["closed"], i, u)
                    nc.tensor.matmul(ps_e[u][:], K.w_score[:, 3, :], xnt[u][:], start=True, stop=False)
                    for t in range(GT):
                        nc.tensor.matmul(ps_e[u][:, t * P:(t + 1) * P], xnt[u][:, t * P:(t + 1) * P], K.w_score[:, 2, :],
                                         start=False, stop=False, skip_group_check=True)
                    nc.tensor.matmul(ps_e[u][:], K.ident_b[:], closed[u][:], start=False, stop=True).then_inc(S["score_ps"], 1)
                for u in both:
                    ready(pe, S["wh"], i, u)
                    nc.tensor.matmul(ps_w[u][:], w_hh[:, 2, :], xnt[u][:], start=True, stop=True).then_inc(S["hn_ps"], 1)
                for u in both:
                    ready(pe, S["prob"], i, u)
                    turn(ps_t[u], flat(prob[u])).then_inc(S["prob_t_ps"], 1)
                for u in both:
                    ready(pe, S["prob_t"], i, u)
                    ready(pe, S["hn"], i, u)
                    for t in range(GT):
                        last = nc.tensor.matmul(ps_w[u][:, t * P:(t + 1) * P], wh[u][:, t, :], prob_t[u][:, t, :],
                                                start=True, stop=True)
                    last.then_inc(S["mixed_ps"], 1)
                for u in both:
                    ready(pe, S["mixed"], i, u)
                    for k, (ps, n) in enumerate(((ps_t, "r_ps"), (ps_e, "z_ps"))):
                        nc.tensor.matmul(ps[u][:], w_hh[:, k, :], xnt[u][:], start=True, stop=False)
                        nc.tensor.matmul(ps[u][:], w_ih[:, k, :], mixed[u][:], start=False, stop=True).then_inc(S[n], 1)
                    nc.tensor.matmul(ps_r[u][:], w_ih[:, 2, :], mixed[u][:], start=True, stop=True).then_inc(S["in_ps"], 1)
                for u in both:
                    ready(pe, S["gru"], i, u)
                    turn(ps_t[u], mixed[u]).then_inc(S["gru_ps"], 1)
                for u in both:
                    ready(pe, S["xn1"], i, u)
                    turn(ps_e[u], flat(T.xn[u])).then_inc(S["xnt1_ps"], 1)
                for u in both:
                    ready(pe, S["xnt1"], i, u)
                    for t in range(GT):
                        last = nc.tensor.matmul(ps_r[u][:, t * E1:(t + 1) * E1], xnt[u][:, t * P:(t + 1) * P], w_r1[:],
                                                start=True, stop=True)
                    last.then_inc(S["logit_ps"], 1)
                for u in both:
                    ready(pe, S["only_hot"], i, u)
                    for t in range(GT):
                        last = nc.tensor.transpose(ps_t[u][0:E1, t * P:(t + 1) * P], T.hot[u][:, 0, t, :], K.ident[:])
                    last.then_inc(S["hot_ps"], 1)
                for c in range(C1 + 1):
                    for u in both:
                        if c < C1:
                            bank_, done = ((ps_w, hidden_even), (ps_e, hidden_odd))[c % 2]
                            if c == 0:
                                ready(pe, S["hot_m"], i, u)
                            else:
                                pe.wait_ge(done, U * (C1 // 2) * i + (U * (c // 2) + u + 1))
                            nc.tensor.matmul(bank_[u][:], w1[:, c, :], xnt[u][:], start=True, stop=False)
                            nc.tensor.matmul(bank_[u][:], shut[:, c, :], hot_m[u][:], start=False, stop=True).then_inc(up_ps, 1)
                        if c > 0:
                            d = c - 1
                            done = (hidden_even, hidden_odd)[d % 2]
                            pe.wait_ge(done, U * (C1 // 2) * i + (U * (d // 2) + u + 1 + U))
                            if d == 0:
                                nc.tensor.matmul(ps_r[u][:], b2[:], hot_t[u][:], start=True, stop=False)
                            last = nc.tensor.matmul(ps_r[u][:], w2[:, d, :], hidden[d % 2][u][:], start=False, stop=(d == C1 - 1))
                            last.then_inc(down_done, 1)
                for u in both:
                    ready(pe, S["y"], i, u)
                    turn(ps_t[u], mixed[u]).then_inc(S["y_t_ps"], 1)


INPUTS = ["x", "adj", "L0_gnn_W", "L0_gnn_a", "L0_ffn_Wr", "L0_ffn_W1s", "L0_ffn_b1s", "L0_ffn_W2s", "L0_ffn_b2s", "L0_ffn_W1p",
          "L0_ffn_b1p", "L0_ffn_W2p", "L0_ffn_b2p", "L1_gnn_W", "L1_gnn_a", "L1_gnn_w_ih", "L1_gnn_w_hh", "L1_gnn_b_ih",
          "L1_gnn_b_hh", "L1_ffn_router_w", "L1_ffn_router_b", "L1_ffn_W1", "L1_ffn_b1", "L1_ffn_W2", "L1_ffn_b2"]


def two_gnn_moe_blocks(nc, W, out):
    with ExitStack() as ctx:
        X = ctx.enter_context(nc.sbuf_tensor("X", [P, B, P], F32))
        K = Constants(ctx, nc)
        setup(nc, ctx, K, W)
        with ExitStack() as first:
            XNT = first.enter_context(nc.sbuf_tensor("XNT", [P, B * P], F32))
            MASK = first.enter_context(nc.sbuf_tensor("MASK", [P, B, E0], F32))
            phase_a(nc, K, X, XNT, MASK, W["x"], W["adj"])
            phase_b(nc, K, X, XNT, MASK, W)
        phase_c(nc, K, X, W, W["adj"], out)


def laid_out(inputs):
    import numpy as np
    a = {n: np.asarray(v) for n, v in inputs.items()}
    for l in ("L0_gnn_a", "L1_gnn_a"):
        a[l] = a[l].reshape(2, P).T
    a["L0_ffn_b1s"] = a["L0_ffn_b1s"].reshape(FC, P).T
    a["L0_ffn_b1p"] = a["L0_ffn_b1p"].reshape(E0, FC, P).transpose(2, 0, 1)
    a["L0_ffn_b2s"] = a["L0_ffn_b2s"].reshape(P, 1)
    for l in ("L1_gnn_w_ih", "L1_gnn_w_hh"):
        a[l] = a[l].reshape(3, P, P).transpose(2, 0, 1)
    for l in ("L1_gnn_b_ih", "L1_gnn_b_hh"):
        a[l] = a[l].reshape(3, P).T
    a["L1_ffn_router_w"] = a["L1_ffn_router_w"].T
    a["L1_ffn_router_b"] = a["L1_ffn_router_b"].reshape(1, E1)
    a["L1_ffn_W1"] = a["L1_ffn_W1"].transpose(1, 0, 2).reshape(P, C1, P)
    a["L1_ffn_b1"] = a["L1_ffn_b1"].reshape(C1, P).T
    a["L1_ffn_W2"] = a["L1_ffn_W2"].reshape(C1, P, P).transpose(1, 0, 2)
    return {n: np.ascontiguousarray(v) for n, v in a.items()}


def kernel(**inputs):
    import concourse.bacc as bacc
    from concourse.bass_utils import run_bass_kernel_spmd

    nc = bacc.Bacc("TRN2", target_bir_lowering=False, num_devices=1)
    arrays = laid_out({n: inputs[n] for n in INPUTS})
    W = {n: nc.dram_tensor(n, arrays[n].shape, mybir.dt.from_np(arrays[n].dtype), kind="ExternalInput").ap() for n in INPUTS}
    out = nc.dram_tensor("out", (B, P, P), F32, kind="ExternalOutput").ap()
    two_gnn_moe_blocks(nc, W, out)
    return run_bass_kernel_spmd(nc, [arrays], core_ids=[0]).results[0]["out"]
```

```python
from contextlib import ExitStack, contextmanager

import concourse.bass as bass
from concourse import mybir

P = 128
B = 64
GT = 4
G = B // GT
TOK = GT * P
U = 4
E0, F0, K0 = 8, 512, 2
FC = F0 // P
NP = B * P * K0 // P + E0
UT = 8
NI = NP // UT
LAG = 2
E_BITS = 3
assert NP % UT == 0 and E0 <= 2 ** E_BITS and E_BITS * (UT + LAG) <= 31
E1, H1 = 32, 32
EC = P // H1
C1 = E1 // EC
EPS = 1e-5
SLOPE = 0.2
BIG = 2.0 ** 60

F32 = mybir.dt.float32
F32R = mybir.dt.float32r
BF16 = mybir.dt.bfloat16
I32 = mybir.dt.int32
U32 = mybir.dt.uint32
ALU = mybir.AluOpType
ACT = mybir.ActivationFunctionType
AXX = mybir.AxisListType.X


def ready(eng, sem, i, u):
    eng.wait_ge(sem, U * i + (u + 1 + U))


def freed(eng, sem, i, u):
    eng.wait_ge(sem, U * i + (u + 1))


def landed(eng, sem, i):
    eng.wait_ge(sem, 16 * i + 16)


@contextmanager
def phase_semaphores(nc, prefix):
    with ExitStack() as ctx:
        made = []

        def sem(name):
            made.append(ctx.enter_context(nc.semaphore(prefix + name)))
            return made[-1]

        yield sem
        with nc.Block() as block:
            @block.gpsimd
            def _(pool):
                for s in made:
                    pool.sem_clear(s)


def stages(sem, names):
    return {name: sem(name) for name in names.split()}


def normalise(nc, dve, i, src, T, S, n, arrived, meanwhile=None):
    for u in range(U):
        arrived(u)
        for t in range(GT):
            last = nc.vector.bn_stats(T.stats[u][:, t, :], src[u][:, t, :])
        last.then_inc(S["stats" + n], 1)
    for u in range(U):
        ready(dve, S["stats" + n], i, u)
        even, odd = T.stats[u][:, :, 0:3], T.stats[u][:, :, 3:6]
        nc.vector.tensor_tensor(T.half[u][:, 0], even[:, :, 1], odd[:, :, 1], ALU.add)
        nc.vector.tensor_tensor(T.half[u][:, 1], even[:, :, 1], odd[:, :, 1], ALU.subtract)
        nc.vector.tensor_tensor(T.half[u][:, 2], even[:, :, 2], odd[:, :, 2], ALU.add).then_inc(S["halves" + n], 1)
    for u in range(U):
        ready(dve, S["halves" + n], i, u)
        nc.vector.tensor_scalar(T.mom[u][:, 0], T.half[u][:, 0], 0.5, None, ALU.mult)
        nc.vector.scalar_tensor_tensor(T.mom[u][:, 1], T.half[u][:, 1], 0.25, T.half[u][:, 1], ALU.mult, ALU.mult)
        nc.vector.tensor_scalar(T.mom[u][:, 2], T.half[u][:, 2], 1.0 / P, EPS, ALU.mult, ALU.add).then_inc(S["moments" + n], 1)
    for u in range(U):
        ready(dve, S["moments" + n], i, u)
        nc.vector.tensor_tensor(T.var[u][:], T.mom[u][:, 1], T.mom[u][:, 2], ALU.add).then_inc(S["var" + n], 1)
    if meanwhile is not None:
        meanwhile()
    for u in range(U):
        ready(dve, S["rstd" + n], i, u)
        for t in range(GT):
            last = nc.vector.tensor_scalar(T.xn[u][:, t, :], src[u][:, t, :], T.mom[u][:, 0, t:t + 1], T.rstd[u][:, t:t + 1],
                                           ALU.subtract, ALU.mult)
        last.then_inc(S["xn" + n], 1)


def one_hot(nc, dve, i, src, T, S, K, experts, k, came, n):
    def wide(a):
        return a.unsqueeze(2).to_broadcast([P, GT, experts])

    index_of = K.iota[:, 0:experts].unsqueeze(1).to_broadcast([P, GT, experts])
    for u in range(U):
        ready(dve, came, i, u)
        nc.vector.tensor_reduce(T.top[u][:, k], src[u][:], AXX, ALU.max).then_inc(S[n + "_max"], 1)
    for u in range(U):
        ready(dve, S[n + "_max"], i, u)
        nc.vector.tensor_tensor(T.equal[u][:], src[u][:], wide(T.top[u][:, k]), ALU.is_equal).then_inc(S[n + "_eq"], 1)
    for u in range(U):
        ready(dve, S[n + "_eq"], i, u)
        nc.vector.scalar_tensor_tensor(T.key[u][:], T.equal[u][:], -float(experts), index_of, ALU.mult, ALU.add).then_inc(S[n + "_key"], 1)
    for u in range(U):
        ready(dve, S[n + "_key"], i, u)
        nc.vector.tensor_reduce(T.index[u][:, k], T.key[u][:], AXX, ALU.min).then_inc(S[n + "_index"], 1)
    for u in range(U):
        ready(dve, S[n + "_index"], i, u)
        nc.vector.tensor_tensor(T.hot[u][:, k], T.key[u][:], wide(T.index[u][:, k]), ALU.is_equal).then_inc(S[n + "_hot"], 1)


class Tiles:

    def __init__(self, sb, experts, picks):
        self.stats, self.half, self.mom = sb("stats", [P, GT, 6]), sb("half", [P, 3, GT]), sb("mom", [P, 3, GT])
        self.var, self.rstd, self.xn = sb("var", [P, GT]), sb("rstd", [P, GT]), sb("xn", [P, GT, P])
        self.equal, self.key = sb("equal", [P, GT, experts]), sb("key", [P, GT, experts])
        self.top, self.index = sb("top", [P, picks, GT]), sb("index", [P, picks, GT])
        self.hot = sb("hot", [P, picks, GT, experts])


def setup(nc, ctx, K, W):
    with phase_semaphores(nc, "setup_") as sem, ExitStack() as tmp:
        def sb(name, shape, dt=F32):
            return tmp.enter_context(nc.sbuf_tensor(name, shape, dt))

        a_col = sb("a_col", [P, 4])
        a_rep = sb("a_rep", [P, 4, P])
        w_t = sb("w_t", [P, 2, P])
        loaded, zeroed, ident_made, ident_cast = sem("loaded"), sem("zeroed"), sem("ident_made"), sem("ident_cast")
        wt_ps, wt_sb, rep_made, wa_ps, wa_sb = sem("wt_ps"), sem("wt_sb"), sem("rep_made"), sem("wa_ps"), sem("wa_sb")
        iota_made = sem("iota_made")
        ps = tmp.enter_context(nc.psum_tensor("setup_ps", [P, 2, 512], F32))
        ps2 = tmp.enter_context(nc.psum_tensor("setup_ps2", [P, 512], F32))
        block = tmp.enter_context(nc.Block())
        loads = [
            (K.w_att[:, 0, :], W["L0_gnn_W"]), (K.w_att[:, 1, :], W["L1_gnn_W"]),
            (a_col[:, 0:2], W["L0_gnn_a"]),
            (a_col[:, 2:4], W["L1_gnn_a"]),
            (K.w_r0[:], W["L0_ffn_Wr"]),
        ]

        @block.sync
        def _(sp):
            for dst, src in loads:
                sp.dma_start(dst, src).then_inc(loaded, 16)

        @block.gpsimd
        def _(pool):
            nc.gpsimd.memset(K.ident[:], 0.0).then_inc(zeroed, 1)
            nc.gpsimd.memset(K.nhalf[:], -0.5)
            nc.gpsimd.iota(K.iota_i[:], [[1, E1]], base=0, channel_multiplier=0).then_inc(iota_made, 1)
            pool.wait_ge(zeroed, 1)
            nc.gpsimd.affine_select(out=K.ident[:], in_=K.ident[:], compare_op=ALU.not_equal, fill=1.0, base=0,
                                    pattern=[[-1, P]], channel_multiplier=1).then_inc(ident_made, 1)

        @block.tensor
        def _(pe):
            pe.wait_ge(ident_made, 1)
            pe.wait_ge(loaded, 16 * len(loads))
            for l in range(2):
                last = nc.tensor.transpose(ps[:, l, 0:P], K.w_att[:, l, :], K.ident[:])
            last.then_inc(wt_ps, 1)
            pe.wait_ge(wt_sb, 1)
            pe.wait_ge(rep_made, 1)
            for l in range(2):
                for k in range(2):
                    m = 2 * l + k
                    last = nc.tensor.matmul(ps2[:, m * P:(m + 1) * P], w_t[:, l, :], a_rep[:, m, :], start=True, stop=True)
            last.then_inc(wa_ps, 1)

        @block.vector
        def _(dve):
            dve.wait_ge(iota_made, 1)
            nc.vector.tensor_copy(K.iota[:], K.iota_i[:])
            dve.wait_ge(ident_made, 1)
            nc.vector.tensor_copy(K.ident_b[:], K.ident[:]).then_inc(ident_cast, 1)
            dve.wait_ge(loaded, 16 * len(loads))
            nc.vector.tensor_copy(a_rep[:], a_col[:].unsqueeze(2).to_broadcast([P, 4, P])).then_inc(rep_made, 1)
            dve.wait_ge(wt_ps, 1)
            nc.vector.tensor_copy(w_t[:], ps[:, :, 0:P]).then_inc(wt_sb, 1)
            dve.wait_ge(wa_ps, 1)
            nc.vector.tensor_copy(K.w_score[:], ps2[:].rearrange("p (m f) -> p m f", m=4)).then_inc(wa_sb, 1)


class Constants:
    def __init__(self, ctx, nc):
        def sb(name, shape, dt=F32):
            return ctx.enter_context(nc.sbuf_tensor(name, shape, dt))

        self.ident = sb("ident", [P, P])
        self.ident_b = sb("ident_b", [P, P], BF16)
        self.nhalf = sb("nhalf", [P, GT])
        self.iota_i = sb("iota_i", [P, E1], I32)
        self.iota = sb("iota", [P, E1])
        self.w_att = sb("w_att", [P, 2, P])
        self.w_score = sb("w_score", [P, 4, P])
        self.w_r0 = sb("w_r0", [P, E0])


def phase_a(nc, K, X, XNT, R, x, adj):
    with phase_semaphores(nc, "a_") as sem, ExitStack() as ctx:
        def sb(name, shape, dt=F32):
            return [ctx.enter_context(nc.sbuf_tensor(f"a_{name}{u}", shape, dt)) for u in range(U)]

        def bank(name):
            return [ctx.enter_context(nc.psum_tensor(f"a_{name}{u}", [P, 512], F32)) for u in range(U)]

        adj_sb = sb("adj", [P, GT, P], I32)
        closed = sb("closed", [P, TOK], BF16)
        x_new, x1 = sb("x_new", [P, GT, P]), sb("x1", [P, GT, P])
        T = Tiles(sb, E0, K0)
        xnt = sb("xnt", [P, TOK])
        wh, scaled, score = sb("wh", [P, GT, P]), sb("scaled", [P, TOK]), sb("score", [P, GT, P])
        neg_max, sums, inv = sb("neg_max", [P, GT]), sb("sums", [P, GT]), sb("inv", [P, GT])
        prob, prob_t, gain = sb("prob", [P, GT, P]), sb("prob_t", [P, GT, P]), sb("gain", [P, GT, P])
        logit, rest = sb("logit", [P, GT, E0]), sb("rest", [P, GT, E0])
        gap, ratio, den = sb("gap", [P, GT]), sb("ratio", [P, GT]), sb("den", [P, GT])
        weight = sb("weight", [P, K0, GT])
        ps_a, ps_b = bank("ps_a"), bank("ps_b")

        S = stages(sem, """
            closed stats halves moments var rstd xn xnt_ps xnt wh_ps score_ps wh scaled score neg_max prob inv
            prob_t_ps prob_t mixed gain x1 stats1 halves1 moments1 var1 rstd1 xn1 xnt1_ps xnt1 kept logit_ps logit
            first_max first_eq first_key first_index first_hot rest second_max second_eq second_key
            second_index second_hot gap ratio den w0 w1 hot_kept w_kept x_kept""")
        x_in = [sem(f"x_in{u}") for u in range(U)]
        adj_in = [sem(f"adj_in{u}") for u in range(U)]
        units = range(U)
        rows_out = [sem(f"rows_out{u}") for u in range(U)]
        xd = x.rearrange("b p f -> p b f")
        ad = adj.rearrange("b p f -> p b f")

        with nc.Block() as start:
            @start.gpsimd
            def _(pool):
                for s in S.values():
                    pool.sem_inc(s, U)
                for u in range(U):
                    pool.sem_inc(rows_out[u], 16)

        block = ctx.enter_context(nc.Block())

        @block.sync
        def _(sp):
            def load(i, u):
                sp.dma_start(x_new[u][:], xd[:, bass.ds((U * i + u) * GT, GT), :]).then_inc(x_in[u], 16)
                sp.dma_start(adj_sb[u][:], ad[:, bass.ds((U * i + u) * GT, GT), :]).then_inc(adj_in[u], 16)

            def store(i, u):
                ready(sp, S["xn1"], i, u)
                sp.dma_start(R.rows[:, bass.ds((U * i + u) * GT, GT), :], T.xn[u][:]).then_inc(rows_out[u], 16)

            for u in units:
                load(0, u)
            with sp.Fori(0, G // U - 1) as i:
                for u in units:
                    ready(sp, S["closed"], i, u)
                    ready(sp, S["x1"], i, u)
                    load(i + 1, u)
                for u in units:
                    store(i, u)
            for u in units:
                store(G // U - 1, u)
            for u in units:
                sp.wait_ge(rows_out[u], 16 * (G // U) + 16)

        @block.gpsimd
        def _(pool):
            with pool.Fori(0, G // U) as i:
                for u in units:
                    ready(pool, S["var"], i, u)
                    nc.gpsimd.tensor_tensor(T.rstd[u][:], T.var[u][:], K.nhalf[:], ALU.pow).then_inc(S["rstd"], 1)
                for u in units:
                    ready(pool, S["x1"], i, u)
                    nc.gpsimd.tensor_copy(X[:, bass.ds((U * i + u) * GT, GT), :], x1[u][:]).then_inc(S["x_kept"], 1)
                for u in units:
                    ready(pool, S["var1"], i, u)
                    nc.gpsimd.tensor_tensor(T.rstd[u][:], T.var[u][:], K.nhalf[:], ALU.pow).then_inc(S["rstd1"], 1)
                for u in units:
                    ready(pool, S["xnt1"], i, u)
                    nc.gpsimd.tensor_copy(XNT[:, bass.ds((U * i + u) * TOK, TOK)], xnt[u][:]).then_inc(S["kept"], 1)

        @block.vector
        def _(dve):
            with dve.Fori(0, G // U) as i:
                def close():
                    for u in units:
                        landed(dve, adj_in[u], i)
                        freed(dve, S["score_ps"], i, u)
                        nc.vector.tensor_scalar(closed[u][:], adj_sb[u][:].rearrange("p t f -> p (t f)"), 0.0, -BIG,
                                                ALU.is_le, ALU.mult).then_inc(S["closed"], 1)

                for u in units:
                    dve.wait_ge(rows_out[u], 16 * i + 16)
                normalise(nc, dve, i, x_new, T, S, "", lambda u: landed(dve, x_in[u], i), close)
                for u in units:
                    ready(dve, S["scaled"], i, u)
                    freed(dve, S["prob"], i, u)
                    nc.vector.tensor_tensor(score[u][:].rearrange("p t f -> p (t f)"), scaled[u][:], ps_b[u][:],
                                            ALU.max).then_inc(S["score"], 1)
                for u in units:
                    ready(dve, S["score"], i, u)
                    nc.vector.tensor_reduce(neg_max[u][:], score[u][:], AXX, ALU.max, negate=True).then_inc(S["neg_max"], 1)
                for u in units:
                    ready(dve, S["prob"], i, u)
                    nc.vector.reciprocal(inv[u][:], sums[u][:]).then_inc(S["inv"], 1)
                for u in units:
                    ready(dve, S["inv"], i, u)
                    ready(dve, S["mixed"], i, u)
                    for t in range(GT):
                        last = nc.vector.tensor_scalar(gain[u][:, t, :], ps_b[u][:, t * P:(t + 1) * P], inv[u][:, t:t + 1],
                                                       0.0, ALU.mult, ALU.max)
                    last.then_inc(S["gain"], 1)
                for u in units:
                    ready(dve, S["gain"], i, u)
                    freed(dve, S["x_kept"], i, u)
                    nc.vector.tensor_tensor(x1[u][:], x_new[u][:], gain[u][:], ALU.add).then_inc(S["x1"], 1)
                normalise(nc, dve, i, x1, T, S, "1", lambda u: ready(dve, S["x1"], i, u))
                for u in units:
                    ready(dve, S["logit_ps"], i, u)
                    nc.vector.tensor_copy(logit[u][:].rearrange("p t e -> p (t e)"), ps_b[u][:, 0:GT * E0]).then_inc(S["logit"], 1)
                one_hot(nc, dve, i, logit, T, S, K, E0, 0, S["logit"], "first")
                for u in units:
                    ready(dve, S["first_hot"], i, u)
                    nc.vector.scalar_tensor_tensor(rest[u][:], T.hot[u][:, 0], -BIG, logit[u][:], ALU.mult, ALU.add).then_inc(S["rest"], 1)
                one_hot(nc, dve, i, rest, T, S, K, E0, 1, S["rest"], "second")
                for u in units:
                    nc.vector.tensor_tensor(gap[u][:], T.top[u][:, 1], T.top[u][:, 0], ALU.subtract).then_inc(S["gap"], 1)
                for u in units:
                    ready(dve, S["ratio"], i, u)
                    nc.vector.tensor_scalar(den[u][:], ratio[u][:], 1.0, None, ALU.add).then_inc(S["den"], 1)
                for u in units:
                    ready(dve, S["den"], i, u)
                    nc.vector.reciprocal(weight[u][:, 0], den[u][:]).then_inc(S["w0"], 1)
                for u in units:
                    ready(dve, S["w0"], i, u)
                    nc.vector.tensor_tensor(weight[u][:, 1], weight[u][:, 0], ratio[u][:], ALU.mult).then_inc(S["w1"], 1)
                for u in units:
                    ready(dve, S["second_hot"], i, u)
                    for k in range(K0):
                        last = nc.vector.tensor_copy(R.hot[k][:, bass.ds((U * i + u) * GT, GT), :], T.hot[u][:, k])
                    last.then_inc(S["hot_kept"], 1)
                    ready(dve, S["w1"], i, u)
                    for k in range(K0):
                        last = nc.vector.tensor_copy(R.weight[:, bass.ds((U * i + u) * GT, GT), k], weight[u][:, k])
                    last.then_inc(S["w_kept"], 1)

        @block.scalar
        def _(act):
            with act.Fori(0, G // U) as i:
                for u in units:
                    ready(act, S["xnt_ps"], i, u)
                    freed(act, S["kept"], i, u)
                    nc.scalar.copy(xnt[u][:], ps_a[u][:]).then_inc(S["xnt"], 1)
                for u in units:
                    ready(act, S["wh_ps"], i, u)
                    nc.scalar.copy(wh[u][:].rearrange("p t f -> p (t f)"), ps_a[u][:]).then_inc(S["wh"], 1)
                    ready(act, S["score_ps"], i, u)
                    nc.scalar.mul(scaled[u][:], ps_b[u][:], SLOPE).then_inc(S["scaled"], 1)
                for u in units:
                    ready(act, S["neg_max"], i, u)
                    freed(act, S["prob_t_ps"], i, u)
                    for t in range(GT):
                        last = nc.scalar.activation(prob[u][:, t, :], score[u][:, t, :], ACT.Exp, bias=neg_max[u][:, t:t + 1],
                                                    accum_out=sums[u][:, t:t + 1])
                    last.then_inc(S["prob"], 1)
                for u in units:
                    ready(act, S["prob_t_ps"], i, u)
                    nc.scalar.copy(prob_t[u][:].rearrange("p t f -> p (t f)"), ps_a[u][:]).then_inc(S["prob_t"], 1)
                for u in units:
                    ready(act, S["xnt1_ps"], i, u)
                    nc.scalar.copy(xnt[u][:], ps_a[u][:]).then_inc(S["xnt1"], 1)
                for u in units:
                    ready(act, S["gap"], i, u)
                    nc.scalar.activation(ratio[u][:], gap[u][:], ACT.Exp).then_inc(S["ratio"], 1)

        @block.tensor
        def _(pe):
            with pe.Fori(0, G // U) as i:
                for u in units:
                    ready(pe, S["xn"], i, u)
                    freed(pe, S["xnt1"], i, u)
                    for t in range(GT):
                        last = nc.tensor.transpose(ps_a[u][:, t * P:(t + 1) * P], T.xn[u][:, t, :], K.ident[:])
                    last.then_inc(S["xnt_ps"], 1)
                for u in units:
                    ready(pe, S["xnt"], i, u)
                    for t in range(GT):
                        last = nc.tensor.matmul(ps_a[u][:, t * P:(t + 1) * P], xnt[u][:, t * P:(t + 1) * P], K.w_att[:, 0, :],
                                                start=True, stop=True)
                    last.then_inc(S["wh_ps"], 1)
                    freed(pe, S["logit"], i, u)
                    ready(pe, S["closed"], i, u)
                    nc.tensor.matmul(ps_b[u][:], K.w_score[:, 1, :], xnt[u][:], start=True, stop=False)
                    for t in range(GT):
                        nc.tensor.matmul(ps_b[u][:, t * P:(t + 1) * P], xnt[u][:, t * P:(t + 1) * P], K.w_score[:, 0, :],
                                         start=False, stop=False, skip_group_check=True)
                    nc.tensor.matmul(ps_b[u][:], K.ident_b[:], closed[u][:], start=False, stop=True).then_inc(S["score_ps"], 1)
                for u in units:
                    ready(pe, S["prob"], i, u)
                    for t in range(GT):
                        last = nc.tensor.transpose(ps_a[u][:, t * P:(t + 1) * P], prob[u][:, t, :], K.ident[:])
                    last.then_inc(S["prob_t_ps"], 1)
                for u in units:
                    ready(pe, S["prob_t"], i, u)
                    for t in range(GT):
                        last = nc.tensor.matmul(ps_b[u][:, t * P:(t + 1) * P], prob_t[u][:, t, :], wh[u][:, t, :],
                                                start=True, stop=True)
                    last.then_inc(S["mixed"], 1)
                for u in units:
                    ready(pe, S["xn1"], i, u)
                    for t in range(GT):
                        last = nc.tensor.transpose(ps_a[u][:, t * P:(t + 1) * P], T.xn[u][:, t, :], K.ident[:])
                    last.then_inc(S["xnt1_ps"], 1)
                for u in units:
                    ready(pe, S["xnt1"], i, u)
                    for t in range(GT):
                        last = nc.tensor.matmul(ps_b[u][:, t * E0:(t + 1) * E0], xnt[u][:, t * P:(t + 1) * P], K.w_r0[:],
                                                start=True, stop=True)
                    last.then_inc(S["logit_ps"], 1)


class Routing:

    def __init__(self, ctx, nc):
        def sb(name, shape, dt=F32):
            return ctx.enter_context(nc.sbuf_tensor(name, shape, dt))

        self.hot = [sb(f"hot_{k}", [P, B, E0]) for k in range(K0)]
        self.weight = sb("pick_weight", [P, B, K0])
        self.slot = sb("slot", [P, B, K0], U32)
        self.expert = sb("tile_experts", [1, NI], U32)
        self.cleared = ctx.enter_context(nc.semaphore("rows_cleared"))
        self.rows = nc.dram_tensor("rows", (P, B, P), F32, kind="Internal").ap()
        self.sorted = nc.dram_tensor("sorted_rows", (NP * P, P), F32, kind="Internal").ap()
        self.routed = nc.dram_tensor("routed_rows", (NP * P, P), F32, kind="Internal").ap()


def clear_rows(nc, R):
    with nc.sbuf_tensor("no_rows", [P, NP * P // 4], F32) as zeros, phase_semaphores(nc, "clear_") as sem:
        zeroed = sem("zeroed")
        with nc.Block() as block:
            @block.vector
            def _(dve):
                nc.vector.memset(zeros[:], 0.0).then_inc(zeroed, 1)

            @block.sync
            def _(sp):
                sp.wait_ge(zeroed, 1)
                for n in range(4):
                    sp.dma_start(R.sorted.rearrange("(n p r) f -> n p (r f)", n=4, p=P)[n], zeros[:]).then_inc(R.cleared, 16)
                sp.wait_ge(R.cleared, 64)


def sort_picks(nc, K, R):
    with phase_semaphores(nc, "s_") as sem, ExitStack() as ctx:
        def sb(name, shape, dt=F32):
            return ctx.enter_context(nc.sbuf_tensor("s_" + name, shape, dt))

        earlier_f, earlier, ones = sb("earlier_f", [P, P]), sb("earlier", [P, P], BF16), sb("ones", [P, P], BF16)
        hots = sb("hots", [P, B * E0], BF16)
        count, run = sb("count", [P, B, E0]), [sb(f"run{n}", [P, B, E0]) for n in range(2)]
        rounded, tiles_i, tiles = sb("rounded", [P, E0], I32), sb("tiles_i", [P, E0], I32), sb("tiles", [P, E0])
        ends = [sb(f"ends{n}", [P, E0]) for n in range(2)]
        first, before, row = sb("first", [P, E0]), sb("before", [P, B, E0]), sb("row", [P, B, E0])
        own, slot_f = sb("own", [P, B, E0]), sb("slot_f", [P, B, K0])
        tile_i, tile_f = sb("tile_i", [1, NP], I32), sb("tile_f", [1, NP])
        past, expert_f, expert = sb("past", [1, NP, E0]), sb("expert_f", [1, NP]), sb("expert", [1, UT + NP], U32)
        ps_rank = ctx.enter_context(nc.psum_tensor("s_ps_rank", [P, B, E0], F32))
        ps_count = ctx.enter_context(nc.psum_tensor("s_ps_count", [P, B, E0], F32))
        zeroed, masks_made, tile_made, hots_made, counted, step = (sem(n) for n in ("zeroed", "masks_made", "tile_made", "hots_made", "counted", "step"))
        block = ctx.enter_context(nc.Block())

        @block.gpsimd
        def _(pool):
            nc.gpsimd.iota(tile_i[:], [[1, NP]], base=0, channel_multiplier=0).then_inc(tile_made, 1)
            nc.gpsimd.memset(earlier_f[:], 1.0).then_inc(zeroed, 1)
            pool.wait_ge(zeroed, 1)
            nc.gpsimd.affine_select(out=earlier_f[:], in_=earlier_f[:], compare_op=ALU.is_gt, fill=0.0, base=0,
                                    pattern=[[1, P]], channel_multiplier=-1).then_inc(masks_made, 1)

        @block.tensor
        def _(pe):
            pe.wait_ge(hots_made, 1)
            nc.tensor.matmul(ps_rank[:].rearrange("p b e -> p (b e)"), earlier[:], hots[:], start=True, stop=True)
            nc.tensor.matmul(ps_count[:].rearrange("p b e -> p (b e)"), ones[:], hots[:], start=True, stop=True).then_inc(counted, 1)

        @block.vector
        def _(dve):
            steps = [0]

            def then(ins):
                steps[0] += 1
                ins.then_inc(step, 1)
                dve.wait_ge(step, steps[0])

            def running(a, n, size):
                s = 1
                while s < size:
                    nc.vector.tensor_copy(a[1 - n][:, 0:s], a[n][:, 0:s])
                    then(nc.vector.tensor_tensor(a[1 - n][:, s:size], a[n][:, s:size], a[n][:, 0:size - s], ALU.add))
                    n, s = 1 - n, 2 * s
                return a[n]

            nc.vector.memset(ones[:], 1.0)
            nc.vector.memset(expert[:, 0:UT], 0)
            nc.vector.memset(R.expert[:], 0)
            dve.wait_ge(tile_made, 1)
            nc.vector.tensor_copy(tile_f[:], tile_i[:])
            dve.wait_ge(masks_made, 1)
            nc.vector.tensor_copy(earlier[:], earlier_f[:])
            nc.vector.tensor_tensor(hots[:].rearrange("p (b e) -> p b e", e=E0), R.hot[0][:], R.hot[1][:], ALU.add).then_inc(hots_made, 1)
            dve.wait_ge(counted, 1)
            nc.vector.tensor_copy(count[:], ps_count[:])
            then(nc.vector.tensor_copy(run[0][:], ps_count[:]))
            upto = running(run, 0, B)
            then(nc.vector.tensor_scalar(rounded[:], upto[:, B - 1, :], float(P - 1), None, ALU.add))
            then(nc.vector.tensor_scalar(tiles_i[:], rounded[:], 7, None, ALU.logical_shift_right))
            nc.vector.tensor_copy(tiles[:], tiles_i[:])
            then(nc.vector.tensor_copy(ends[0][:], tiles_i[:]))
            end = running(ends, 0, E0)
            nc.vector.tensor_tensor(past[:], tile_f[:].unsqueeze(2).to_broadcast([1, NP, E0]),
                                    end[0:1].unsqueeze(1).to_broadcast([1, NP, E0]), ALU.is_ge)
            nc.vector.tensor_tensor(before[:], upto[:], count[:], ALU.subtract)
            then(nc.vector.tensor_tensor(first[:], end[:], tiles[:], ALU.subtract))
            nc.vector.tensor_reduce(expert_f[:], past[:], AXX, ALU.add)
            then(nc.vector.scalar_tensor_tensor(before[:], first[:].unsqueeze(1).to_broadcast([P, B, E0]), float(P), before[:],
                                                ALU.mult, ALU.add))
            nc.vector.tensor_scalar(expert[:, UT:], expert_f[:], float(E0 - 1), None, ALU.min)
            then(nc.vector.tensor_tensor(row[:], before[:], ps_rank[:], ALU.add))
            for k in range(UT + LAG):
                tiles_k = expert[:, UT - LAG + k:UT - LAG + k + UT * (NI - 1) + 1:UT]
                then(nc.vector.scalar_tensor_tensor(R.expert[:], tiles_k, E_BITS * k, R.expert[:], ALU.logical_shift_left,
                                                    ALU.bitwise_or))
            for k in range(K0):
                then(nc.vector.tensor_tensor(own[:], row[:], R.hot[k][:], ALU.mult))
                then(nc.vector.tensor_reduce(slot_f[:, :, k], own[:], AXX, ALU.add))
            nc.vector.tensor_copy(R.slot[:], slot_f[:])


class Experts:

    def __init__(self, ctx, nc):
        self.b = ctx.enter_context(nc.sbuf_tensor("e_b", [2, E0 * (F0 + P)], F32R))
        self.b1 = self.b[:, 0:E0 * F0].rearrange("o (e f) -> o e f", e=E0)
        self.b2 = self.b[:, E0 * F0:].rearrange("o (e f) -> o e f", e=E0)
        self.ones = ctx.enter_context(nc.sbuf_tensor("e_ones", [2, P], F32R))

    def hold_weights(self, ctx, nc):
        self.w = ctx.enter_context(nc.sbuf_tensor("e_w", [P, 2, 2 * E0, F0], F32R))


def split_biases(nc, E, W):
    with phase_semaphores(nc, "eb_") as sem, ExitStack() as ctx:
        raw = ctx.enter_context(nc.sbuf_tensor("eb_raw", [2, E0 * (F0 + P)], F32))
        low = ctx.enter_context(nc.sbuf_tensor("eb_low", [2, E0 * (F0 + P)], F32R))
        ones = ctx.enter_context(nc.sbuf_tensor("eb_ones", [2, P], F32))
        loaded, high_made, low_made, moved, ones_made = (sem(n) for n in ("loaded", "high_made", "low_made", "moved", "ones_made"))
        block = ctx.enter_context(nc.Block())

        @block.sync
        def _(sp):
            for r in range(2):
                sp.dma_start(raw[r:r + 1, 0:E0 * F0], W["L0_ffn_b1p"]).then_inc(loaded, 16)
                sp.dma_start(raw[r:r + 1, E0 * F0:], W["L0_ffn_b2p"]).then_inc(loaded, 16)

        @block.gpsimd
        def _(pool):
            pool.wait_ge(low_made, 1)
            pool.dma_start(E.b[1:2], low[1:2]).then_inc(moved, 16)
            pool.wait_ge(moved, 16)

        @block.vector
        def _(dve):
            nc.vector.memset(ones[:], 1.0).then_inc(ones_made, 1)
            dve.wait_ge(ones_made, 1)
            nc.vector.tensor_copy(E.ones[:], ones[:])
            dve.wait_ge(loaded, 64)
            nc.vector.tensor_copy(E.b[:], raw[:]).then_inc(high_made, 1)
            dve.wait_ge(high_made, 1)
            nc.vector.tensor_tensor(low[:], raw[:], E.b[:].bitcast(F32), ALU.subtract).then_inc(low_made, 1)


def shared_expert(nc, K, X, XNT, R, E, W):
    with phase_semaphores(nc, "b_") as sem, ExitStack() as ctx:
        def sb(name, shape, dt=F32):
            return ctx.enter_context(nc.sbuf_tensor("b_" + name, shape, dt))

        w1_raw, w2_raw = sb("w1_raw", [P, F0]), sb("w2_raw", [P, FC, P])
        w1, w2 = [sb(f"w1_{h}", [P, F0], F32R) for h in "hl"], [sb(f"w2_{h}", [P, FC, P], F32R) for h in "hl"]
        b1, b2 = sb("b1", [P, FC]), sb("b2", [P, 1])
        raw = [sb(f"raw{k}", [P, F0]) for k in range(2)]
        rows = [sb(f"rows{k}", [P, GT, P]) for k in range(2)]
        slots = [sb(f"slots{k}", [P, GT * K0]) for k in range(2)]
        xs = [sb(f"x_{h}", [P, TOK], F32R) for h in "hl"]
        hidden = [sb(f"hidden{k}", [P, TOK]) for k in range(2)]
        hs = [[sb(f"hs{k}{h}", [P, TOK], F32R) for h in "hl"] for k in range(2)]
        total = sb("total", [P, TOK])
        gate = sb("gate", [P, 1])

        def bank(name, n):
            return [ctx.enter_context(nc.psum_tensor(f"b_{name}{k}", [P, 512], F32)) for k in range(n)]

        ps_h, ps_y, ps_t = bank("ps_h", 3), bank("ps_y", 1)[0], bank("ps_t", 1)[0]
        PASSES = ((0, 0), (0, 1), (1, 0))

        w_loaded, w_high = sem("w_loaded"), sem("w_high")
        with ExitStack() as tmp:
            start = tmp.enter_context(nc.Block())

            @start.sync
            def _(sp):
                sp.dma_start(w1_raw[:], W["L0_ffn_W1s"]).then_inc(w_loaded, 16)
                sp.dma_start(w2_raw[:], W["L0_ffn_W2s"].rearrange("(c f) d -> f c d", c=FC)).then_inc(w_loaded, 16)
                sp.dma_start(b1[:], W["L0_ffn_b1s"]).then_inc(w_loaded, 16)
                sp.dma_start(b2[:], W["L0_ffn_b2s"]).then_inc(w_loaded, 16)
                sp.wait_ge(w_loaded, 64)

            @start.vector
            def _(dve):
                dve.wait_ge(w_loaded, 64)
                nc.vector.tensor_copy(w1[0][:], w1_raw[:])
                nc.vector.tensor_copy(w2[0][:], w2_raw[:]).then_inc(w_high, 1)
                dve.wait_ge(w_high, 1)
                nc.vector.tensor_tensor(w1[1][:], w1_raw[:], w1[0][:].bitcast(F32), ALU.subtract)
                nc.vector.tensor_tensor(w2[1][:], w2_raw[:], w2[0][:].bitcast(F32), ALU.subtract)

            @start.gpsimd
            def _(pool):
                pool.wait_ge(R.cleared, 64)

        x_high, x_low, h_ps, h_act, h_high, h_low, h_used = (sem(n) for n in ("x_high", "x_low", "h_ps", "h_act", "h_high", "h_low", "h_used"))
        y_out, out_ps, x_done, gated = sem("y_out"), sem("out_ps"), sem("x_done"), sem("gated")
        raw_in, rows_in, slots_in, scattered = ([sem(f"{n}{k}") for k in range(2)] for n in ("raw_in", "rows_in", "slots_in", "scattered"))
        raw_high, raw_low = sem("raw_high"), sem("raw_low")
        SCATTERS = 16 * GT * K0
        with nc.Block() as credits:
            @credits.gpsimd
            def _(pool):
                for s, n in ((h_ps, 1), (h_act, 3), (h_low, 2), (h_used, 2), (gated, 1), (y_out, 1), (out_ps, 1), (x_done, 1)):
                    pool.sem_inc(s, n)

        block = ctx.enter_context(nc.Block())

        @block.sync
        def _(sp):
            def load(g, k):
                sp.dma_start(rows[k][:], R.rows[:, bass.ds(g * GT, GT), :]).then_inc(rows_in[k], 16)
                sp.dma_start(slots[k][:], R.slot[:, bass.ds(g * GT, GT), :].bitcast(F32).rearrange("p t k -> p (t k)")).then_inc(slots_in[k], 16)
                sp.dma_start(raw[k][:], W["L0_ffn_Wp"][:, bass.ds(g, 1), :].rearrange("p o f -> p (o f)")).then_inc(raw_in[k], 16)

            for k in range(2):
                load(k, k)
            with sp.Fori(1, G // 2) as i:
                for k in range(2):
                    sp.wait_ge(scattered[k], SCATTERS * i)
                    sp.wait_ge(raw_low, 2 * i + (k - 1))
                    load(2 * i + k, k)
            for k in range(2):
                sp.wait_ge(scattered[k], SCATTERS * (G // 2))

        @block.gpsimd
        def _(pool):
            with pool.Fori(0, G // 2) as i:
                for k in range(2):
                    pool.wait_ge(rows_in[k], 16 * i + 16)
                    pool.wait_ge(slots_in[k], 16 * i + 16)
                    pool.wait_ge(gated, 2 * i + (k + 1))
                    nc.gpsimd.tensor_tensor(gate[:], K.nhalf[:, 0:1], K.nhalf[:, 0:1], ALU.add).then_inc(gated, 1)
                    for t in range(GT):
                        for j in range(K0):
                            n = K0 * t + j
                            pool.indirect_dma_start(R.sorted, bass.IndirectOffsetOnAxis(ap=slots[k][:, n:n + 1].bitcast(U32), axis=0),
                                                    rows[k][:, t, :], None).then_inc(scattered[k], 16)

        @block.tensor
        def _(pe):
            with pe.Fori(0, G) as g:
                def up(c):
                    if c == 0:
                        pe.wait_ge(x_low, g + 1)
                    pe.wait_ge(h_act, FC * g + (c + 1))
                    for n, (a, b) in enumerate(PASSES):
                        last = nc.tensor.matmul(ps_h[c % 3][:], w1[a][:, c * P:(c + 1) * P], xs[b][:], start=(n == 0), stop=(n == 2))
                    last.then_inc(h_ps, 1)

                def down(c):
                    if c == 0:
                        pe.wait_ge(y_out, g + 1)
                    pe.wait_ge(h_low, FC * g + (c + 3))
                    for n, (a, b) in enumerate(PASSES):
                        last = nc.tensor.matmul(ps_y[:], w2[a][:, c, :], hs[c % 2][b][:], start=(c == 0 and n == 0),
                                                stop=(c == FC - 1 and n == 2))
                    last.then_inc(h_used, 1)

                for c in range(FC + 2):
                    if c < FC:
                        up(c)
                    if c >= 2:
                        down(c - 2)
                pe.wait_ge(y_out, g + 2)
                pe.wait_ge(x_done, g + 1)
                for t in range(GT):
                    last = nc.tensor.transpose(ps_t[:, t * P:(t + 1) * P], total[:, t * P:(t + 1) * P], K.ident[:])
                last.then_inc(out_ps, 1)

        @block.scalar
        def _(act):
            with act.Fori(0, G // 2) as i:
                for k in range(2):
                    g = 2 * i + k
                    act.wait_ge(h_ps, FC * g + 1)
                    nc.scalar.copy(xs[0][:], XNT[:, bass.ds(g * TOK, TOK)]).then_inc(x_high, 1)
                    for c in range(FC):
                        act.wait_ge(h_ps, FC * g + (c + 2))
                        act.wait_ge(h_low, FC * g + (c + 1))
                        nc.scalar.activation(hidden[c % 2][:], ps_h[c % 3][:], ACT.Gelu, bias=b1[:, c:c + 1]).then_inc(h_act, 1)
                    act.wait_ge(h_used, FC * g + (FC + 2))
                    act.wait_ge(out_ps, g + 1)
                    nc.scalar.activation(total[:], ps_y[:], ACT.Identity, bias=b2[:]).then_inc(y_out, 1)
                    act.wait_ge(raw_in[k], 16 * i + 16)
                    nc.scalar.copy(E.w[:, 0, bass.ds(g, 1), :].rearrange("p o f -> p (o f)"), raw[k][:]).then_inc(raw_high, 1)

        @block.vector
        def _(dve):
            with dve.Fori(0, G // 2) as i:
                for k in range(2):
                    g = 2 * i + k
                    dve.wait_ge(x_high, g + 1)
                    nc.vector.tensor_tensor(xs[1][:], XNT[:, bass.ds(g * TOK, TOK)], xs[0][:].bitcast(F32), ALU.subtract).then_inc(x_low, 1)
                    for c in range(FC):
                        dve.wait_ge(h_act, FC * g + (c + 4))
                        dve.wait_ge(h_used, FC * g + (c + 1))
                        nc.vector.tensor_copy(hs[c % 2][0][:], hidden[c % 2][:]).then_inc(h_high, 1)
                        dve.wait_ge(h_high, FC * g + (c + 1))
                        nc.vector.tensor_tensor(hs[c % 2][1][:], hidden[c % 2][:], hs[c % 2][0][:].bitcast(F32),
                                                ALU.subtract).then_inc(h_low, 1)
                    dve.wait_ge(raw_high, g + 1)
                    high = E.w[:, 0, bass.ds(g, 1), :].rearrange("p o f -> p (o f)").bitcast(F32)
                    nc.vector.tensor_tensor(E.w[:, 1, bass.ds(g, 1), :].rearrange("p o f -> p (o f)"), raw[k][:], high,
                                            ALU.subtract).then_inc(raw_low, 1)
                    dve.wait_ge(out_ps, g + 2)
                    nc.vector.tensor_tensor(X[:, bass.ds(g * GT, GT), :], X[:, bass.ds(g * GT, GT), :],
                                            ps_t[:].rearrange("p (t f) -> p t f", t=GT), ALU.add).then_inc(x_done, 1)


def routed_experts(nc, K, R, E):
    with phase_semaphores(nc, "r_") as sem, ExitStack() as ctx:
        def sb(name, shape, dt=F32, n=2):
            return [ctx.enter_context(nc.sbuf_tensor(f"r_{name}{k}", shape, dt)) for k in range(n)]

        def bank(name, n=2):
            return [ctx.enter_context(nc.psum_tensor(f"r_{name}{k}", [P, 512], F32)) for k in range(n)]

        rows = sb("rows", [P, P], n=UT)
        x_h, x_l = sb("x_h", [P, P], F32R), sb("x_l", [P, P], F32R)
        hidden = sb("hidden", [P, F0])
        h_h, h_l = sb("h_h", [P, F0], F32R), sb("h_l", [P, F0], F32R)
        y = sb("y", [P, P], n=UT)
        ps_x, ps_h, ps_t, ps_y = bank("ps_x"), bank("ps_h"), bank("ps_t"), bank("ps_y")
        x_ps, x_high, x_low, h_ps, h_act, t_ps, h_high, h_low, y_ps, y_sb = (
            sem(n) for n in ("x_ps", "x_high", "x_low", "h_ps", "h_act", "t_ps", "h_high", "h_low", "y_ps", "y_sb"))
        rows_in, y_stored = [sem(f"rows_in{k}") for k in range(UT)], [sem(f"y_stored{k}") for k in range(UT)]

        def after(eng, s, i, j, back=0):
            if not (isinstance(i, int) and UT * i + j - back < 0):
                eng.wait_ge(s, UT * i + (j - back + 1))

        block = ctx.enter_context(nc.Block())

        @block.sync
        def _(sp):
            def load(i, j):
                if not isinstance(i, int) or i > 0:
                    after(sp, x_ps, i, j, UT)
                sp.dma_start(rows[j][:], R.sorted.rearrange("(n p) f -> p n f", p=P)[:, bass.ds(UT * i + j, 1), :]
                             .rearrange("p o f -> p (o f)")).then_inc(rows_in[j], 16)

            def store(i, j):
                after(sp, y_sb, i, j)
                sp.dma_start(R.routed.rearrange("(n p) f -> p n f", p=P)[:, bass.ds(UT * i + j, 1), :]
                             .rearrange("p o f -> p (o f)"), y[j][:]).then_inc(y_stored[j], 16)

            for j in range(UT):
                load(0, j)
            with sp.Fori(0, NI - 1) as i:
                for j in range(UT):
                    load(i + 1, j)
                    store(i, j)
            for j in range(UT):
                store(NI - 1, j)
            for j in range(UT):
                sp.wait_ge(y_stored[j], 16 * NI)

        def tile_before(i, j):
            return (i + j // UT if j // UT else i, j % UT)

        def exists(i, j):
            return not isinstance(i, int) or 0 <= i < NI

        @block.tensor
        def _(pe):
            def tile_experts(i):
                packed = pe.value_load(R.expert[:, bass.ds(i, 1)], min_val=0, max_val=2 ** (E_BITS * (UT + LAG)) - 1)
                return [(packed >> (E_BITS * k)) & (E0 - 1) for k in range(UT + LAG)]

            def turn_rows(i, j):
                pe.wait_ge(rows_in[j], 16 * i + 16)
                after(pe, x_low, i, j, 2)
                nc.tensor.transpose(ps_x[j % 2][:, 0:P], rows[j][:], K.ident[:]).then_inc(x_ps, 1)

            def up(i, j, e):
                after(pe, h_act, i, j, 2)
                nc.tensor.matmul(ps_h[j % 2][:], E.ones[:], E.b1[:, bass.ds(e, 1), :].rearrange("p o f -> p (o f)"), start=True, stop=False)
                after(pe, x_low, i, j)
                w = [E.w[:, part, bass.ds(e, 1), :].rearrange("p o f -> p (o f)") for part in range(2)]
                nc.tensor.matmul(ps_h[j % 2][:], x_h[j % 2][:], w[0], start=False, stop=False)
                nc.tensor.matmul(ps_h[j % 2][:], x_h[j % 2][:], w[1], start=False, stop=False)
                nc.tensor.matmul(ps_h[j % 2][:], x_l[j % 2][:], w[0], start=False, stop=True).then_inc(h_ps, 1)

            def turn_hidden(i, j):
                after(pe, h_act, i, j)
                after(pe, h_low, i, j, 2)
                for c in range(FC):
                    last = nc.tensor.transpose(ps_t[j % 2][:, c * P:(c + 1) * P], hidden[j % 2][:, c * P:(c + 1) * P], K.ident[:])
                last.then_inc(t_ps, 1)

            def down(i, j, e):
                after(pe, y_sb, i, j, 2)
                after(pe, h_low, i, j)
                for c in range(FC):
                    cols = slice(c * P, (c + 1) * P)
                    w = E.w[:, :, bass.ds(e + E0, 1), cols].rearrange("p h o f -> p h (o f)")
                    nc.tensor.matmul(ps_y[j % 2][:, 0:2 * P], h_h[j % 2][:, cols], w, start=(c == 0), stop=(c == FC - 1),
                                     skip_group_check=True)
                    last = nc.tensor.matmul(ps_y[j % 2][:, 0:P], h_l[j % 2][:, cols], w[:, 0, :], start=False, stop=(c == FC - 1),
                                     skip_group_check=True)
                last = nc.tensor.matmul(ps_y[j % 2][:, 0:P], E.ones[:], E.b2[:, bass.ds(e, 1), :].rearrange("p o f -> p (o f)"),
                                        start=False, stop=True, skip_group_check=True)
                last.then_inc(y_ps, 1)

            def body(i):
                experts = tile_experts(i)
                for j in range(UT):
                    for stage, ahead in ((turn_rows, 1), (up, 0), (turn_hidden, -1), (down, -LAG)):
                        a, b = tile_before(i, j + ahead)
                        if exists(a, b):
                            stage(a, b, experts[j + ahead + LAG]) if stage in (up, down) else stage(a, b)

            turn_rows(0, 0)
            body(0)
            with pe.Fori(1, NI - 1) as i:
                body(i)
            body(NI - 1)
            turn_hidden(NI - 1, UT - 1)
            for j in range(UT - LAG, UT):
                down(NI - 1, j, tile_experts(NI - 1)[j + LAG])

        @block.scalar
        def _(act):
            def round_rows(i, j):
                after(act, x_ps, i, j)
                after(act, h_ps, i, j, 2)
                nc.scalar.copy(x_h[j % 2][:], ps_x[j % 2][:, 0:P]).then_inc(x_high, 1)

            def gelu(i, j):
                after(act, h_ps, i, j)
                after(act, t_ps, i, j, 2)
                nc.scalar.activation(hidden[j % 2][:], ps_h[j % 2][:], ACT.Gelu).then_inc(h_act, 1)

            def round_hidden(i, j):
                after(act, t_ps, i, j)
                after(act, y_ps, i, j, 2)
                nc.scalar.copy(h_h[j % 2][:], ps_t[j % 2][:]).then_inc(h_high, 1)

            def body(i):
                for j in range(UT):
                    for stage, ahead in ((round_rows, 1), (gelu, 0), (round_hidden, -1)):
                        a, b = tile_before(i, j + ahead)
                        if exists(a, b):
                            stage(a, b)

            round_rows(0, 0)
            body(0)
            with act.Fori(1, NI - 1) as i:
                body(i)
            body(NI - 1)
            round_hidden(NI - 1, UT - 1)

        @block.vector
        def _(dve):
            def rest_rows(i, j):
                after(dve, x_high, i, j)
                nc.vector.tensor_tensor(x_l[j % 2][:], ps_x[j % 2][:, 0:P], x_h[j % 2][:].bitcast(F32), ALU.subtract).then_inc(x_low, 1)

            def rest_hidden(i, j):
                after(dve, h_high, i, j)
                nc.vector.tensor_tensor(h_l[j % 2][:], ps_t[j % 2][:], h_h[j % 2][:].bitcast(F32), ALU.subtract).then_inc(h_low, 1)

            def take(i, j):
                after(dve, y_ps, i, j)
                if not isinstance(i, int) or i > 0:
                    dve.wait_ge(y_stored[j], 16 * i)
                nc.vector.tensor_reduce(y[j][:], ps_y[j % 2][:, 0:2 * P].rearrange("p (h f) -> p f h", h=2), AXX, ALU.add).then_inc(y_sb, 1)

            def body(i):
                for j in range(UT):
                    for stage, ahead in ((rest_rows, 1), (rest_hidden, -1), (take, -2)):
                        a, b = tile_before(i, j + ahead)
                        if exists(a, b):
                            stage(a, b)

            rest_rows(0, 0)
            body(0)
            with dve.Fori(1, NI - 1) as i:
                body(i)
            body(NI - 1)
            rest_hidden(NI - 1, UT - 1)
            take(NI - 1, UT - 2)
            take(NI - 1, UT - 1)


def phase_c(nc, K, X, R, W, adj, out):
    with phase_semaphores(nc, "c_") as sem, ExitStack() as ctx:
        def one(name, shape, dt=F32):
            return ctx.enter_context(nc.sbuf_tensor("c_" + name, shape, dt))

        def sb(name, shape, dt=F32):
            return [one(f"{name}{u}", shape, dt) for u in range(U)]

        def bank(name):
            return [ctx.enter_context(nc.psum_tensor(f"c_{name}{u}", [P, 512], F32)) for u in range(U)]

        w_ih, w_hh, w_r1 = one("w_ih", [P, 3, P]), one("w_hh", [P, 3, P]), one("w_r1", [P, E1])
        b_ih, b_hh, b_gate = one("b_ih", [P, 3]), one("b_hh", [P, 3]), one("b_gate", [P, 2])
        b_r1 = one("b_r1", [P, E1])
        w1, b1 = one("w1", [P, C1, P]), one("b1", [P, C1])
        w2, b2 = one("w2", [P, C1, P]), one("b2", [E1, P])
        shut = one("shut", [E1, C1, P], BF16)
        T = Tiles(sb, E1, 1)
        adj_sb, closed = sb("adj", [P, GT, P], I32), sb("closed", [P, TOK], BF16)
        x2, x3, x4 = sb("x2", [P, GT, P]), sb("x3", [P, GT, P]), sb("x4", [P, GT, P])
        xnt, wh, scaled, score = sb("xnt", [P, TOK]), sb("wh", [P, GT, P]), sb("scaled", [P, TOK]), sb("score", [P, GT, P])
        neg_max, sums, inv = sb("neg_max", [P, GT]), sb("sums", [P, GT]), sb("inv", [P, GT])
        prob, mixed, new = sb("prob", [P, GT, P]), sb("mixed", [P, TOK]), sb("new", [P, TOK])
        prob_t = [a.rearrange("p (t f) -> p t f", t=GT) for a in scaled]
        gate_r = [a.rearrange("p t f -> p (t f)") for a in score]
        gate_z = [a.rearrange("p t f -> p (t f)") for a in wh]
        logit, hot_t, hot_m = sb("logit", [P, GT, E1]), sb("hot_t", [E1, TOK]), sb("hot_m", [E1, TOK], BF16)
        hidden = sb("hidden", [P, TOK])
        ps_a, ps_b = bank("ps_a"), bank("ps_b")
        units = range(U)

        slots, weight = sb("slots", [P, GT * K0]), sb("weight", [P, GT * K0])
        pick = sb("pick", [P, GT * K0, P])
        gate, gated = one("gate", [P, 1]), sem("gated")
        slots_in, weight_in, picked = ([sem(f"{n}{u}") for u in units] for n in ("slots_in", "weight_in", "picked"))
        PICKS = 16 * GT * K0
        S = stages(sem, """
            x2_first x2
            closed stats halves moments var rstd xn xnt_ps xnt wh_ps score_ps wh scaled score neg_max exp inv prob
            prob_t_ps prob_t mixed_ps mixed hn_ps r_ps z_ps in_ps gate_r gate_z hn reset pre new gap keep gru gru_ps x3
            stats1 halves1 moments1 var1 rstd1 xn1 xnt1_ps xnt1 logit_ps logit
            only_max only_eq only_key only_index only_hot hot_ps hot_t hot_m down y y_t_ps x4""")
        up_ps, hidden_done = sem("up_ps"), [sem("hidden_even"), sem("hidden_odd")]
        x_in, adj_in, out_done = [sem(f"x_in{u}") for u in units], [sem(f"adj_in{u}") for u in units], [sem(f"out{u}") for u in units]

        w_loaded, b_summed, shut_zero, shut_f32, shut_made = (sem(n) for n in ("w_loaded", "b_summed", "shut_zero", "shut_f32", "shut_made"))
        loads = [(w_ih[:], W["L1_gnn_w_ih"]), (w_hh[:], W["L1_gnn_w_hh"]), (b_ih[:], W["L1_gnn_b_ih"]), (b_hh[:], W["L1_gnn_b_hh"]),
                 (w_r1[:], W["L1_ffn_router_w"]), (b_r1[:], W["L1_ffn_router_b"].to_broadcast([P, E1])),
                 (w1[:], W["L1_ffn_W1"]), (b1[:], W["L1_ffn_b1"]), (w2[:], W["L1_ffn_W2"]), (b2[:], W["L1_ffn_b2"])]
        with ExitStack() as tmp:
            shut_f = tmp.enter_context(nc.sbuf_tensor("c_shut_f", [E1, C1 * P], F32))
            b_sum = tmp.enter_context(nc.sbuf_tensor("c_b_sum", [P, 2], F32))
            start = tmp.enter_context(nc.Block())

            @start.sync
            def _(sp):
                for dst, src in loads:
                    sp.dma_start(dst, src).then_inc(w_loaded, 16)

            @start.gpsimd
            def _(pool):
                for s in S.values():
                    pool.sem_inc(s, U)
                pool.sem_inc(gated, 1)
                for u in units:
                    pool.sem_inc(out_done[u], 16)
                nc.gpsimd.memset(shut_f[:], 0.0).then_inc(shut_zero, 1)
                pool.wait_ge(shut_zero, 1)
                v = shut_f[:].rearrange("k (c e h) -> k c e h", c=C1, e=EC)
                nc.gpsimd.affine_select(out=v, in_=v, compare_op=ALU.not_equal, fill=BIG, base=0,
                                        pattern=[[-EC, C1], [-1, EC], [0, H1]], channel_multiplier=1).then_inc(shut_f32, 1)

            @start.vector
            def _(dve):
                dve.wait_ge(shut_f32, 1)
                nc.vector.tensor_copy(shut[:].rearrange("k c f -> k (c f)"), shut_f[:]).then_inc(shut_made, 1)
                dve.wait_ge(w_loaded, 16 * len(loads))
                nc.vector.tensor_tensor(b_sum[:], b_ih[:, 0:2], b_hh[:, 0:2], ALU.add).then_inc(b_summed, 1)
                dve.wait_ge(b_summed, 1)
                nc.vector.tensor_scalar(b_gate[:], b_sum[:], 0.5, None, ALU.mult)

        ad = adj.rearrange("b p f -> p b f")
        od = out.rearrange("b p f -> p b f")
        block = ctx.enter_context(nc.Block())

        def graphs(i, u):
            return bass.ds((U * i + u) * GT, GT)

        @block.sync
        def _(sp):
            def load(i, u):
                sp.dma_start(slots[u][:], R.slot[:, graphs(i, u), :].bitcast(F32).rearrange("p t k -> p (t k)")).then_inc(slots_in[u], 16)
                sp.dma_start(weight[u][:], R.weight[:, graphs(i, u), :].rearrange("p t k -> p (t k)")).then_inc(weight_in[u], 16)
                sp.dma_start(x2[u][:], X[:, graphs(i, u), :]).then_inc(x_in[u], 16)
                sp.dma_start(adj_sb[u][:], ad[:, graphs(i, u), :]).then_inc(adj_in[u], 16)

            def store(i, u):
                ready(sp, S["x4"], i, u)
                sp.dma_start(od[:, graphs(i, u), :], x4[u][:]).then_inc(out_done[u], 16)

            for u in units:
                load(0, u)
            with sp.Fori(0, G // U - 1) as i:
                for u in units:
                    ready(sp, S["closed"], i, u)
                    ready(sp, S["x3"], i, u)
                    sp.wait_ge(picked[u], PICKS * (i + 1))
                    load(i + 1, u)
                for u in units:
                    store(i, u)
            for u in units:
                store(G // U - 1, u)
            for u in units:
                sp.wait_ge(out_done[u], 16 * (G // U) + 16)

        @block.gpsimd
        def _(pool):
            def gather(i, u):
                pool.wait_ge(slots_in[u], 16 * i + 16)
                pool.wait_ge(gated, U * i + (u + 1))
                nc.gpsimd.tensor_tensor(gate[:], K.nhalf[:, 0:1], K.nhalf[:, 0:1], ALU.add).then_inc(gated, 1)
                for t in range(GT):
                    for k in range(K0):
                        n = K0 * t + k
                        pool.indirect_dma_start(pick[u][:, n, :], None, R.routed,
                                                bass.IndirectOffsetOnAxis(ap=slots[u][:, n:n + 1].bitcast(U32), axis=0)
                                                ).then_inc(picked[u], 16)

            def powers(i, n):
                for u in units:
                    ready(pool, S["var" + n], i, u)
                    nc.gpsimd.tensor_tensor(T.rstd[u][:], T.var[u][:], K.nhalf[:], ALU.pow).then_inc(S["rstd" + n], 1)

            for u in units:
                gather(0, u)
            with pool.Fori(0, G // U - 1) as i:
                powers(i, "")
                powers(i, "1")
                for u in units:
                    ready(pool, S["x2"], i, u)
                    gather(i + 1, u)
            for n in ("", "1"):
                powers(G // U - 1, n)

        @block.vector
        def _(dve):
            with dve.Fori(0, G // U) as i:
                def close():
                    for u in units:
                        landed(dve, adj_in[u], i)
                        freed(dve, S["score_ps"], i, u)
                        nc.vector.tensor_scalar(closed[u][:], adj_sb[u][:].rearrange("p t f -> p (t f)"), 0.0, -BIG,
                                                ALU.is_le, ALU.mult).then_inc(S["closed"], 1)

                for k in range(K0):
                    for u in units:
                        if k == 0:
                            landed(dve, x_in[u], i)
                            landed(dve, weight_in[u], i)
                            dve.wait_ge(picked[u], PICKS * (i + 1))
                        else:
                            ready(dve, S["x2_first"], i, u)
                        for t in range(GT):
                            n = K0 * t + k
                            last = nc.vector.scalar_tensor_tensor(x2[u][:, t, :], pick[u][:, n, :], weight[u][:, n:n + 1], x2[u][:, t, :],
                                                                  ALU.mult, ALU.add)
                        last.then_inc(S["x2" if k else "x2_first"], 1)
                normalise(nc, dve, i, x2, T, S, "", lambda u: ready(dve, S["x2"], i, u), close)
                for u in units:
                    ready(dve, S["scaled"], i, u)
                    freed(dve, S["exp"], i, u)
                    nc.vector.tensor_tensor(score[u][:].rearrange("p t f -> p (t f)"), scaled[u][:], ps_b[u][:],
                                            ALU.max).then_inc(S["score"], 1)
                for u in units:
                    ready(dve, S["score"], i, u)
                    nc.vector.tensor_reduce(neg_max[u][:], score[u][:], AXX, ALU.max, negate=True).then_inc(S["neg_max"], 1)
                for u in units:
                    ready(dve, S["exp"], i, u)
                    nc.vector.reciprocal(inv[u][:], sums[u][:]).then_inc(S["inv"], 1)
                for u in units:
                    ready(dve, S["inv"], i, u)
                    for t in range(GT):
                        last = nc.vector.tensor_scalar(prob[u][:, t, :], prob[u][:, t, :], inv[u][:, t:t + 1], None, ALU.mult)
                    last.then_inc(S["prob"], 1)
                for u in units:
                    ready(dve, S["gate_r"], i, u)
                    ready(dve, S["hn"], i, u)
                    nc.vector.scalar_tensor_tensor(gate_r[u][:], gate_r[u][:], 1.0, new[u][:], ALU.add, ALU.mult).then_inc(S["reset"], 1)
                for u in units:
                    ready(dve, S["reset"], i, u)
                    ready(dve, S["in_ps"], i, u)
                    nc.vector.scalar_tensor_tensor(gate_r[u][:], gate_r[u][:], 0.5, ps_b[u][:], ALU.mult, ALU.add).then_inc(S["pre"], 1)
                for u in units:
                    ready(dve, S["new"], i, u)
                    nc.vector.tensor_tensor(mixed[u][:], xnt[u][:], new[u][:], ALU.subtract).then_inc(S["gap"], 1)
                for u in units:
                    ready(dve, S["gap"], i, u)
                    nc.vector.scalar_tensor_tensor(mixed[u][:], gate_z[u][:], 1.0, mixed[u][:], ALU.add, ALU.mult).then_inc(S["keep"], 1)
                for u in units:
                    ready(dve, S["keep"], i, u)
                    nc.vector.scalar_tensor_tensor(mixed[u][:], mixed[u][:], 0.5, new[u][:], ALU.mult, ALU.add).then_inc(S["gru"], 1)
                for u in units:
                    ready(dve, S["gru_ps"], i, u)
                    freed(dve, S["x4"], i, u)
                    nc.vector.tensor_tensor(x3[u][:].rearrange("p t f -> p (t f)"), x2[u][:].rearrange("p t f -> p (t f)"), ps_a[u][:],
                                            ALU.add).then_inc(S["x3"], 1)
                normalise(nc, dve, i, x3, T, S, "1", lambda u: ready(dve, S["x3"], i, u))
                for u in units:
                    ready(dve, S["logit_ps"], i, u)
                    nc.vector.tensor_tensor(logit[u][:], ps_a[u][:, 0:GT * E1].rearrange("p (t e) -> p t e", e=E1),
                                            b_r1[:].unsqueeze(1).to_broadcast([P, GT, E1]), ALU.add).then_inc(S["logit"], 1)
                one_hot(nc, dve, i, logit, T, S, K, E1, 0, S["logit"], "only")
                for u in units:
                    ready(dve, S["hot_t"], i, u)
                    nc.vector.tensor_scalar(hot_m[u][:], hot_t[u][:], -1.0, None, ALU.add).then_inc(S["hot_m"], 1)
                for c in range(1, C1, 2):
                    for u in units:
                        dve.wait_ge(up_ps, U * C1 * i + (U * c + u + 1))
                        nc.vector.tensor_scalar(hidden[u][:], ps_b[u][:], b1[:, c:c + 1], 0.0, ALU.add, ALU.max).then_inc(hidden_done[1], 1)
                for u in units:
                    ready(dve, S["y_t_ps"], i, u)
                    dve.wait_ge(out_done[u], 16 * i + 16)
                    nc.vector.tensor_tensor(x4[u][:].rearrange("p t f -> p (t f)"), x3[u][:].rearrange("p t f -> p (t f)"), ps_b[u][:],
                                            ALU.add).then_inc(S["x4"], 1)

        @block.scalar
        def _(act):
            with act.Fori(0, G // U) as i:
                for u in units:
                    ready(act, S["xnt_ps"], i, u)
                    nc.scalar.copy(xnt[u][:], ps_a[u][:]).then_inc(S["xnt"], 1)
                for u in units:
                    ready(act, S["wh_ps"], i, u)
                    nc.scalar.copy(wh[u][:].rearrange("p t f -> p (t f)"), ps_a[u][:]).then_inc(S["wh"], 1)
                    ready(act, S["score_ps"], i, u)
                    nc.scalar.mul(scaled[u][:], ps_b[u][:], SLOPE).then_inc(S["scaled"], 1)
                for u in units:
                    ready(act, S["neg_max"], i, u)
                    freed(act, S["prob_t_ps"], i, u)
                    for t in range(GT):
                        last = nc.scalar.activation(prob[u][:, t, :], score[u][:, t, :], ACT.Exp, bias=neg_max[u][:, t:t + 1],
                                                    accum_out=sums[u][:, t:t + 1])
                    last.then_inc(S["exp"], 1)
                for u in units:
                    ready(act, S["hn_ps"], i, u)
                    nc.scalar.activation(new[u][:], ps_a[u][:], ACT.Identity, bias=b_hh[:, 2:3]).then_inc(S["hn"], 1)
                for u in units:
                    ready(act, S["prob_t_ps"], i, u)
                    nc.scalar.copy(scaled[u][:], ps_b[u][:]).then_inc(S["prob_t"], 1)
                for u in units:
                    ready(act, S["mixed_ps"], i, u)
                    nc.scalar.copy(mixed[u][:], ps_a[u][:]).then_inc(S["mixed"], 1)
                for u in units:
                    ready(act, S["r_ps"], i, u)
                    nc.scalar.activation(gate_r[u][:], ps_b[u][:], ACT.Tanh, bias=b_gate[:, 0:1], scale=0.5).then_inc(S["gate_r"], 1)
                for u in units:
                    ready(act, S["z_ps"], i, u)
                    nc.scalar.activation(gate_z[u][:], ps_a[u][:], ACT.Tanh, bias=b_gate[:, 1:2], scale=0.5).then_inc(S["gate_z"], 1)
                for u in units:
                    ready(act, S["pre"], i, u)
                    nc.scalar.activation(new[u][:], gate_r[u][:], ACT.Tanh, bias=b_ih[:, 2:3]).then_inc(S["new"], 1)
                for u in units:
                    ready(act, S["xnt1_ps"], i, u)
                    nc.scalar.copy(xnt[u][:], ps_b[u][:]).then_inc(S["xnt1"], 1)
                for u in units:
                    ready(act, S["hot_ps"], i, u)
                    nc.scalar.copy(hot_t[u][:], ps_b[u][0:E1, :]).then_inc(S["hot_t"], 1)
                for c in range(0, C1, 2):
                    for u in units:
                        act.wait_ge(up_ps, U * C1 * i + (U * c + u + 1))
                        nc.scalar.activation(hidden[u][:], ps_b[u][:], ACT.Relu, bias=b1[:, c:c + 1]).then_inc(hidden_done[0], 1)
                for u in units:
                    ready(act, S["down"], i, u)
                    nc.scalar.activation(mixed[u][:], ps_a[u][:], ACT.Relu).then_inc(S["y"], 1)

        @block.tensor
        def _(pe):
            def turn(dst, src):
                for t in range(GT):
                    last = nc.tensor.transpose(dst[:, t * P:(t + 1) * P], src[:, t * P:(t + 1) * P], K.ident[:])
                return last

            def flat(a):
                return a[:].rearrange("p t f -> p (t f)")

            with pe.Fori(0, G // U) as i:
                for u in units:
                    ready(pe, S["xn"], i, u)
                    freed(pe, S["y"], i, u)
                    turn(ps_a[u], flat(T.xn[u])).then_inc(S["xnt_ps"], 1)
                for u in units:
                    ready(pe, S["xnt"], i, u)
                    for t in range(GT):
                        last = nc.tensor.matmul(ps_a[u][:, t * P:(t + 1) * P], xnt[u][:, t * P:(t + 1) * P], K.w_att[:, 1, :],
                                                start=True, stop=True)
                    last.then_inc(S["wh_ps"], 1)
                    ready(pe, S["closed"], i, u)
                    freed(pe, S["x4"], i, u)
                    nc.tensor.matmul(ps_b[u][:], K.w_score[:, 3, :], xnt[u][:], start=True, stop=False)
                    for t in range(GT):
                        nc.tensor.matmul(ps_b[u][:, t * P:(t + 1) * P], xnt[u][:, t * P:(t + 1) * P], K.w_score[:, 2, :],
                                         start=False, stop=False, skip_group_check=True)
                    nc.tensor.matmul(ps_b[u][:], K.ident_b[:], closed[u][:], start=False, stop=True).then_inc(S["score_ps"], 1)
                for u in units:
                    ready(pe, S["wh"], i, u)
                    nc.tensor.matmul(ps_a[u][:], w_hh[:, 2, :], xnt[u][:], start=True, stop=True).then_inc(S["hn_ps"], 1)
                for u in units:
                    ready(pe, S["prob"], i, u)
                    turn(ps_b[u], flat(prob[u])).then_inc(S["prob_t_ps"], 1)
                for u in units:
                    ready(pe, S["prob_t"], i, u)
                    ready(pe, S["hn"], i, u)
                    for t in range(GT):
                        last = nc.tensor.matmul(ps_a[u][:, t * P:(t + 1) * P], wh[u][:, t, :], prob_t[u][:, t, :],
                                                start=True, stop=True)
                    last.then_inc(S["mixed_ps"], 1)
                for u in units:
                    ready(pe, S["mixed"], i, u)
                    for k, (ps, n) in enumerate(((ps_b, "r_ps"), (ps_a, "z_ps"))):
                        nc.tensor.matmul(ps[u][:], w_hh[:, k, :], xnt[u][:], start=True, stop=False)
                        nc.tensor.matmul(ps[u][:], w_ih[:, k, :], mixed[u][:], start=False, stop=True).then_inc(S[n], 1)
                for u in units:
                    ready(pe, S["gate_r"], i, u)
                    nc.tensor.matmul(ps_b[u][:], w_ih[:, 2, :], mixed[u][:], start=True, stop=True).then_inc(S["in_ps"], 1)
                for u in units:
                    ready(pe, S["gru"], i, u)
                    ready(pe, S["gate_z"], i, u)
                    turn(ps_a[u], mixed[u]).then_inc(S["gru_ps"], 1)
                for u in units:
                    ready(pe, S["xn1"], i, u)
                    turn(ps_b[u], flat(T.xn[u])).then_inc(S["xnt1_ps"], 1)
                for u in units:
                    ready(pe, S["xnt1"], i, u)
                    for t in range(GT):
                        last = nc.tensor.matmul(ps_a[u][:, t * E1:(t + 1) * E1], xnt[u][:, t * P:(t + 1) * P], w_r1[:],
                                                start=True, stop=True)
                    last.then_inc(S["logit_ps"], 1)
                for u in units:
                    ready(pe, S["only_hot"], i, u)
                    for t in range(GT):
                        last = nc.tensor.transpose(ps_b[u][0:E1, t * P:(t + 1) * P], T.hot[u][:, 0, t, :], K.ident[:])
                    last.then_inc(S["hot_ps"], 1)
                def down(c, u):
                    pe.wait_ge(hidden_done[c % 2], U * (C1 // 2) * i + (U * (c // 2) + u + 1))
                    if c == 0:
                        nc.tensor.matmul(ps_a[u][:], b2[:], hot_t[u][:], start=True, stop=False)
                    return nc.tensor.matmul(ps_a[u][:], w2[:, c, :], hidden[u][:], start=False, stop=(c == C1 - 1))

                for c in range(C1):
                    for u in units:
                        if c == 0:
                            ready(pe, S["hot_m"], i, u)
                        else:
                            down(c - 1, u)
                        nc.tensor.matmul(ps_b[u][:], w1[:, c, :], xnt[u][:], start=True, stop=False)
                        nc.tensor.matmul(ps_b[u][:], shut[:, c, :], hot_m[u][:], start=False, stop=True).then_inc(up_ps, 1)
                for u in units:
                    down(C1 - 1, u).then_inc(S["down"], 1)
                for u in units:
                    ready(pe, S["y"], i, u)
                    turn(ps_b[u], mixed[u]).then_inc(S["y_t_ps"], 1)


INPUTS = ["x", "adj", "L0_gnn_W", "L0_gnn_a", "L0_ffn_Wr", "L0_ffn_W1s", "L0_ffn_b1s", "L0_ffn_W2s", "L0_ffn_b2s", "L0_ffn_W1p",
          "L0_ffn_b1p", "L0_ffn_W2p", "L0_ffn_b2p", "L1_gnn_W", "L1_gnn_a", "L1_gnn_w_ih", "L1_gnn_w_hh", "L1_gnn_b_ih",
          "L1_gnn_b_hh", "L1_ffn_router_w", "L1_ffn_router_b", "L1_ffn_W1", "L1_ffn_b1", "L1_ffn_W2", "L1_ffn_b2"]


def two_gnn_moe_blocks(nc, W, out):
    with ExitStack() as ctx:
        X = ctx.enter_context(nc.sbuf_tensor("X", [P, B, P], F32))
        K = Constants(ctx, nc)
        setup(nc, ctx, K, W)
        R = Routing(ctx, nc)
        with ExitStack() as first:
            XNT = first.enter_context(nc.sbuf_tensor("XNT", [P, B * P], F32))
            clear_rows(nc, R)
            phase_a(nc, K, X, XNT, R, W["x"], W["adj"])
            sort_picks(nc, K, R)
            with ExitStack() as experts:
                E = Experts(experts, nc)
                split_biases(nc, E, W)
                E.hold_weights(experts, nc)
                shared_expert(nc, K, X, XNT, R, E, W)
                routed_experts(nc, K, R, E)
        phase_c(nc, K, X, R, W, W["adj"], out)


def laid_out(inputs):
    import numpy as np
    a = {n: np.asarray(v) for n, v in inputs.items()}
    for l in ("L0_gnn_a", "L1_gnn_a"):
        a[l] = a[l].reshape(2, P).T
    a["L0_ffn_b1s"] = a["L0_ffn_b1s"].reshape(FC, P).T
    w1p, w2p = a.pop("L0_ffn_W1p"), a.pop("L0_ffn_W2p")
    w2p = w2p.reshape(E0, FC, P, P).transpose(0, 2, 1, 3).reshape(E0, P, F0)
    a["L0_ffn_Wp"] = np.stack([w1p, w2p]).reshape(2 * E0, P, F0).transpose(1, 0, 2)
    a["L0_ffn_b1p"] = a["L0_ffn_b1p"].reshape(1, E0 * F0)
    a["L0_ffn_b2p"] = a["L0_ffn_b2p"].reshape(1, E0 * P)
    a["L0_ffn_b2s"] = a["L0_ffn_b2s"].reshape(P, 1)
    for l in ("L1_gnn_w_ih", "L1_gnn_w_hh"):
        a[l] = a[l].reshape(3, P, P).transpose(2, 0, 1)
    for l in ("L1_gnn_b_ih", "L1_gnn_b_hh"):
        a[l] = a[l].reshape(3, P).T
    a["L1_ffn_router_w"] = a["L1_ffn_router_w"].T
    a["L1_ffn_router_b"] = a["L1_ffn_router_b"].reshape(1, E1)
    a["L1_ffn_W1"] = a["L1_ffn_W1"].transpose(1, 0, 2).reshape(P, C1, P)
    a["L1_ffn_b1"] = a["L1_ffn_b1"].reshape(C1, P).T
    a["L1_ffn_W2"] = a["L1_ffn_W2"].reshape(C1, P, P).transpose(1, 0, 2)
    return {n: np.ascontiguousarray(v) for n, v in a.items()}


def kernel(**inputs):
    import concourse.bacc as bacc
    from concourse.bass_utils import run_bass_kernel_spmd

    nc = bacc.Bacc("TRN2", target_bir_lowering=False, num_devices=1)
    arrays = laid_out({n: inputs[n] for n in INPUTS})
    W = {n: nc.dram_tensor(n, a.shape, mybir.dt.from_np(a.dtype), kind="ExternalInput").ap() for n, a in arrays.items()}
    out = nc.dram_tensor("out", (B, P, P), F32, kind="ExternalOutput").ap()
    two_gnn_moe_blocks(nc, W, out)
    return run_bass_kernel_spmd(nc, [arrays], core_ids=[0]).results[0]["out"]
```

```python
from contextlib import ExitStack, contextmanager

import concourse.bass as bass
from concourse import mybir

P = 128
B = 64
GT = 4
G = B // GT
TOK = GT * P
U = 4
E0, F0, K0 = 8, 512, 2
FC = F0 // P
NP = B * P * K0 // P + E0
UT = 8
NI = NP // UT
LAG = 2
E_BITS = 3
assert NP % UT == 0 and E0 <= 2 ** E_BITS and E_BITS * (UT + LAG) <= 31
E1, H1 = 32, 32
EC = P // H1
C1 = E1 // EC
EPS = 1e-5
SLOPE = 0.2
BIG = 2.0 ** 60

F32 = mybir.dt.float32
F32R = mybir.dt.float32r
BF16 = mybir.dt.bfloat16
I32 = mybir.dt.int32
U32 = mybir.dt.uint32
ALU = mybir.AluOpType
ACT = mybir.ActivationFunctionType
AXX = mybir.AxisListType.X


A_TIMES = {
    "load": 0.02, "stats": 1.15, "halves": 45.42, "moments": 51.98, "var": 55.36, "rstd": 71.65, "xn": 93.96,
    "turn_xn": 148.66, "take_xnt": 165.92, "close": 173.5, "scores": 215.33, "scale": 227.35, "project": 277.25,
    "take_wh": 300.16, "take_score": 300.39, "top_score": 302.47, "exponents": 305.99, "turn_prob": 344.38, "invert": 400.58,
    "take_prob_t": 414.31, "mix": 415.96, "take_gain": 437.68, "add_gain": 514.37, "stats1": 573.84, "halves1": 586.92,
    "moments1": 622.3, "var1": 637.69, "rstd1": 646.02, "xn1": 724.99, "turn_xn1": 762.71, "store": 775.27,
    "take_xnt1": 781.54, "logits": 797.54, "take_logit": 832.34, "first_max": 839.27, "first_eq": 863.67, "clear": 877.97,
    "first_key": 885.97, "first_index": 896.61, "first_hot": 912.53, "others": 915.71, "second_max": 916.76,
    "take_gap": 917.33, "second_eq": 918.86, "take_ratio": 928.06, "keep_xnt": 928.17, "second_key": 929.44,
    "denominator": 932.87, "second_index": 935.15, "first_weight": 949.11, "second_hot": 958.72, "keep_x": 965.19,
    "second_weight": 974.18, "keep_picks": 975.27,
}
B_TIMES = {
    "round_x": 41.66, "rest_x": 68.95, "load": 76.83, "up0": 108.23, "gelu0": 167.3, "scatter": 213.47, "up1": 218.51,
    "round_weight": 219.68, "high0": 223.4, "rest_weight": 264.61, "low0": 291.16, "gelu1": 295.3, "down0": 324.68,
    "up2": 378.03, "high1": 378.04, "low1": 400.51, "down1": 437.35, "gelu2": 457.6, "up3": 506.97, "high2": 509.94,
    "low2": 544.75, "down2": 611.22, "gelu3": 611.22, "high3": 670.3, "low3": 727.11, "down3": 769.31, "take_y": 820.75,
    "turn_y": 875.1, "add_y": 932.32,
}
C_TIMES = {
    "load": 1.05, "gather0": 46.75, "gather1": 46.75, "gather2": 59.71, "gather3": 62.97, "close": 108.88,
    "add_picks0": 156.02, "add_picks1": 171.24, "stats": 171.25, "halves": 177.72, "moments": 179.93, "var": 181.09,
    "rstd": 211.91, "xn": 225.62, "turn_xn": 257.89, "take_xnt": 265.18, "round_xnt": 276.4, "rest_xnt": 282.05,
    "project": 289.52, "scores": 302.52, "scale": 312.08, "take_wh": 316.58, "take_score": 321.7, "top_score": 337.5,
    "project_hn": 342.98, "exponents": 345.61, "invert": 351.81, "divide": 354.81, "take_hn": 362.39, "turn_prob": 367.94,
    "take_prob_t": 375.52, "mix": 400.49, "take_mixed": 405.52, "rest_mixed": 409.27, "gate_r": 426.04, "tanh_r": 429.78,
    "reset": 434.42, "project_in": 441.24, "add_input": 468.89, "tanh_new": 470.11, "gate_z": 505.93, "tanh_z": 505.94,
    "take_gap": 505.94, "keep": 518.49, "end_cell": 518.5, "turn_cell": 529.24, "add_cell": 533.14, "stats1": 537.89,
    "halves1": 546.48, "moments1": 546.49, "var1": 546.5, "rstd1": 548.71, "xn1": 562.02, "turn_xn1": 595.87,
    "take_xnt1": 605.68, "logits": 609.06, "take_logit": 611.38, "round_xnt1": 634.33, "only_max": 634.53, "only_eq": 634.54,
    "only_key": 645.74, "only_index": 652.4, "only_hot": 653.51, "turn_hot": 656.84, "take_hot": 659.0, "rest_xnt1": 659.4,
    "unchosen": 661.46, "experts0": 688.38, "relu0": 693.5, "experts1": 713.18, "relu1": 747.88, "experts2": 767.94,
    "relu2": 797.56, "experts3": 797.57, "relu3": 797.58, "experts4": 825.05, "relu4": 830.52, "experts5": 853.9,
    "relu5": 858.62, "experts6": 896.27, "relu6": 903.35, "experts7": 906.92, "relu7": 912.88, "last_down": 926.94,
    "relu_out": 940.04, "turn_y": 941.33, "add_experts": 967.8, "store": 968.74,
}

assert max(A_TIMES["rstd"], B_TIMES["load"], B_TIMES["round_x"], C_TIMES["rstd"]) < 1000 / U


def ready(eng, sem, i, u):
    eng.wait_ge(sem, U * i + (u + 1 + U))


def freed(eng, sem, i, u):
    eng.wait_ge(sem, U * i + (u + 1))


def landed(eng, sem, i):
    eng.wait_ge(sem, 16 * i + 16)


def open_stages(block, S):
    sems = list(S.values())

    @block.sync
    def _(sp):
        for s in sems[0::4]:
            sp.sem_inc(s, U)

    @block.scalar
    def _(act):
        for s in sems[1::4]:
            act.sem_inc(s, U)

    @block.vector
    def _(dve):
        for s in sems[2::4]:
            dve.sem_inc(s, U)

    @block.tensor
    def _(pe):
        for s in sems[3::4]:
            pe.sem_inc(s, U)


@contextmanager
def phase_semaphores(nc, prefix, last=False):
    with ExitStack() as ctx:
        made = []

        def sem(name):
            made.append(ctx.enter_context(nc.semaphore(prefix + name)))
            return made[-1]

        yield sem
        if last:
            return
        numbers = sorted(s.num for s in made)
        starts = [n for n in numbers if n - 1 not in numbers]
        ends = [n + 1 for n in numbers if n + 1 not in numbers]
        with nc.Block() as block:
            @block.gpsimd
            def _(pool):
                for first, end in zip(starts, ends):
                    pool.sem_clear(range(first, end))


def stages(sem, names):
    return {name: sem(name) for name in names.split()}


def staggered(eng, stages):
    turns = sorted(((when + u / U) % 1, int(when + u / U), u, n) for n, (when, _) in enumerate(stages) for u in range(U))

    def body(i, laps):
        for _, lap, u, n in turns:
            if lap in laps:
                stages[n][1](i - 1 if lap else i, u)

    body(0, (0,))
    with eng.Fori(1, G // U) as i:
        body(i, (0, 1))
    body(G // U, (1,))


def normalising(nc, dve, src, T, S, n, arrived, at):
    def stats(i, u):
        arrived(i, u)
        for t in range(GT):
            last = nc.vector.bn_stats(T.stats[u][:, t, :], src[u][:, t, :])
        last.then_inc(S["stats" + n], 1)

    def halves(i, u):
        ready(dve, S["stats" + n], i, u)
        even, odd = T.stats[u][:, :, 0:3], T.stats[u][:, :, 3:6]
        nc.vector.tensor_tensor(T.half[u][:, 0], even[:, :, 1], odd[:, :, 1], ALU.add)
        nc.vector.tensor_tensor(T.half[u][:, 1], even[:, :, 1], odd[:, :, 1], ALU.subtract)
        nc.vector.tensor_tensor(T.half[u][:, 2], even[:, :, 2], odd[:, :, 2], ALU.add).then_inc(S["halves" + n], 1)

    def moments(i, u):
        ready(dve, S["halves" + n], i, u)
        nc.vector.tensor_scalar(T.mom[u][:, 0], T.half[u][:, 0], 0.5, None, ALU.mult)
        nc.vector.scalar_tensor_tensor(T.mom[u][:, 1], T.half[u][:, 1], 0.25, T.half[u][:, 1], ALU.mult, ALU.mult)
        nc.vector.tensor_scalar(T.mom[u][:, 2], T.half[u][:, 2], 1.0 / P, EPS, ALU.mult, ALU.add).then_inc(S["moments" + n], 1)

    def var(i, u):
        ready(dve, S["moments" + n], i, u)
        nc.vector.tensor_tensor(T.var[u][:], T.mom[u][:, 1], T.mom[u][:, 2], ALU.add).then_inc(S["var" + n], 1)

    def xn(i, u):
        ready(dve, S["rstd" + n], i, u)
        for t in range(GT):
            last = nc.vector.tensor_scalar(T.xn[u][:, t, :], src[u][:, t, :], T.mom[u][:, 0, t:t + 1], T.rstd[u][:, t:t + 1],
                                           ALU.subtract, ALU.mult)
        last.then_inc(S["xn" + n], 1)

    return [(at("stats" + n), stats), (at("halves" + n), halves), (at("moments" + n), moments), (at("var" + n), var), (at("xn" + n), xn)]


def power(nc, pool, T, K, S, n, stored=None):
    def rstd(i, u):
        if stored and (not isinstance(i, int) or i > 0):
            pool.wait_ge(stored[u], 16 * i)
        ready(pool, S["var" + n], i, u)
        nc.gpsimd.tensor_tensor(T.rstd[u][:], T.var[u][:], K.nhalf[:], ALU.pow).then_inc(S["rstd" + n], 1)

    return rstd


def one_hot(nc, dve, src, T, S, K, experts, k, came, n, at):
    def wide(a):
        return a.unsqueeze(2).to_broadcast([P, GT, experts])

    index_of = K.iota[:, 0:experts].unsqueeze(1).to_broadcast([P, GT, experts])

    def top(i, u):
        ready(dve, came, i, u)
        nc.vector.tensor_reduce(T.top[u][:, k], src[u][:], AXX, ALU.max).then_inc(S[n + "_max"], 1)

    def equal(i, u):
        ready(dve, S[n + "_max"], i, u)
        nc.vector.tensor_tensor(T.equal[u][:], src[u][:], wide(T.top[u][:, k]), ALU.is_equal).then_inc(S[n + "_eq"], 1)

    def key(i, u):
        ready(dve, S[n + "_eq"], i, u)
        nc.vector.scalar_tensor_tensor(T.key[u][:], T.equal[u][:], -float(experts), index_of, ALU.mult, ALU.add).then_inc(S[n + "_key"], 1)

    def index(i, u):
        ready(dve, S[n + "_key"], i, u)
        nc.vector.tensor_reduce(T.index[u][:, k], T.key[u][:], AXX, ALU.min).then_inc(S[n + "_index"], 1)

    def hot(i, u):
        ready(dve, S[n + "_index"], i, u)
        nc.vector.tensor_tensor(T.hot[u][:, k], T.key[u][:], wide(T.index[u][:, k]), ALU.is_equal).then_inc(S[n + "_hot"], 1)

    return [(at(n + "_max"), top), (at(n + "_eq"), equal), (at(n + "_key"), key), (at(n + "_index"), index), (at(n + "_hot"), hot)]


class Tiles:

    def __init__(self, sb, experts, picks):
        self.stats, self.half, self.mom = sb("stats", [P, GT, 6]), sb("half", [P, 3, GT]), sb("mom", [P, 3, GT])
        self.var, self.rstd, self.xn = sb("var", [P, GT]), sb("rstd", [P, GT]), sb("xn", [P, GT, P])
        self.equal, self.key = sb("equal", [P, GT, experts]), sb("key", [P, GT, experts])
        self.top, self.index = sb("top", [P, picks, GT]), sb("index", [P, picks, GT])
        self.hot = sb("hot", [P, picks, GT, experts])


def setup(nc, ctx, K, W):
    with phase_semaphores(nc, "setup_") as sem, ExitStack() as tmp:
        def sb(name, shape, dt=F32):
            return tmp.enter_context(nc.sbuf_tensor(name, shape, dt))

        a_col = sb("a_col", [P, 4])
        a_rep = sb("a_rep", [P, 4, P])
        w_t = sb("w_t", [P, 2, P])
        loaded, zeroed, ident_made, ident_cast = sem("loaded"), sem("zeroed"), sem("ident_made"), sem("ident_cast")
        wt_ps, wt_sb, rep_made, wa_ps, wa_sb = sem("wt_ps"), sem("wt_sb"), sem("rep_made"), sem("wa_ps"), sem("wa_sb")
        iota_made = sem("iota_made")
        ps = tmp.enter_context(nc.psum_tensor("setup_ps", [P, 2, 512], F32))
        ps2 = tmp.enter_context(nc.psum_tensor("setup_ps2", [P, 512], F32))
        block = tmp.enter_context(nc.Block())
        loads = [
            (K.w_att[:, 0, :], W["L0_gnn_W"]), (K.w_att[:, 1, :], W["L1_gnn_W"]),
            (a_col[:, 0:2], W["L0_gnn_a"]),
            (a_col[:, 2:4], W["L1_gnn_a"]),
            (K.w_r0[:], W["L0_ffn_Wr"]),
        ]

        @block.sync
        def _(sp):
            for dst, src in loads:
                sp.dma_start(dst, src).then_inc(loaded, 16)

        @block.gpsimd
        def _(pool):
            nc.gpsimd.memset(K.ident[:], 0.0).then_inc(zeroed, 1)
            nc.gpsimd.memset(K.nhalf[:], -0.5)
            nc.gpsimd.iota(K.iota_i[:], [[1, E1]], base=0, channel_multiplier=0).then_inc(iota_made, 1)
            pool.wait_ge(zeroed, 1)
            nc.gpsimd.affine_select(out=K.ident[:], in_=K.ident[:], compare_op=ALU.not_equal, fill=1.0, base=0,
                                    pattern=[[-1, P]], channel_multiplier=1).then_inc(ident_made, 1)

        @block.tensor
        def _(pe):
            pe.wait_ge(ident_made, 1)
            pe.wait_ge(loaded, 16 * len(loads))
            for l in range(2):
                last = nc.tensor.transpose(ps[:, l, 0:P], K.w_att[:, l, :], K.ident[:])
            last.then_inc(wt_ps, 1)
            pe.wait_ge(wt_sb, 1)
            pe.wait_ge(rep_made, 1)
            for l in range(2):
                for k in range(2):
                    m = 2 * l + k
                    last = nc.tensor.matmul(ps2[:, m * P:(m + 1) * P], w_t[:, l, :], a_rep[:, m, :], start=True, stop=True)
            last.then_inc(wa_ps, 1)

        @block.vector
        def _(dve):
            dve.wait_ge(iota_made, 1)
            nc.vector.tensor_copy(K.iota[:], K.iota_i[:])
            dve.wait_ge(ident_made, 1)
            nc.vector.tensor_copy(K.ident_b[:], K.ident[:]).then_inc(ident_cast, 1)
            dve.wait_ge(loaded, 16 * len(loads))
            nc.vector.tensor_copy(a_rep[:], a_col[:].unsqueeze(2).to_broadcast([P, 4, P])).then_inc(rep_made, 1)
            dve.wait_ge(wt_ps, 1)
            nc.vector.tensor_copy(w_t[:], ps[:, :, 0:P]).then_inc(wt_sb, 1)
            dve.wait_ge(wa_ps, 1)
            nc.vector.tensor_copy(K.w_score[:], ps2[:].rearrange("p (m f) -> p m f", m=4)).then_inc(wa_sb, 1)


class Constants:
    def __init__(self, ctx, nc):
        def sb(name, shape, dt=F32):
            return ctx.enter_context(nc.sbuf_tensor(name, shape, dt))

        self.ident = sb("ident", [P, P])
        self.ident_b = sb("ident_b", [P, P], BF16)
        self.nhalf = sb("nhalf", [P, GT])
        self.iota_i = sb("iota_i", [P, E1], I32)
        self.iota = sb("iota", [P, E1])
        self.w_att = sb("w_att", [P, 2, P])
        self.w_score = sb("w_score", [P, 4, P])
        self.w_r0 = sb("w_r0", [P, E0])


def phase_a(nc, K, X, XNT, R, x, adj):
    with phase_semaphores(nc, "a_") as sem, ExitStack() as ctx:
        def sb(name, shape, dt=F32):
            return [ctx.enter_context(nc.sbuf_tensor(f"a_{name}{u}", shape, dt)) for u in range(U)]

        def bank(name):
            return [ctx.enter_context(nc.psum_tensor(f"a_{name}{u}", [P, 512], F32)) for u in range(U)]

        adj_sb = sb("adj", [P, GT, P], I32)
        closed = sb("closed", [P, TOK], BF16)
        x_new, x1 = sb("x_new", [P, GT, P]), sb("x1", [P, GT, P])
        T = Tiles(sb, E0, K0)
        xnt = sb("xnt", [P, TOK])
        wh, scaled, score = sb("wh", [P, GT, P]), sb("scaled", [P, TOK]), sb("score", [P, GT, P])
        neg_max, sums, inv = sb("neg_max", [P, GT]), sb("sums", [P, GT]), sb("inv", [P, GT])
        prob, prob_t, gain = sb("prob", [P, GT, P]), sb("prob_t", [P, GT, P]), sb("gain", [P, GT, P])
        logit, rest = sb("logit", [P, GT, E0]), sb("rest", [P, GT, E0])
        gap, ratio, den = sb("gap", [P, GT]), sb("ratio", [P, GT]), sb("den", [P, GT])
        weight = sb("weight", [P, K0, GT])
        ps_a, ps_b = bank("ps_a"), bank("ps_b")
        no_rows = ctx.enter_context(nc.sbuf_tensor("a_no_rows", [P, NP * P // G], F32))
        zeroed = sem("zeroed")

        S = stages(sem, """
            closed stats halves moments var rstd xn xnt_ps xnt wh_ps score_ps wh scaled score neg_max prob inv
            prob_t_ps prob_t mixed gain x1 stats1 halves1 moments1 var1 rstd1 xn1 xnt1_ps xnt1 kept logit_ps logit
            first_max first_eq first_key first_index first_hot rest second_max second_eq second_key
            second_index second_hot gap ratio den w0 w1 hot_kept w_kept x_kept""")
        x_in = [sem(f"x_in{u}") for u in range(U)]
        adj_in = [sem(f"adj_in{u}") for u in range(U)]
        units = range(U)
        rows_out = [sem(f"rows_out{u}") for u in range(U)]
        cleared = R.sorted.rearrange("r f -> (r f)").rearrange("(n p q) -> p n q", n=G, p=P)
        xd = x.rearrange("b p f -> p b f")
        ad = adj.rearrange("b p f -> p b f")

        with nc.Block() as start:
            open_stages(start, S)

            @start.gpsimd
            def _(pool):
                nc.gpsimd.memset(no_rows[:], 0.0).then_inc(zeroed, 1)
                pool.wait_ge(zeroed, 1)

        block = ctx.enter_context(nc.Block())

        def at(stage):
            return A_TIMES[stage] / 1000

        def graphs(i, u):
            return bass.ds((U * i + u) * GT, GT)

        @block.sync
        def _(sp):
            def load(i, u):
                freed(sp, S["x1"], i, u)
                sp.dma_start(x_new[u][:], xd[:, graphs(i, u), :]).then_inc(x_in[u], 16)
                freed(sp, S["closed"], i, u)
                sp.dma_start(adj_sb[u][:], ad[:, graphs(i, u), :]).then_inc(adj_in[u], 16)

            def clear(i, u):
                sp.dma_start(cleared[:, bass.ds(U * i + u, 1), :].rearrange("p o q -> p (o q)"), no_rows[:]).then_inc(R.cleared, 16)

            def store(i, u):
                ready(sp, S["xn1"], i, u)
                sp.dma_start(R.rows[:, graphs(i, u), :], T.xn[u][:]).then_inc(rows_out[u], 16)

            staggered(sp, [(at("load"), load), (at("clear"), clear), (at("store"), store)])
            for u in units:
                sp.wait_ge(rows_out[u], 16 * (G // U))
            sp.wait_ge(R.cleared, 16 * G)

        @block.gpsimd
        def _(pool):
            def keep_x(i, u):
                ready(pool, S["x1"], i, u)
                nc.gpsimd.tensor_copy(X[:, graphs(i, u), :], x1[u][:]).then_inc(S["x_kept"], 1)

            def keep_xnt(i, u):
                ready(pool, S["xnt1"], i, u)
                nc.gpsimd.tensor_copy(XNT[:, bass.ds((U * i + u) * TOK, TOK)], xnt[u][:]).then_inc(S["kept"], 1)

            staggered(pool, [(at("rstd"), power(nc, pool, T, K, S, "", rows_out)), (at("rstd1"), power(nc, pool, T, K, S, "1")),
                             (at("keep_x"), keep_x), (at("keep_xnt"), keep_xnt)])

        @block.vector
        def _(dve):
            def close(i, u):
                landed(dve, adj_in[u], i)
                freed(dve, S["score_ps"], i, u)
                nc.vector.tensor_scalar(closed[u][:], adj_sb[u][:].rearrange("p t f -> p (t f)"), 0.0, -BIG,
                                        ALU.is_le, ALU.mult).then_inc(S["closed"], 1)

            def take_score(i, u):
                ready(dve, S["scaled"], i, u)
                freed(dve, S["prob"], i, u)
                nc.vector.tensor_tensor(score[u][:].rearrange("p t f -> p (t f)"), scaled[u][:], ps_b[u][:],
                                        ALU.max).then_inc(S["score"], 1)

            def top_score(i, u):
                ready(dve, S["score"], i, u)
                nc.vector.tensor_reduce(neg_max[u][:], score[u][:], AXX, ALU.max, negate=True).then_inc(S["neg_max"], 1)

            def invert(i, u):
                ready(dve, S["prob"], i, u)
                nc.vector.reciprocal(inv[u][:], sums[u][:]).then_inc(S["inv"], 1)

            def add_gain(i, u):
                ready(dve, S["gain"], i, u)
                freed(dve, S["x_kept"], i, u)
                nc.vector.tensor_tensor(x1[u][:], x_new[u][:], gain[u][:], ALU.add).then_inc(S["x1"], 1)

            def take_logit(i, u):
                ready(dve, S["logit_ps"], i, u)
                nc.vector.tensor_copy(logit[u][:].rearrange("p t e -> p (t e)"), ps_b[u][:, 0:GT * E0]).then_inc(S["logit"], 1)

            def others(i, u):
                ready(dve, S["first_hot"], i, u)
                nc.vector.scalar_tensor_tensor(rest[u][:], T.hot[u][:, 0], -BIG, logit[u][:], ALU.mult, ALU.add).then_inc(S["rest"], 1)

            def take_gap(i, u):
                ready(dve, S["second_max"], i, u)
                nc.vector.tensor_tensor(gap[u][:], T.top[u][:, 1], T.top[u][:, 0], ALU.subtract).then_inc(S["gap"], 1)

            def denominator(i, u):
                ready(dve, S["ratio"], i, u)
                nc.vector.tensor_scalar(den[u][:], ratio[u][:], 1.0, None, ALU.add).then_inc(S["den"], 1)

            def first_weight(i, u):
                ready(dve, S["den"], i, u)
                nc.vector.reciprocal(weight[u][:, 0], den[u][:]).then_inc(S["w0"], 1)

            def second_weight(i, u):
                ready(dve, S["w0"], i, u)
                nc.vector.tensor_tensor(weight[u][:, 1], weight[u][:, 0], ratio[u][:], ALU.mult).then_inc(S["w1"], 1)

            def keep_picks(i, u):
                ready(dve, S["second_hot"], i, u)
                for k in range(K0):
                    last = nc.vector.tensor_copy(R.hot[k][:, graphs(i, u), :], T.hot[u][:, k])
                last.then_inc(S["hot_kept"], 1)
                ready(dve, S["w1"], i, u)
                for k in range(K0):
                    last = nc.vector.tensor_copy(R.weight[:, graphs(i, u), k], weight[u][:, k])
                last.then_inc(S["w_kept"], 1)

            staggered(dve, [
                *normalising(nc, dve, x_new, T, S, "", lambda i, u: landed(dve, x_in[u], i), at), (at("close"), close),
                (at("take_score"), take_score), (at("top_score"), top_score), (at("invert"), invert), (at("add_gain"), add_gain),
                *normalising(nc, dve, x1, T, S, "1", lambda i, u: ready(dve, S["x1"], i, u), at),
                (at("take_logit"), take_logit), *one_hot(nc, dve, logit, T, S, K, E0, 0, S["logit"], "first", at),
                (at("others"), others), *one_hot(nc, dve, rest, T, S, K, E0, 1, S["rest"], "second", at),
                (at("take_gap"), take_gap), (at("denominator"), denominator), (at("first_weight"), first_weight), (at("second_weight"), second_weight),
                (at("keep_picks"), keep_picks)])

        @block.scalar
        def _(act):
            def take_xnt(i, u):
                ready(act, S["xnt_ps"], i, u)
                freed(act, S["kept"], i, u)
                nc.scalar.copy(xnt[u][:], ps_a[u][:]).then_inc(S["xnt"], 1)

            def take_wh(i, u):
                ready(act, S["wh_ps"], i, u)
                nc.scalar.copy(wh[u][:].rearrange("p t f -> p (t f)"), ps_a[u][:]).then_inc(S["wh"], 1)

            def scale(i, u):
                ready(act, S["score_ps"], i, u)
                nc.scalar.mul(scaled[u][:], ps_b[u][:], SLOPE).then_inc(S["scaled"], 1)

            def exponents(i, u):
                ready(act, S["neg_max"], i, u)
                freed(act, S["prob_t_ps"], i, u)
                for t in range(GT):
                    last = nc.scalar.activation(prob[u][:, t, :], score[u][:, t, :], ACT.Exp, bias=neg_max[u][:, t:t + 1],
                                                accum_out=sums[u][:, t:t + 1])
                last.then_inc(S["prob"], 1)

            def take_prob_t(i, u):
                ready(act, S["prob_t_ps"], i, u)
                nc.scalar.copy(prob_t[u][:].rearrange("p t f -> p (t f)"), ps_a[u][:]).then_inc(S["prob_t"], 1)

            def take_gain(i, u):
                ready(act, S["inv"], i, u)
                ready(act, S["mixed"], i, u)
                for t in range(GT):
                    last = nc.scalar.activation(gain[u][:, t, :], ps_b[u][:, t * P:(t + 1) * P], ACT.Relu, scale=inv[u][:, t:t + 1])
                last.then_inc(S["gain"], 1)

            def take_xnt1(i, u):
                ready(act, S["xnt1_ps"], i, u)
                nc.scalar.copy(xnt[u][:], ps_a[u][:]).then_inc(S["xnt1"], 1)

            def take_ratio(i, u):
                ready(act, S["gap"], i, u)
                nc.scalar.activation(ratio[u][:], gap[u][:], ACT.Exp).then_inc(S["ratio"], 1)

            staggered(act, [(at("take_gain"), take_gain), (at("take_xnt"), take_xnt), (at("take_wh"), take_wh), (at("scale"), scale), (at("exponents"), exponents), (at("take_prob_t"), take_prob_t),
                            (at("take_xnt1"), take_xnt1), (at("take_ratio"), take_ratio)])

        @block.tensor
        def _(pe):
            def turn_xn(i, u):
                ready(pe, S["xn"], i, u)
                freed(pe, S["xnt1"], i, u)
                for t in range(GT):
                    last = nc.tensor.transpose(ps_a[u][:, t * P:(t + 1) * P], T.xn[u][:, t, :], K.ident[:])
                last.then_inc(S["xnt_ps"], 1)

            def project(i, u):
                ready(pe, S["xnt"], i, u)
                for t in range(GT):
                    last = nc.tensor.matmul(ps_a[u][:, t * P:(t + 1) * P], xnt[u][:, t * P:(t + 1) * P], K.w_att[:, 0, :],
                                            start=True, stop=True)
                last.then_inc(S["wh_ps"], 1)

            def scores(i, u):
                ready(pe, S["xnt"], i, u)
                freed(pe, S["logit"], i, u)
                ready(pe, S["closed"], i, u)
                nc.tensor.matmul(ps_b[u][:], K.w_score[:, 1, :], xnt[u][:], start=True, stop=False)
                for t in range(GT):
                    nc.tensor.matmul(ps_b[u][:, t * P:(t + 1) * P], xnt[u][:, t * P:(t + 1) * P], K.w_score[:, 0, :],
                                     start=False, stop=False, skip_group_check=True)
                nc.tensor.matmul(ps_b[u][:], K.ident_b[:], closed[u][:], start=False, stop=True).then_inc(S["score_ps"], 1)

            def turn_prob(i, u):
                ready(pe, S["prob"], i, u)
                ready(pe, S["wh"], i, u)
                for t in range(GT):
                    last = nc.tensor.transpose(ps_a[u][:, t * P:(t + 1) * P], prob[u][:, t, :], K.ident[:])
                last.then_inc(S["prob_t_ps"], 1)

            def mix(i, u):
                ready(pe, S["prob_t"], i, u)
                for t in range(GT):
                    last = nc.tensor.matmul(ps_b[u][:, t * P:(t + 1) * P], prob_t[u][:, t, :], wh[u][:, t, :],
                                            start=True, stop=True)
                last.then_inc(S["mixed"], 1)

            def turn_xn1(i, u):
                ready(pe, S["xn1"], i, u)
                for t in range(GT):
                    last = nc.tensor.transpose(ps_a[u][:, t * P:(t + 1) * P], T.xn[u][:, t, :], K.ident[:])
                last.then_inc(S["xnt1_ps"], 1)

            def logits(i, u):
                ready(pe, S["xnt1"], i, u)
                for t in range(GT):
                    last = nc.tensor.matmul(ps_b[u][:, t * E0:(t + 1) * E0], xnt[u][:, t * P:(t + 1) * P], K.w_r0[:],
                                            start=True, stop=True)
                last.then_inc(S["logit_ps"], 1)

            staggered(pe, [(at("turn_xn"), turn_xn), (at("project"), project), (at("scores"), scores), (at("turn_prob"), turn_prob), (at("mix"), mix),
                           (at("turn_xn1"), turn_xn1), (at("logits"), logits)])


class Routing:

    def __init__(self, ctx, nc):
        def sb(name, shape, dt=F32):
            return ctx.enter_context(nc.sbuf_tensor(name, shape, dt))

        self.weight = sb("pick_weight", [P, B, K0])
        self.slot = sb("slot", [P, B, K0], U32)
        self.expert = sb("tile_experts", [1, NI], U32)
        self.cleared = ctx.enter_context(nc.semaphore("rows_cleared"))
        self.b_moved = ctx.enter_context(nc.semaphore("bias_moved"))
        self.scattered = [ctx.enter_context(nc.semaphore(f"scattered{k}")) for k in range(2)]
        self.picked = [ctx.enter_context(nc.semaphore(f"picked{u}")) for u in range(U)]
        self.rows = nc.dram_tensor("rows", (P, B, P), F32, kind="Internal").ap()
        self.sorted = nc.dram_tensor("sorted_rows", (NP * P, P), F32, kind="Internal").ap()
        self.routed = nc.dram_tensor("routed_rows", (NP * P, P), F32, kind="Internal").ap()

    def hold_choices(self, ctx, nc):
        self.hot = [ctx.enter_context(nc.sbuf_tensor(f"hot_{k}", [P, B, E0], F32)) for k in range(K0)]


def sort_picks(nc, K, R, E, W):
    with phase_semaphores(nc, "s_") as sem, ExitStack() as ctx:
        def sb(name, shape, dt=F32):
            return ctx.enter_context(nc.sbuf_tensor("s_" + name, shape, dt))

        earlier_f, earlier, ones = sb("earlier_f", [P, P]), sb("earlier", [P, P], BF16), sb("ones", [P, P], BF16)
        hots = sb("hots", [P, B * E0], BF16)
        count, run = sb("count", [P, B, E0]), [sb(f"run{n}", [P, B, E0]) for n in range(2)]
        rounded, tiles_i, tiles = sb("rounded", [P, E0], I32), sb("tiles_i", [P, E0], I32), sb("tiles", [P, E0])
        ends = [sb(f"ends{n}", [P, E0]) for n in range(2)]
        first, before, row = sb("first", [P, E0]), sb("before", [P, B, E0]), sb("row", [P, B, E0])
        own, slot_f = sb("own", [P, B, E0]), sb("slot_f", [P, B, K0])
        tile_i, tile_f = sb("tile_i", [1, NP], I32), sb("tile_f", [1, NP])
        past, expert_f, expert = sb("past", [1, NP, E0]), sb("expert_f", [1, NP]), sb("expert", [1, UT + NP], U32)
        b_raw, b_low, b_ones = sb("b_raw", [2, E0 * (F0 + P)]), sb("b_low", [2, E0 * (F0 + P)], F32R), sb("b_ones", [2, P])
        b_loaded, b_high_made, b_low_made, ones_made = (sem(n) for n in ("b_loaded", "b_high", "b_low", "ones"))
        ps_rank = ctx.enter_context(nc.psum_tensor("s_ps_rank", [P, B, E0], F32))
        ps_count = ctx.enter_context(nc.psum_tensor("s_ps_count", [P, B, E0], F32))
        zeroed, masks_made, tile_made, hots_made, counted, step = (sem(n) for n in ("zeroed", "masks_made", "tile_made", "hots_made", "counted", "step"))
        block = ctx.enter_context(nc.Block())

        @block.gpsimd
        def _(pool):
            nc.gpsimd.iota(tile_i[:], [[1, NP]], base=0, channel_multiplier=0).then_inc(tile_made, 1)
            nc.gpsimd.memset(earlier_f[:], 1.0).then_inc(zeroed, 1)
            pool.wait_ge(zeroed, 1)
            nc.gpsimd.affine_select(out=earlier_f[:], in_=earlier_f[:], compare_op=ALU.is_gt, fill=0.0, base=0,
                                    pattern=[[1, P]], channel_multiplier=-1).then_inc(masks_made, 1)
            pool.wait_ge(b_high_made, 1)
            nc.gpsimd.tensor_tensor(b_low[:], b_raw[:], E.b[:].bitcast(F32), ALU.subtract).then_inc(b_low_made, 1)
            pool.wait_ge(b_low_made, 1)
            pool.dma_start(E.b[1:2], b_low[1:2]).then_inc(R.b_moved, 16)
            pool.wait_ge(R.b_moved, 16)

        @block.sync
        def _(sp):
            for r in range(2):
                sp.dma_start(b_raw[r:r + 1, 0:E0 * F0], W["L0_ffn_b1p"]).then_inc(b_loaded, 16)
                sp.dma_start(b_raw[r:r + 1, E0 * F0:], W["L0_ffn_b2p"]).then_inc(b_loaded, 16)

        @block.scalar
        def _(act):
            act.wait_ge(b_loaded, 64)
            nc.scalar.copy(E.b[:], b_raw[:]).then_inc(b_high_made, 1)
            act.wait_ge(ones_made, 1)
            nc.scalar.copy(E.ones[:], b_ones[:])

        @block.tensor
        def _(pe):
            pe.wait_ge(hots_made, 1)
            nc.tensor.matmul(ps_rank[:].rearrange("p b e -> p (b e)"), earlier[:], hots[:], start=True, stop=True)
            nc.tensor.matmul(ps_count[:].rearrange("p b e -> p (b e)"), ones[:], hots[:], start=True, stop=True).then_inc(counted, 1)

        @block.vector
        def _(dve):
            steps = [0]

            def then(ins):
                steps[0] += 1
                ins.then_inc(step, 1)
                dve.wait_ge(step, steps[0])

            def running(a, n, size):
                s = 1
                while s < size:
                    nc.vector.tensor_copy(a[1 - n][:, 0:s], a[n][:, 0:s])
                    then(nc.vector.tensor_tensor(a[1 - n][:, s:size], a[n][:, s:size], a[n][:, 0:size - s], ALU.add))
                    n, s = 1 - n, 2 * s
                return a[n]

            nc.vector.memset(b_ones[:], 1.0).then_inc(ones_made, 1)
            nc.vector.memset(ones[:], 1.0)
            nc.vector.memset(expert[:, 0:UT], 0)
            nc.vector.memset(R.expert[:], 0)
            dve.wait_ge(tile_made, 1)
            nc.vector.tensor_copy(tile_f[:], tile_i[:])
            dve.wait_ge(masks_made, 1)
            nc.vector.tensor_copy(earlier[:], earlier_f[:])
            nc.vector.tensor_tensor(hots[:].rearrange("p (b e) -> p b e", e=E0), R.hot[0][:], R.hot[1][:], ALU.add).then_inc(hots_made, 1)
            dve.wait_ge(counted, 1)
            nc.vector.tensor_copy(count[:], ps_count[:])
            then(nc.vector.tensor_copy(run[0][:], ps_count[:]))
            upto = running(run, 0, B)
            then(nc.vector.tensor_scalar(rounded[:], upto[:, B - 1, :], float(P - 1), None, ALU.add))
            then(nc.vector.tensor_scalar(tiles_i[:], rounded[:], 7, None, ALU.logical_shift_right))
            nc.vector.tensor_copy(tiles[:], tiles_i[:])
            then(nc.vector.tensor_copy(ends[0][:], tiles_i[:]))
            end = running(ends, 0, E0)
            nc.vector.tensor_tensor(past[:], tile_f[:].unsqueeze(2).to_broadcast([1, NP, E0]),
                                    end[0:1].unsqueeze(1).to_broadcast([1, NP, E0]), ALU.is_ge)
            nc.vector.tensor_tensor(before[:], upto[:], count[:], ALU.subtract)
            then(nc.vector.tensor_tensor(first[:], end[:], tiles[:], ALU.subtract))
            nc.vector.tensor_reduce(expert_f[:], past[:], AXX, ALU.add)
            then(nc.vector.scalar_tensor_tensor(before[:], first[:].unsqueeze(1).to_broadcast([P, B, E0]), float(P), before[:],
                                                ALU.mult, ALU.add))
            nc.vector.tensor_scalar(expert[:, UT:], expert_f[:], float(E0 - 1), None, ALU.min)
            then(nc.vector.tensor_tensor(row[:], before[:], ps_rank[:], ALU.add))
            for k in range(UT + LAG):
                tiles_k = expert[:, UT - LAG + k:UT - LAG + k + UT * (NI - 1) + 1:UT]
                then(nc.vector.scalar_tensor_tensor(R.expert[:], tiles_k, E_BITS * k, R.expert[:], ALU.logical_shift_left,
                                                    ALU.bitwise_or))
            for k in range(K0):
                then(nc.vector.tensor_tensor(own[:], row[:], R.hot[k][:], ALU.mult))
                then(nc.vector.tensor_reduce(slot_f[:, :, k], own[:], AXX, ALU.add))
            nc.vector.tensor_copy(R.slot[:], slot_f[:])


class Experts:

    def __init__(self, ctx, nc):
        self.b = ctx.enter_context(nc.sbuf_tensor("e_b", [2, E0 * (F0 + P)], F32R))
        self.b1 = self.b[:, 0:E0 * F0].rearrange("o (e f) -> o e f", e=E0)
        self.b2 = self.b[:, E0 * F0:].rearrange("o (e f) -> o e f", e=E0)
        self.ones = ctx.enter_context(nc.sbuf_tensor("e_ones", [2, P], F32R))

    def hold_weights(self, ctx, nc):
        self.w = ctx.enter_context(nc.sbuf_tensor("e_w", [P, 2, 2 * E0, F0], F32R))


def shared_expert(nc, K, X, XNT, R, E, W):
    with phase_semaphores(nc, "b_") as sem, ExitStack() as ctx:
        def one(name, shape, dt=F32):
            return ctx.enter_context(nc.sbuf_tensor("b_" + name, shape, dt))

        def sb(name, shape, n=U, dt=F32):
            return [one(f"{name}{u}", shape, dt) for u in range(n)] * (U // n)

        units = range(U)
        w1, w2 = [one(f"w1_{h}", [P, F0], F32R) for h in "hl"], [one(f"w2_{h}", [P, FC, P], F32R) for h in "hl"]
        b1, b2, gate = one("b1", [P, FC]), one("b2", [P, 1]), one("gate", [P, 1])
        raw, rows, slots = sb("raw", [P, F0], 2), sb("rows", [P, GT, P], 2), sb("slots", [P, GT * K0], 2)
        x_h, x_l = sb("x_h", [P, TOK], 2, F32R), sb("x_l", [P, TOK], 2, F32R)
        hidden = sb("hidden", [P, TOK])
        h_h, h_l = sb("h_h", [P, TOK], U, F32R), sb("h_l", [P, TOK], U, F32R)
        ps_h, ps_y = ([ctx.enter_context(nc.psum_tensor(f"b_{n}{u}", [P, 512], F32)) for u in units] for n in ("ps_h", "ps_y"))

        w_loaded, w_high, gated = sem("w_loaded"), sem("w_high"), sem("gated")
        S = stages(sem, "x_high x_low y_out out_ps x_done raw_high raw_low")
        h_ps, h_act, h_high, h_low, h_used = ([sem(f"{n}{u}") for u in units] for n in ("h_ps", "h_act", "h_high", "h_low", "h_used"))
        raw_in, rows_in, slots_in = ([sem(f"{n}{k}") for k in range(2)] for n in ("raw_in", "rows_in", "slots_in"))
        SCATTERS = 16 * GT * K0
        w1_raw, w2_raw = raw[0], raw[1][:].rearrange("p (c d) -> p c d", c=FC)
        with nc.Block() as start:
            @start.sync
            def _(sp):
                sp.dma_start(w1_raw[:], W["L0_ffn_W1s"]).then_inc(w_loaded, 16)
                sp.dma_start(w2_raw, W["L0_ffn_W2s"].rearrange("(c f) d -> f c d", c=FC)).then_inc(w_loaded, 16)
                sp.dma_start(b1[:], W["L0_ffn_b1s"]).then_inc(w_loaded, 16)
                sp.dma_start(b2[:], W["L0_ffn_b2s"]).then_inc(w_loaded, 16)

            @start.vector
            def _(dve):
                dve.wait_ge(w_loaded, 64)
                nc.vector.tensor_copy(w1[0][:], w1_raw[:])
                nc.vector.tensor_copy(w2[0][:], w2_raw).then_inc(w_high, 1)
                dve.wait_ge(w_high, 1)
                nc.vector.tensor_tensor(w1[1][:], w1_raw[:], w1[0][:].bitcast(F32), ALU.subtract)
                nc.vector.tensor_tensor(w2[1][:], w2_raw, w2[0][:].bitcast(F32), ALU.subtract)

            @start.gpsimd
            def _(pool):
                for s in S.values():
                    pool.sem_inc(s, U)
                pool.sem_inc(gated, 1)

        def at(stage):
            return B_TIMES[stage] / 1000

        def group(i, u):
            return U * i + u

        def loads_before(i, u):
            return (U // 2) * i + u // 2

        def exist(i, u):
            return not isinstance(i, int) or i > 0 or u >= 2

        def tokens(i, u):
            return XNT[:, bass.ds(group(i, u) * TOK, TOK)]

        def graphs(i, u):
            return bass.ds(group(i, u) * GT, GT)

        def weight(part, i, u):
            return E.w[:, part, bass.ds(group(i, u), 1), :].rearrange("p o f -> p (o f)")

        def chunk(eng, s, i, u, c):
            eng.wait_ge(s[u], FC * i + (c + 1))

        block = ctx.enter_context(nc.Block())

        @block.sync
        def _(sp):
            def load(i, u):
                if exist(i, u):
                    sp.wait_ge(R.scattered[u % 2], SCATTERS * loads_before(i, u))
                sp.dma_start(rows[u][:], R.rows[:, graphs(i, u), :]).then_inc(rows_in[u % 2], 16)
                sp.dma_start(slots[u][:], R.slot[:, graphs(i, u), :].bitcast(F32).rearrange("p t k -> p (t k)")).then_inc(slots_in[u % 2], 16)
                sp.wait_ge(S["raw_low"], group(i, u) - 1 + U)
                sp.dma_start(raw[u][:], W["L0_ffn_Wp"][:, bass.ds(group(i, u), 1), :].rearrange("p o f -> p (o f)")).then_inc(raw_in[u % 2], 16)

            staggered(sp, [(at("load"), load)])
            for k in range(2):
                sp.wait_ge(R.scattered[k], SCATTERS * (G // 2))

        @block.gpsimd
        def _(pool):
            def scatter(i, u):
                pool.wait_ge(rows_in[u % 2], 16 * loads_before(i, u) + 16)
                pool.wait_ge(slots_in[u % 2], 16 * loads_before(i, u) + 16)
                pool.wait_ge(gated, group(i, u) + 1)
                nc.gpsimd.tensor_tensor(gate[:], K.nhalf[:, 0:1], K.nhalf[:, 0:1], ALU.add).then_inc(gated, 1)
                for t in range(GT):
                    for k in range(K0):
                        n = K0 * t + k
                        pool.indirect_dma_start(R.sorted, bass.IndirectOffsetOnAxis(ap=slots[u][:, n:n + 1].bitcast(U32), axis=0),
                                                rows[u][:, t, :], None).then_inc(R.scattered[u % 2], 16)

            staggered(pool, [(at("scatter"), scatter)])

        @block.tensor
        def _(pe):
            def product(dst, a, b, c, first=True, last=True):
                nc.tensor.matmul(dst, a[0], b[0], start=first, stop=False)
                nc.tensor.matmul(dst, a[0], b[1], start=False, stop=False)
                return nc.tensor.matmul(dst, a[1], b[0], start=False, stop=last)

            def up(c):
                def step(i, u):
                    if c == 0:
                        ready(pe, S["x_low"], i, u)
                        freed(pe, S["x_done"], i, u)
                    else:
                        chunk(pe, h_act, i, u, c - 1)
                    product(ps_h[u][:], [w[:, c * P:(c + 1) * P] for w in w1], (x_h[u][:], x_l[u][:]), c).then_inc(h_ps[u], 1)

                return step

            def down(c):
                def step(i, u):
                    if c == 0:
                        freed(pe, S["y_out"], i, u)
                    chunk(pe, h_low, i, u, c)
                    product(ps_y[u][:], [w[:, c, :] for w in w2], (h_h[u][:], h_l[u][:]), c, c == 0, c == FC - 1).then_inc(h_used[u], 1)

                return step

            def turn_y(i, u):
                ready(pe, S["y_out"], i, u)
                for t in range(GT):
                    last = nc.tensor.transpose(ps_h[u][:, t * P:(t + 1) * P], hidden[u][:, t * P:(t + 1) * P], K.ident[:])
                last.then_inc(S["out_ps"], 1)

            staggered(pe, [*((at(f"up{c}"), up(c)) for c in range(FC)), *((at(f"down{c}"), down(c)) for c in range(FC)),
                           (at("turn_y"), turn_y)])

        @block.scalar
        def _(act):
            def round_x(i, u):
                if exist(i, u):
                    act.wait_ge(h_ps[(u + 2) % U], FC * (i + u // 2))
                nc.scalar.copy(x_h[u][:], tokens(i, u)).then_inc(S["x_high"], 1)

            def gelu(c):
                def step(i, u):
                    chunk(act, h_ps, i, u, c)
                    if c == 0:
                        freed(act, S["out_ps"], i, u)
                    else:
                        chunk(act, h_low, i, u, c - 1)
                    nc.scalar.activation(hidden[u][:], ps_h[u][:], ACT.Gelu, bias=b1[:, c:c + 1]).then_inc(h_act[u], 1)

                return step

            def take_y(i, u):
                chunk(act, h_used, i, u, FC - 1)
                nc.scalar.activation(hidden[u][:], ps_y[u][:], ACT.Identity, bias=b2[:]).then_inc(S["y_out"], 1)

            def round_weight(i, u):
                act.wait_ge(raw_in[u % 2], 16 * loads_before(i, u) + 16)
                nc.scalar.copy(weight(0, i, u), raw[u][:]).then_inc(S["raw_high"], 1)

            staggered(act, [(at("round_x"), round_x), *((at(f"gelu{c}"), gelu(c)) for c in range(FC)), (at("take_y"), take_y),
                            (at("round_weight"), round_weight)])

        @block.vector
        def _(dve):
            def rest_x(i, u):
                ready(dve, S["x_high"], i, u)
                nc.vector.tensor_tensor(x_l[u][:], tokens(i, u), x_h[u][:].bitcast(F32), ALU.subtract).then_inc(S["x_low"], 1)

            def high(c):
                def step(i, u):
                    chunk(dve, h_act, i, u, c)
                    if c > 0:
                        chunk(dve, h_used, i, u, c - 1)
                    nc.vector.tensor_copy(h_h[u][:], hidden[u][:]).then_inc(h_high[u], 1)

                return step

            def low(c):
                def step(i, u):
                    chunk(dve, h_high, i, u, c)
                    nc.vector.tensor_tensor(h_l[u][:], hidden[u][:], h_h[u][:].bitcast(F32), ALU.subtract).then_inc(h_low[u], 1)

                return step

            def rest_weight(i, u):
                ready(dve, S["raw_high"], i, u)
                nc.vector.tensor_tensor(weight(1, i, u), raw[u][:], weight(0, i, u).bitcast(F32), ALU.subtract).then_inc(S["raw_low"], 1)

            def add_y(i, u):
                ready(dve, S["out_ps"], i, u)
                nc.vector.tensor_tensor(X[:, graphs(i, u), :], X[:, graphs(i, u), :], ps_h[u][:].rearrange("p (t f) -> p t f", t=GT),
                                        ALU.add).then_inc(S["x_done"], 1)

            staggered(dve, [(at("rest_x"), rest_x), *((at(f"high{c}"), high(c)) for c in range(FC)),
                            *((at(f"low{c}"), low(c)) for c in range(FC)), (at("rest_weight"), rest_weight), (at("add_y"), add_y)])


def routed_experts(nc, K, R, E):
    with phase_semaphores(nc, "r_") as sem, ExitStack() as ctx:
        def sb(name, shape, dt=F32, n=2):
            return [ctx.enter_context(nc.sbuf_tensor(f"r_{name}{k}", shape, dt)) for k in range(n)]

        def bank(name, n=2):
            return [ctx.enter_context(nc.psum_tensor(f"r_{name}{k}", [P, 512], F32)) for k in range(n)]

        rows = sb("rows", [P, P], n=UT)
        x_h, x_l = sb("x_h", [P, P], F32R), sb("x_l", [P, P], F32R)
        hidden = sb("hidden", [P, F0])
        h_h, h_l = sb("h_h", [P, F0], F32R), sb("h_l", [P, F0], F32R)
        y = sb("y", [P, P], n=UT)
        ps_x, ps_h, ps_t, ps_y = bank("ps_x"), bank("ps_h"), bank("ps_t"), bank("ps_y")
        x_ps, x_high, x_low, h_ps, h_act, t_ps, h_high, h_low, y_ps, y_sb = (
            sem(n) for n in ("x_ps", "x_high", "x_low", "h_ps", "h_act", "t_ps", "h_high", "h_low", "y_ps", "y_sb"))
        rows_in, y_stored = [sem(f"rows_in{k}") for k in range(UT)], [sem(f"y_stored{k}") for k in range(UT)]

        def after(eng, s, i, j, back=0):
            if not (isinstance(i, int) and UT * i + j - back < 0):
                eng.wait_ge(s, UT * i + (j - back + 1))

        block = ctx.enter_context(nc.Block())

        @block.sync
        def _(sp):
            def load(i, j):
                if not isinstance(i, int) or i > 0:
                    after(sp, x_ps, i, j, UT)
                sp.dma_start(rows[j][:], R.sorted.rearrange("(n p) f -> p n f", p=P)[:, bass.ds(UT * i + j, 1), :]
                             .rearrange("p o f -> p (o f)")).then_inc(rows_in[j], 16)

            def store(i, j):
                after(sp, y_sb, i, j)
                sp.dma_start(R.routed.rearrange("(n p) f -> p n f", p=P)[:, bass.ds(UT * i + j, 1), :]
                             .rearrange("p o f -> p (o f)"), y[j][:]).then_inc(y_stored[j], 16)

            for j in range(UT):
                load(0, j)
            with sp.Fori(0, NI - 1) as i:
                for j in range(UT):
                    load(i + 1, j)
                    store(i, j)
            for j in range(UT):
                store(NI - 1, j)
            for j in range(UT):
                sp.wait_ge(y_stored[j], 16 * NI)

        def tile_before(i, j):
            return (i + j // UT if j // UT else i, j % UT)

        def exists(i, j):
            return not isinstance(i, int) or 0 <= i < NI

        @block.tensor
        def _(pe):
            def tile_experts(i):
                packed = pe.value_load(R.expert[:, bass.ds(i, 1)], min_val=0, max_val=2 ** (E_BITS * (UT + LAG)) - 1)
                return [(packed >> (E_BITS * k)) & (E0 - 1) for k in range(UT + LAG)]

            def turn_rows(i, j):
                pe.wait_ge(rows_in[j], 16 * i + 16)
                after(pe, x_low, i, j, 2)
                nc.tensor.transpose(ps_x[j % 2][:, 0:P], rows[j][:], K.ident[:]).then_inc(x_ps, 1)

            def up(i, j, e):
                after(pe, h_act, i, j, 2)
                nc.tensor.matmul(ps_h[j % 2][:], E.ones[:], E.b1[:, bass.ds(e, 1), :].rearrange("p o f -> p (o f)"), start=True, stop=False)
                after(pe, x_low, i, j)
                w = [E.w[:, part, bass.ds(e, 1), :].rearrange("p o f -> p (o f)") for part in range(2)]
                nc.tensor.matmul(ps_h[j % 2][:], x_h[j % 2][:], w[0], start=False, stop=False)
                nc.tensor.matmul(ps_h[j % 2][:], x_h[j % 2][:], w[1], start=False, stop=False)
                nc.tensor.matmul(ps_h[j % 2][:], x_l[j % 2][:], w[0], start=False, stop=True).then_inc(h_ps, 1)

            def turn_hidden(i, j):
                after(pe, h_act, i, j)
                after(pe, h_low, i, j, 2)
                for c in range(FC):
                    last = nc.tensor.transpose(ps_t[j % 2][:, c * P:(c + 1) * P], hidden[j % 2][:, c * P:(c + 1) * P], K.ident[:])
                last.then_inc(t_ps, 1)

            def down(i, j, e):
                after(pe, y_sb, i, j, 2)
                after(pe, h_low, i, j)
                for c in range(FC):
                    cols = slice(c * P, (c + 1) * P)
                    w = E.w[:, :, bass.ds(e + E0, 1), cols].rearrange("p h o f -> p h (o f)")
                    nc.tensor.matmul(ps_y[j % 2][:, 0:2 * P], h_h[j % 2][:, cols], w, start=(c == 0), stop=(c == FC - 1),
                                     skip_group_check=True)
                    last = nc.tensor.matmul(ps_y[j % 2][:, 0:P], h_l[j % 2][:, cols], w[:, 0, :], start=False, stop=(c == FC - 1),
                                     skip_group_check=True)
                last = nc.tensor.matmul(ps_y[j % 2][:, 0:P], E.ones[:], E.b2[:, bass.ds(e, 1), :].rearrange("p o f -> p (o f)"),
                                        start=False, stop=True, skip_group_check=True)
                last.then_inc(y_ps, 1)

            def body(i):
                experts = tile_experts(i)
                for j in range(UT):
                    for stage, ahead in ((turn_rows, 1), (up, 0), (turn_hidden, -1), (down, -LAG)):
                        a, b = tile_before(i, j + ahead)
                        if exists(a, b):
                            stage(a, b, experts[j + ahead + LAG]) if stage in (up, down) else stage(a, b)

            turn_rows(0, 0)
            body(0)
            with pe.Fori(1, NI - 1) as i:
                body(i)
            body(NI - 1)
            turn_hidden(NI - 1, UT - 1)
            for j in range(UT - LAG, UT):
                down(NI - 1, j, tile_experts(NI - 1)[j + LAG])

        @block.scalar
        def _(act):
            def round_rows(i, j):
                after(act, x_ps, i, j)
                after(act, h_ps, i, j, 2)
                nc.scalar.copy(x_h[j % 2][:], ps_x[j % 2][:, 0:P]).then_inc(x_high, 1)

            def gelu(i, j):
                after(act, h_ps, i, j)
                after(act, t_ps, i, j, 2)
                nc.scalar.activation(hidden[j % 2][:], ps_h[j % 2][:], ACT.Gelu).then_inc(h_act, 1)

            def round_hidden(i, j):
                after(act, t_ps, i, j)
                after(act, y_ps, i, j, 2)
                nc.scalar.copy(h_h[j % 2][:], ps_t[j % 2][:]).then_inc(h_high, 1)

            def body(i):
                for j in range(UT):
                    for stage, ahead in ((round_rows, 1), (gelu, 0), (round_hidden, -1)):
                        a, b = tile_before(i, j + ahead)
                        if exists(a, b):
                            stage(a, b)

            round_rows(0, 0)
            body(0)
            with act.Fori(1, NI - 1) as i:
                body(i)
            body(NI - 1)
            round_hidden(NI - 1, UT - 1)

        @block.vector
        def _(dve):
            def rest_rows(i, j):
                after(dve, x_high, i, j)
                nc.vector.tensor_tensor(x_l[j % 2][:], ps_x[j % 2][:, 0:P], x_h[j % 2][:].bitcast(F32), ALU.subtract).then_inc(x_low, 1)

            def rest_hidden(i, j):
                after(dve, h_high, i, j)
                nc.vector.tensor_tensor(h_l[j % 2][:], ps_t[j % 2][:], h_h[j % 2][:].bitcast(F32), ALU.subtract).then_inc(h_low, 1)

            def take(i, j):
                after(dve, y_ps, i, j)
                if not isinstance(i, int) or i > 0:
                    dve.wait_ge(y_stored[j], 16 * i)
                nc.vector.tensor_reduce(y[j][:], ps_y[j % 2][:, 0:2 * P].rearrange("p (h f) -> p f h", h=2), AXX, ALU.add).then_inc(y_sb, 1)

            def body(i):
                for j in range(UT):
                    for stage, ahead in ((rest_rows, 1), (rest_hidden, -1), (take, -2)):
                        a, b = tile_before(i, j + ahead)
                        if exists(a, b):
                            stage(a, b)

            rest_rows(0, 0)
            body(0)
            with dve.Fori(1, NI - 1) as i:
                body(i)
            body(NI - 1)
            rest_hidden(NI - 1, UT - 1)
            take(NI - 1, UT - 2)
            take(NI - 1, UT - 1)


def phase_c(nc, K, X, R, W, adj, out):
    with phase_semaphores(nc, "c_", last=True) as sem, ExitStack() as ctx:
        def one(name, shape, dt=F32):
            return ctx.enter_context(nc.sbuf_tensor("c_" + name, shape, dt))

        def sb(name, shape, dt=F32):
            return [one(f"{name}{u}", shape, dt) for u in range(U)]

        def bank(name):
            return [ctx.enter_context(nc.psum_tensor(f"c_{name}{u}", [P, 512], F32)) for u in range(U)]

        w_r1 = one("w_r1", [P, E1])
        b_ih, b_hh, b_gate = one("b_ih", [P, 3]), one("b_hh", [P, 3]), one("b_gate", [P, 2])
        b_r1 = one("b_r1", [P, E1])
        b1 = one("b1", [P, C1])
        w2, b2 = one("w2", [P, C1, P]), one("b2", [E1, P])
        w_dst_p, w_ih_p, w_hh_p, w1_p, b2_p = ([one(f"{n}_{h}", shape, F32R) for h in "hl"] for n, shape in (
            ("w_dst", [P, P]), ("w_ih", [P, 3, P]), ("w_hh", [P, 3, P]), ("w1", [P, C1, P]), ("b2", [E1, P])))
        shut = one("shut", [E1, C1, P], BF16)
        T = Tiles(sb, E1, 1)
        adj_sb, closed = sb("adj", [P, GT, P], I32), sb("closed", [P, TOK], BF16)
        x2 = sb("x2", [P, GT, P])
        xnt, wh, scaled, score = sb("xnt", [P, TOK]), sb("wh", [P, GT, P]), sb("scaled", [P, TOK]), sb("score", [P, GT, P])
        neg_max, sums, inv = sb("neg_max", [P, GT]), sb("sums", [P, GT]), sb("inv", [P, GT])
        prob, new = sb("prob", [P, GT, P]), sb("new", [P, TOK])
        xnt_p = list(zip(sb("xnt_h", [P, TOK], F32R), sb("xnt_l", [P, TOK], F32R)))
        mixed_p = list(zip(sb("mixed_h", [P, TOK], F32R), sb("mixed_l", [P, TOK], F32R)))

        def wide(tiles):
            return [a[:].rearrange("p (t f) -> p t f", t=GT) for a in tiles]

        def flat_of(tiles):
            return [a[:].rearrange("p t f -> p (t f)") for a in tiles]

        prob_t, x4 = wide(scaled), wide(new)
        cell = flat_of(prob)
        gate_r, x3 = flat_of(score), score
        gate_z = hidden = flat_of(wh)
        logit, hot_t, hot_m = sb("logit", [P, GT, E1]), sb("hot_t", [E1, TOK], F32R), sb("hot_m", [E1, TOK], BF16)
        ps_a, ps_b = bank("ps_a"), bank("ps_b")
        units = range(U)

        slots, weight = sb("slots", [P, GT * K0]), sb("weight", [P, GT * K0])
        pick = sb("pick", [P, GT * K0, P])
        gate, gated = one("gate", [P, 1]), sem("gated")
        slots_in, weight_in = ([sem(f"{n}{u}") for u in units] for n in ("slots_in", "weight_in"))
        PICKS = 16 * GT * K0
        S = stages(sem, """
            x2_first x2
            closed stats halves moments var rstd xn xnt_ps xnt xnt_high xnt_low xnt_high1 xnt_low1 mixed_high wh_ps score_ps wh scaled score neg_max exp inv prob
            prob_t_ps prob_t mixed_ps mixed hn_ps r_ps z_ps in_ps gate_r gate_z hn reset pre new gap keep gru gru_ps x3
            stats1 halves1 moments1 var1 rstd1 xn1 xnt1_ps xnt1 logit_ps logit
            only_max only_eq only_key only_index only_hot hot_ps hot_t hot_m down y y_t_ps x4""")
        up_ps = [sem(f"up_ps{u}") for u in units]
        hidden_done = [[sem(f"hidden_{n}{u}") for u in units] for n in ("even", "odd")]
        x_in, adj_in, out_done = [sem(f"x_in{u}") for u in units], [sem(f"adj_in{u}") for u in units], [sem(f"out{u}") for u in units]

        w1, w_ih, w_hh = pick[U - 1], prob[U - 1][:, 0:3, :], prob[U - 2][:, 0:3, :]
        shut_f = pick[U - 2][0:E1].rearrange("k c f -> k (c f)")
        w_loaded, b_summed, shut_zero, shut_f32, w_ready, w_high = (sem(n) for n in ("w_loaded", "b_summed", "shut_zero", "shut_f32", "w_ready", "w_high"))
        loads = [(w_ih, W["L1_gnn_w_ih"]), (w_hh, W["L1_gnn_w_hh"]), (b_ih[:], W["L1_gnn_b_ih"]), (b_hh[:], W["L1_gnn_b_hh"]),
                 (w_r1[:], W["L1_ffn_router_w"]), (b_r1[:], W["L1_ffn_router_b"].to_broadcast([P, E1])),
                 (w1[:], W["L1_ffn_W1"]), (b1[:], W["L1_ffn_b1"]), (w2[:], W["L1_ffn_W2"]), (b2[:], W["L1_ffn_b2"])]
        b_sum = one("b_sum", [P, 2])
        with nc.Block() as start:
            open_stages(start, S)

            @start.gpsimd
            def _(pool):
                pool.sem_inc(gated, 1)

        ad = adj.rearrange("b p f -> p b f")
        od = out.rearrange("b p f -> p b f")
        block = ctx.enter_context(nc.Block())

        def at(stage):
            return C_TIMES[stage] / 1000

        def graphs(i, u):
            return bass.ds((U * i + u) * GT, GT)

        @block.sync
        def _(sp):
            def load(i, u):
                freed(sp, S["x2"], i, u)
                sp.dma_start(slots[u][:], R.slot[:, graphs(i, u), :].bitcast(F32).rearrange("p t k -> p (t k)")).then_inc(slots_in[u], 16)
                sp.dma_start(weight[u][:], R.weight[:, graphs(i, u), :].rearrange("p t k -> p (t k)")).then_inc(weight_in[u], 16)
                freed(sp, S["x3"], i, u)
                sp.dma_start(x2[u][:], X[:, graphs(i, u), :]).then_inc(x_in[u], 16)
                freed(sp, S["closed"], i, u)
                sp.dma_start(adj_sb[u][:], ad[:, graphs(i, u), :]).then_inc(adj_in[u], 16)

            def store(i, u):
                ready(sp, S["x4"], i, u)
                sp.dma_start(od[:, graphs(i, u), :], x4[u]).then_inc(out_done[u], 16)

            staggered(sp, [(at("load"), load), (at("store"), store)])
            for u in units:
                sp.wait_ge(out_done[u], 16 * (G // U))

        @block.gpsimd
        def _(pool):
            nc.gpsimd.memset(shut_f, 0.0).then_inc(shut_zero, 1)
            pool.wait_ge(shut_zero, 1)
            v = shut_f.rearrange("k (c e h) -> k c e h", c=C1, e=EC)
            nc.gpsimd.affine_select(out=v, in_=v, compare_op=ALU.not_equal, fill=BIG, base=0,
                                    pattern=[[-EC, C1], [-1, EC], [0, H1]], channel_multiplier=1).then_inc(shut_f32, 1)

            def open_gate(i, u):
                if isinstance(i, int) and i == 0 and u == U - 2:
                    pool.wait_ge(w_ready, 1)
                pool.wait_ge(slots_in[u], 16 * i + 16)
                freed(pool, S["x2"], i, u)
                pool.wait_ge(gated, U * i + (u + 1))
                nc.gpsimd.tensor_tensor(gate[:], K.nhalf[:, 0:1], K.nhalf[:, 0:1], ALU.add).then_inc(gated, 1)

            def gather(t):
                def rows(i, u):
                    if t == 0:
                        open_gate(i, u)
                    for n in range(K0 * t, K0 * t + K0):
                        pool.indirect_dma_start(pick[u][:, n, :], None, R.routed,
                                                bass.IndirectOffsetOnAxis(ap=slots[u][:, n:n + 1].bitcast(U32), axis=0)
                                                ).then_inc(R.picked[u], 16)

                return rows

            staggered(pool, [*((at(f"gather{t}"), gather(t)) for t in range(GT)),
                             (at("rstd"), power(nc, pool, T, K, S, "", out_done)), (at("rstd1"), power(nc, pool, T, K, S, "1"))])

        @block.vector
        def _(dve):
            dve.wait_ge(shut_f32, 1)
            nc.vector.tensor_copy(shut[:].rearrange("k c f -> k (c f)"), shut_f)
            dve.wait_ge(w_loaded, 16 * len(loads))
            nc.vector.tensor_tensor(b_sum[:], b_ih[:, 0:2], b_hh[:, 0:2], ALU.add).then_inc(b_summed, 1)
            split = ((w_dst_p, K.w_score[:, 3, :]), (w_ih_p, w_ih), (w_hh_p, w_hh), (w1_p, w1[:]), (b2_p, b2[:]))
            for parts, whole in split:
                last = nc.vector.tensor_copy(parts[0][:], whole)
            last.then_inc(w_high, 1)
            dve.wait_ge(b_summed, 1)
            nc.vector.tensor_scalar(b_gate[:], b_sum[:], 0.5, None, ALU.mult)
            dve.wait_ge(w_high, 1)
            for parts, whole in split:
                last = nc.vector.tensor_tensor(parts[1][:], whole, parts[0][:].bitcast(F32), ALU.subtract)
            last.then_inc(w_ready, 1)

            def add_picks(k):
                def add(i, u):
                    if k == 0:
                        landed(dve, x_in[u], i)
                        landed(dve, weight_in[u], i)
                        dve.wait_ge(R.picked[u], PICKS * (i + 1))
                    else:
                        ready(dve, S["x2_first"], i, u)
                    for t in range(GT):
                        n = K0 * t + k
                        last = nc.vector.scalar_tensor_tensor(x2[u][:, t, :], pick[u][:, n, :], weight[u][:, n:n + 1], x2[u][:, t, :],
                                                              ALU.mult, ALU.add)
                    last.then_inc(S["x2" if k else "x2_first"], 1)

                return add

            def close(i, u):
                landed(dve, adj_in[u], i)
                freed(dve, S["score_ps"], i, u)
                nc.vector.tensor_scalar(closed[u][:], adj_sb[u][:].rearrange("p t f -> p (t f)"), 0.0, -BIG,
                                        ALU.is_le, ALU.mult).then_inc(S["closed"], 1)

            def take_score(i, u):
                ready(dve, S["scaled"], i, u)
                nc.vector.tensor_tensor(score[u][:].rearrange("p t f -> p (t f)"), scaled[u][:], ps_b[u][:],
                                        ALU.max).then_inc(S["score"], 1)

            def top_score(i, u):
                ready(dve, S["score"], i, u)
                nc.vector.tensor_reduce(neg_max[u][:], score[u][:], AXX, ALU.max, negate=True).then_inc(S["neg_max"], 1)

            def invert(i, u):
                ready(dve, S["exp"], i, u)
                nc.vector.reciprocal(inv[u][:], sums[u][:]).then_inc(S["inv"], 1)

            def divide(i, u):
                ready(dve, S["inv"], i, u)
                for t in range(GT):
                    last = nc.vector.tensor_scalar(prob[u][:, t, :], prob[u][:, t, :], inv[u][:, t:t + 1], None, ALU.mult)
                last.then_inc(S["prob"], 1)

            def reset(i, u):
                ready(dve, S["gate_r"], i, u)
                ready(dve, S["hn"], i, u)
                nc.vector.scalar_tensor_tensor(gate_r[u], gate_r[u], 1.0, new[u][:], ALU.add, ALU.mult).then_inc(S["reset"], 1)

            def add_input(i, u):
                ready(dve, S["reset"], i, u)
                ready(dve, S["in_ps"], i, u)
                nc.vector.scalar_tensor_tensor(gate_r[u], gate_r[u], 0.5, ps_b[u][:], ALU.mult, ALU.add).then_inc(S["pre"], 1)

            def take_gap(i, u):
                ready(dve, S["new"], i, u)
                nc.vector.tensor_tensor(cell[u], xnt[u][:], new[u][:], ALU.subtract).then_inc(S["gap"], 1)

            def keep(i, u):
                ready(dve, S["gap"], i, u)
                ready(dve, S["gate_z"], i, u)
                nc.vector.scalar_tensor_tensor(cell[u], gate_z[u], 1.0, cell[u], ALU.add, ALU.mult).then_inc(S["keep"], 1)

            def end_cell(i, u):
                ready(dve, S["keep"], i, u)
                nc.vector.scalar_tensor_tensor(cell[u], cell[u], 0.5, new[u][:], ALU.mult, ALU.add).then_inc(S["gru"], 1)

            def add_cell(i, u):
                ready(dve, S["gru_ps"], i, u)
                nc.vector.tensor_tensor(x3[u][:].rearrange("p t f -> p (t f)"), x2[u][:].rearrange("p t f -> p (t f)"), ps_a[u][:],
                                        ALU.add).then_inc(S["x3"], 1)

            def take_logit(i, u):
                ready(dve, S["logit_ps"], i, u)
                nc.vector.tensor_tensor(logit[u][:], ps_a[u][:, 0:GT * E1].rearrange("p (t e) -> p t e", e=E1),
                                        b_r1[:].unsqueeze(1).to_broadcast([P, GT, E1]), ALU.add).then_inc(S["logit"], 1)

            def unchosen(i, u):
                ready(dve, S["hot_t"], i, u)
                nc.vector.tensor_scalar(hot_m[u][:], hot_t[u][:].bitcast(F32), -1.0, None, ALU.add).then_inc(S["hot_m"], 1)

            def relu(c):
                def odd(i, u):
                    dve.wait_ge(up_ps[u], C1 * i + (c + 1))
                    nc.vector.tensor_scalar(hidden[u], ps_b[u][:], b1[:, c:c + 1], 0.0, ALU.add, ALU.max).then_inc(hidden_done[1][u], 1)

                return odd

            def rest_xnt(n):
                def rest(i, u):
                    ready(dve, S["xnt_high" + n], i, u)
                    nc.vector.tensor_tensor(xnt_p[u][1][:], xnt[u][:], xnt_p[u][0][:].bitcast(F32), ALU.subtract).then_inc(S["xnt_low" + n], 1)

                return rest

            def rest_mixed(i, u):
                ready(dve, S["mixed_high"], i, u)
                nc.vector.tensor_tensor(mixed_p[u][1][:], ps_a[u][:], mixed_p[u][0][:].bitcast(F32), ALU.subtract).then_inc(S["mixed"], 1)

            def add_experts(i, u):
                ready(dve, S["y_t_ps"], i, u)
                nc.vector.tensor_tensor(new[u][:], x3[u][:].rearrange("p t f -> p (t f)"), ps_b[u][:],
                                        ALU.add).then_inc(S["x4"], 1)

            staggered(dve, [
                (at("close"), close), (at("add_picks0"), add_picks(0)), (at("add_picks1"), add_picks(1)),
                *normalising(nc, dve, x2, T, S, "", lambda i, u: ready(dve, S["x2"], i, u), at),
                (at("take_score"), take_score), (at("top_score"), top_score), (at("invert"), invert), (at("divide"), divide),
                (at("reset"), reset), (at("add_input"), add_input), (at("take_gap"), take_gap), (at("keep"), keep), (at("end_cell"), end_cell),
                (at("add_cell"), add_cell),
                *normalising(nc, dve, x3, T, S, "1", lambda i, u: ready(dve, S["x3"], i, u), at),
                (at("take_logit"), take_logit), *one_hot(nc, dve, logit, T, S, K, E1, 0, S["logit"], "only", at),
                (at("unchosen"), unchosen), *((at(f"relu{c}"), relu(c)) for c in range(1, C1, 2)), (at("add_experts"), add_experts),
                (at("rest_xnt"), rest_xnt("")), (at("rest_xnt1"), rest_xnt("1")), (at("rest_mixed"), rest_mixed)])

        @block.scalar
        def _(act):
            for dst, src in loads:
                act.dma_start(dst, src).then_inc(w_loaded, 16)
            act.wait_ge(w_ready, 1)

            def take_xnt(i, u):
                ready(act, S["xnt_ps"], i, u)
                nc.scalar.copy(xnt[u][:], ps_a[u][:]).then_inc(S["xnt"], 1)

            def round_xnt(n):
                def high(i, u):
                    ready(act, S["xnt" + n], i, u)
                    nc.scalar.copy(xnt_p[u][0][:], xnt[u][:]).then_inc(S["xnt_high" + n], 1)

                return high

            def take_wh(i, u):
                ready(act, S["wh_ps"], i, u)
                nc.scalar.copy(wh[u][:].rearrange("p t f -> p (t f)"), ps_a[u][:]).then_inc(S["wh"], 1)

            def scale(i, u):
                ready(act, S["score_ps"], i, u)
                nc.scalar.mul(scaled[u][:], ps_b[u][:], SLOPE).then_inc(S["scaled"], 1)

            def exponents(i, u):
                ready(act, S["neg_max"], i, u)
                for t in range(GT):
                    last = nc.scalar.activation(prob[u][:, t, :], score[u][:, t, :], ACT.Exp, bias=neg_max[u][:, t:t + 1],
                                                accum_out=sums[u][:, t:t + 1])
                last.then_inc(S["exp"], 1)

            def take_hn(i, u):
                ready(act, S["hn_ps"], i, u)
                nc.scalar.activation(new[u][:], ps_a[u][:], ACT.Identity, bias=b_hh[:, 2:3]).then_inc(S["hn"], 1)

            def take_prob_t(i, u):
                ready(act, S["prob_t_ps"], i, u)
                nc.scalar.copy(scaled[u][:], ps_b[u][:]).then_inc(S["prob_t"], 1)

            def take_mixed(i, u):
                ready(act, S["mixed_ps"], i, u)
                nc.scalar.copy(mixed_p[u][0][:], ps_a[u][:]).then_inc(S["mixed_high"], 1)

            def tanh_r(i, u):
                ready(act, S["r_ps"], i, u)
                nc.scalar.activation(gate_r[u], ps_b[u][:], ACT.Tanh, bias=b_gate[:, 0:1], scale=0.5).then_inc(S["gate_r"], 1)

            def tanh_z(i, u):
                ready(act, S["z_ps"], i, u)
                nc.scalar.activation(gate_z[u], ps_a[u][:], ACT.Tanh, bias=b_gate[:, 1:2], scale=0.5).then_inc(S["gate_z"], 1)

            def tanh_new(i, u):
                ready(act, S["pre"], i, u)
                nc.scalar.activation(new[u][:], gate_r[u], ACT.Tanh, bias=b_ih[:, 2:3]).then_inc(S["new"], 1)

            def take_xnt1(i, u):
                ready(act, S["xnt1_ps"], i, u)
                nc.scalar.copy(xnt[u][:], ps_b[u][:]).then_inc(S["xnt1"], 1)

            def take_hot(i, u):
                ready(act, S["hot_ps"], i, u)
                nc.scalar.copy(hot_t[u][:], ps_b[u][0:E1, :]).then_inc(S["hot_t"], 1)

            def relu(c):
                def even(i, u):
                    act.wait_ge(up_ps[u], C1 * i + (c + 1))
                    nc.scalar.activation(hidden[u], ps_b[u][:], ACT.Relu, bias=b1[:, c:c + 1]).then_inc(hidden_done[0][u], 1)

                return even

            def relu_out(i, u):
                ready(act, S["down"], i, u)
                nc.scalar.activation(cell[u], ps_a[u][:], ACT.Relu).then_inc(S["y"], 1)

            staggered(act, [
                (at("take_xnt"), take_xnt), (at("take_wh"), take_wh), (at("scale"), scale), (at("take_hn"), take_hn), (at("exponents"), exponents),
                (at("take_prob_t"), take_prob_t), (at("take_mixed"), take_mixed), (at("tanh_r"), tanh_r), (at("tanh_z"), tanh_z), (at("tanh_new"), tanh_new),
                (at("take_xnt1"), take_xnt1), (at("take_hot"), take_hot),
                *((at(f"relu{c}"), relu(c)) for c in range(0, C1, 2)), (at("relu_out"), relu_out),
                (at("round_xnt"), round_xnt("")), (at("round_xnt1"), round_xnt("1"))])

        @block.tensor
        def _(pe):
            pe.wait_ge(w_ready, 1)

            def turn(dst, src):
                for t in range(GT):
                    last = nc.tensor.transpose(dst[:, t * P:(t + 1) * P], src[:, t * P:(t + 1) * P], K.ident[:])
                return last

            def flat(a):
                return a[:].rearrange("p t f -> p (t f)")

            def product(dst, a, b, first=True, last=True):
                nc.tensor.matmul(dst, a[0], b[0][:], start=first, stop=False)
                nc.tensor.matmul(dst, a[0], b[1][:], start=False, stop=False)
                return nc.tensor.matmul(dst, a[1], b[0][:], start=False, stop=last)

            def turn_xn(i, u):
                ready(pe, S["xn"], i, u)
                freed(pe, S["y"], i, u)
                turn(ps_a[u], flat(T.xn[u])).then_inc(S["xnt_ps"], 1)

            def project(i, u):
                ready(pe, S["xnt"], i, u)
                for t in range(GT):
                    last = nc.tensor.matmul(ps_a[u][:, t * P:(t + 1) * P], xnt[u][:, t * P:(t + 1) * P], K.w_att[:, 1, :],
                                            start=True, stop=True)
                last.then_inc(S["wh_ps"], 1)

            def scores(i, u):
                ready(pe, S["xnt"], i, u)
                ready(pe, S["xnt_low"], i, u)
                ready(pe, S["closed"], i, u)
                freed(pe, S["x4"], i, u)
                product(ps_b[u][:], [w[:] for w in w_dst_p], xnt_p[u], last=False)
                for t in range(GT):
                    nc.tensor.matmul(ps_b[u][:, t * P:(t + 1) * P], xnt[u][:, t * P:(t + 1) * P], K.w_score[:, 2, :],
                                     start=False, stop=False, skip_group_check=True)
                nc.tensor.matmul(ps_b[u][:], K.ident_b[:], closed[u][:], start=False, stop=True).then_inc(S["score_ps"], 1)

            def project_hn(i, u):
                ready(pe, S["wh"], i, u)
                product(ps_a[u][:], [w[:, 2, :] for w in w_hh_p], xnt_p[u]).then_inc(S["hn_ps"], 1)

            def turn_prob(i, u):
                ready(pe, S["prob"], i, u)
                turn(ps_b[u], flat(prob[u])).then_inc(S["prob_t_ps"], 1)

            def mix(i, u):
                ready(pe, S["prob_t"], i, u)
                ready(pe, S["hn"], i, u)
                for t in range(GT):
                    last = nc.tensor.matmul(ps_a[u][:, t * P:(t + 1) * P], wh[u][:, t, :], prob_t[u][:, t, :],
                                            start=True, stop=True)
                last.then_inc(S["mixed_ps"], 1)

            def gate(k, ps, name):
                def sums(i, u):
                    ready(pe, S["mixed"], i, u)
                    product(ps[u][:], [w[:, k, :] for w in w_hh_p], xnt_p[u], last=False)
                    product(ps[u][:], [w[:, k, :] for w in w_ih_p], mixed_p[u], first=False).then_inc(S[name], 1)

                return sums

            def project_in(i, u):
                ready(pe, S["gate_r"], i, u)
                product(ps_b[u][:], [w[:, 2, :] for w in w_ih_p], mixed_p[u]).then_inc(S["in_ps"], 1)

            def turn_cell(i, u):
                ready(pe, S["gru"], i, u)
                ready(pe, S["gate_z"], i, u)
                turn(ps_a[u], cell[u]).then_inc(S["gru_ps"], 1)

            def turn_xn1(i, u):
                ready(pe, S["xn1"], i, u)
                turn(ps_b[u], flat(T.xn[u])).then_inc(S["xnt1_ps"], 1)

            def logits(i, u):
                ready(pe, S["xnt1"], i, u)
                for t in range(GT):
                    last = nc.tensor.matmul(ps_a[u][:, t * E1:(t + 1) * E1], xnt[u][:, t * P:(t + 1) * P], w_r1[:],
                                            start=True, stop=True)
                last.then_inc(S["logit_ps"], 1)

            def turn_hot(i, u):
                ready(pe, S["only_hot"], i, u)
                for t in range(GT):
                    last = nc.tensor.transpose(ps_b[u][0:E1, t * P:(t + 1) * P], T.hot[u][:, 0, t, :], K.ident[:])
                last.then_inc(S["hot_ps"], 1)

            def down(c, i, u):
                pe.wait_ge(hidden_done[c % 2][u], (C1 // 2) * i + (c // 2 + 1))
                if c == 0:
                    for part in b2_p:
                        nc.tensor.matmul(ps_a[u][:], part[:], hot_t[u][:], start=(part is b2_p[0]), stop=False)
                return nc.tensor.matmul(ps_a[u][:], w2[:, c, :], hidden[u], start=False, stop=(c == C1 - 1))

            def experts(c):
                def step(i, u):
                    if c == 0:
                        ready(pe, S["hot_m"], i, u)
                        ready(pe, S["xnt_low1"], i, u)
                    else:
                        down(c - 1, i, u)
                    if c < C1:
                        product(ps_b[u][:], [w[:, c, :] for w in w1_p], xnt_p[u], last=False)
                        nc.tensor.matmul(ps_b[u][:], shut[:, c, :], hot_m[u][:], start=False, stop=True).then_inc(up_ps[u], 1)

                return step

            def last_down(i, u):
                down(C1 - 1, i, u).then_inc(S["down"], 1)

            def turn_y(i, u):
                ready(pe, S["y"], i, u)
                turn(ps_b[u], cell[u]).then_inc(S["y_t_ps"], 1)

            staggered(pe, [
                (at("turn_xn"), turn_xn), (at("project"), project), (at("scores"), scores), (at("project_hn"), project_hn), (at("turn_prob"), turn_prob), (at("mix"), mix),
                (at("gate_r"), gate(0, ps_b, "r_ps")), (at("gate_z"), gate(1, ps_a, "z_ps")), (at("project_in"), project_in),
                (at("turn_cell"), turn_cell), (at("turn_xn1"), turn_xn1), (at("logits"), logits), (at("turn_hot"), turn_hot),
                *((at(f"experts{c}"), experts(c)) for c in range(C1)), (at("last_down"), last_down), (at("turn_y"), turn_y)])


INPUTS = ["x", "adj", "L0_gnn_W", "L0_gnn_a", "L0_ffn_Wr", "L0_ffn_W1s", "L0_ffn_b1s", "L0_ffn_W2s", "L0_ffn_b2s", "L0_ffn_W1p",
          "L0_ffn_b1p", "L0_ffn_W2p", "L0_ffn_b2p", "L1_gnn_W", "L1_gnn_a", "L1_gnn_w_ih", "L1_gnn_w_hh", "L1_gnn_b_ih",
          "L1_gnn_b_hh", "L1_ffn_router_w", "L1_ffn_router_b", "L1_ffn_W1", "L1_ffn_b1", "L1_ffn_W2", "L1_ffn_b2"]


def two_gnn_moe_blocks(nc, W, out):
    with ExitStack() as ctx:
        X = ctx.enter_context(nc.sbuf_tensor("X", [P, B, P], F32))
        K = Constants(ctx, nc)
        setup(nc, ctx, K, W)
        R = Routing(ctx, nc)
        with ExitStack() as first:
            R.hold_choices(first, nc)
            XNT = first.enter_context(nc.sbuf_tensor("XNT", [P, B * P], F32))
            phase_a(nc, K, X, XNT, R, W["x"], W["adj"])
            with ExitStack() as experts:
                E = Experts(experts, nc)
                sort_picks(nc, K, R, E, W)
                E.hold_weights(experts, nc)
                shared_expert(nc, K, X, XNT, R, E, W)
                routed_experts(nc, K, R, E)
        phase_c(nc, K, X, R, W, W["adj"], out)


def laid_out(inputs):
    import numpy as np
    a = {n: np.asarray(v) for n, v in inputs.items()}
    for l in ("L0_gnn_a", "L1_gnn_a"):
        a[l] = a[l].reshape(2, P).T
    a["L0_ffn_b1s"] = a["L0_ffn_b1s"].reshape(FC, P).T
    w1p, w2p = a.pop("L0_ffn_W1p"), a.pop("L0_ffn_W2p")
    w2p = w2p.reshape(E0, FC, P, P).transpose(0, 2, 1, 3).reshape(E0, P, F0)
    a["L0_ffn_Wp"] = np.stack([w1p, w2p]).reshape(2 * E0, P, F0).transpose(1, 0, 2)
    a["L0_ffn_b1p"] = a["L0_ffn_b1p"].reshape(1, E0 * F0)
    a["L0_ffn_b2p"] = a["L0_ffn_b2p"].reshape(1, E0 * P)
    a["L0_ffn_b2s"] = a["L0_ffn_b2s"].reshape(P, 1)
    for l in ("L1_gnn_w_ih", "L1_gnn_w_hh"):
        a[l] = a[l].reshape(3, P, P).transpose(2, 0, 1)
    for l in ("L1_gnn_b_ih", "L1_gnn_b_hh"):
        a[l] = a[l].reshape(3, P).T
    a["L1_ffn_router_w"] = a["L1_ffn_router_w"].T
    a["L1_ffn_router_b"] = a["L1_ffn_router_b"].reshape(1, E1)
    a["L1_ffn_W1"] = a["L1_ffn_W1"].transpose(1, 0, 2).reshape(P, C1, P)
    a["L1_ffn_b1"] = a["L1_ffn_b1"].reshape(C1, P).T
    a["L1_ffn_W2"] = a["L1_ffn_W2"].reshape(C1, P, P).transpose(1, 0, 2)
    return {n: np.ascontiguousarray(v) for n, v in a.items()}


def kernel(**inputs):
    import concourse.bacc as bacc
    from concourse.bass_utils import run_bass_kernel_spmd

    nc = bacc.Bacc("TRN2", target_bir_lowering=False, num_devices=1)
    arrays = laid_out({n: inputs[n] for n in INPUTS})
    W = {n: nc.dram_tensor(n, a.shape, mybir.dt.from_np(a.dtype), kind="ExternalInput").ap() for n, a in arrays.items()}
    out = nc.dram_tensor("out", (B, P, P), F32, kind="ExternalOutput").ap()
    two_gnn_moe_blocks(nc, W, out)
    return run_bass_kernel_spmd(nc, [arrays], core_ids=[0]).results[0]["out"]
```
